# Optimizing a Trainium2 kernel written in Bass

```python
import numpy as np
import jax
import jax.numpy as jnp

def _softmax(x, axis=-1):
    return jax.nn.softmax(x, axis=axis)

def _gelu(x):
    return jax.nn.gelu(x, approximate=True)

def _silu(x):
    return jax.nn.silu(x)

def _sigmoid(x):
    return jax.nn.sigmoid(x)

def _layernorm(x, axis=-1, eps=1e-05):
    m = jnp.mean(x, axis=axis, keepdims=True)
    v = jnp.var(x, axis=axis, keepdims=True)
    return (x - m) / jnp.sqrt(v + eps)

def _scatter_add(tgt, idx, src, axis=0):
    return tgt.at[idx].add(src)

def _segment_sum(src, seg, n):
    return jax.ops.segment_sum(src, seg, n)
kernel_name = 'mk_xattn_ffn_d2_seqx_r2_168014'

def setup_inputs(seed: int=0):
    np.random.seed(seed)
    _w = jnp.asarray

    def _rec_inputs():
        import jax
        import jax.numpy as jnp
        _rk = jax.random.key(seed)
        x = -0.0005207 + 1.001 * jax.random.normal(jax.random.fold_in(_rk, 1), (8, 512, 512), jnp.float32)
        _lenS = 512 - jax.random.randint(jax.random.fold_in(_rk, 7), (8,), 0, max(1, 512 // 4) + 1, jnp.int32)
        _lenS2 = 77 - jax.random.randint(jax.random.fold_in(_rk, 8), (8,), 0, max(1, 77 // 4) + 1, jnp.int32)
        _ctx_1024P = jax.random.normal(jax.random.fold_in(_rk, 11), (8, 16, 512), jnp.float32)
        _ctx_1024c = jax.random.dirichlet(jax.random.fold_in(_rk, 511), 0.3 * jnp.ones((16,), jnp.float32), (8, 77))
        _ctx_1024t = jnp.einsum('bsk,bkd->bsd', _ctx_1024c, _ctx_1024P)
        _ctx_1024t = _ctx_1024t * jax.lax.rsqrt(jnp.mean(jnp.square(_ctx_1024t)) + 1e-12) * 0.953939
        ctx_1024 = 4.13588e-05 + 0.999923 * (_ctx_1024t + 0.3 * jax.random.normal(jax.random.fold_in(_rk, 611), (8, 77, 512), jnp.float32))
        _validS = jnp.arange(512)[None, :] < _lenS[:, None]
        _validS2 = jnp.arange(77)[None, :] < _lenS2[:, None]
        _causal = jnp.tril(jnp.ones((512, 512), dtype=bool))
        mask_BxS2_ik0 = jnp.where(jnp.broadcast_to(_validS2[:, :], (8, 77)), 0, 1).astype(jnp.int32)
        mask_BxS2_bk0 = jnp.logical_not(jnp.broadcast_to(_validS2[:, :], (8, 77)))
        return (x, ctx_1024, mask_BxS2_ik0, mask_BxS2_bk0)
    x, ctx_1024, mask_BxS2_ik0, mask_BxS2_bk0 = _rec_inputs()

    def _L0_xattn_setup():
        import jax, jax.numpy as jnp
        import numpy as np
        QUERY_DIM = 512
        KEY_DIM = 512
        NUM_HEADS = 16
        HEAD_DIM = QUERY_DIM // NUM_HEADS
        key = jax.random.key(seed)
        ks = jax.random.split(key, 12)
        B, Sq, Sk = (2, 512, 2048)

        def xavier(k, fan_in, fan_out):
            limit = np.sqrt(6.0 / (fan_in + fan_out))
            return jax.random.uniform(k, (fan_in, fan_out), jnp.float32, -limit, limit)
        return {'query': jax.random.normal(ks[0], (B, Sq, QUERY_DIM), jnp.float32), 'key': jax.random.normal(ks[1], (B, Sk, KEY_DIM), jnp.float32), 'value': jax.random.normal(ks[2], (B, Sk, KEY_DIM), jnp.float32), 'key_mask': jax.random.randint(ks[3], (B, Sk), 0, 2, jnp.int32), 'Wq': xavier(ks[4], QUERY_DIM, NUM_HEADS * HEAD_DIM), 'bq': jnp.zeros((NUM_HEADS * HEAD_DIM,), jnp.float32), 'Wk': xavier(ks[5], KEY_DIM, NUM_HEADS * HEAD_DIM), 'bk': jnp.zeros((NUM_HEADS * HEAD_DIM,), jnp.float32), 'Wv': xavier(ks[6], KEY_DIM, NUM_HEADS * HEAD_DIM), 'bv': jnp.zeros((NUM_HEADS * HEAD_DIM,), jnp.float32), 'Wo': xavier(ks[7], NUM_HEADS * HEAD_DIM, QUERY_DIM), 'bo': jnp.zeros((QUERY_DIM,), jnp.float32)}
    _L0_xattn_all = _L0_xattn_setup()
    _L0_xattn_in = {k: v for k, v in _L0_xattn_all.items() if k in ('Wq', 'bq', 'Wk', 'bk', 'Wv', 'bv', 'Wo', 'bo')}
    del _L0_xattn_all

    def _L0_ffn_setup():
        import jax, jax.numpy as jnp
        import numpy as np
        B, T, D = (8, 2048, 512)
        NUM_SLOTS = 64
        TOP_K = 8
        DQ = D // 4
        DH = D // 2

        def _forward(x, slot_init, w1, b1, w2, b2, tau, Wih, Whh, bih, bhh, wq, bq, wk, bk, wv, bv, ln_g, ln_b, wvp, bvp, wo, bo):
            Bx, Tx, Dx = x.shape
            S = jnp.broadcast_to(slot_init[None], (Bx, NUM_SLOTS, Dx)).astype(x.dtype)
            slot_mean = jnp.broadcast_to(S.mean(axis=1, keepdims=True), (Bx, Tx, Dx))
            ctx = jnp.concatenate([x, slot_mean], axis=-1)
            h = jax.nn.gelu(ctx @ w1 + b1, approximate=False)
            route_logits = (h @ w2 + b2) / (jnp.abs(tau) + 0.1)
            topk_vals, topk_idx = jax.lax.top_k(route_logits, TOP_K)
            topk_w = jax.nn.softmax(topk_vals, axis=-1)
            alpha = (jax.nn.one_hot(topk_idx, NUM_SLOTS, dtype=x.dtype) * topk_w[..., None]).sum(axis=-2)
            slot_input = jnp.einsum('bts,btd->bsd', alpha, x)
            denom = alpha.sum(axis=1) + 1e-08
            si = slot_input / denom[..., None]
            gi = si @ Wih.T + bih
            gh = S @ Whh.T + bhh
            i_r, i_z, i_n = jnp.split(gi, 3, axis=-1)
            h_r, h_z, h_n = jnp.split(gh, 3, axis=-1)
            r = jax.nn.sigmoid(i_r + h_r)
            z = jax.nn.sigmoid(i_z + h_z)
            n = jnp.tanh(i_n + r * h_n)
            S_new = (1.0 - z) * n + z * S
            q = S_new @ wq + bq
            k = S_new @ wk + bk
            v = S_new @ wv + bv
            scale = DQ ** (-0.5)
            attn = jax.nn.softmax(jnp.einsum('bsq,btq->bst', q, k) * scale, axis=-1)
            S_comm = jnp.einsum('bst,btd->bsd', attn, v)
            y = S_new + S_comm
            mu = y.mean(axis=-1, keepdims=True)
            var = y.var(axis=-1, keepdims=True)
            y = (y - mu) * jax.lax.rsqrt(var + 1e-05) * ln_g + ln_b
            slot_values = y @ wvp + bvp
            out = jnp.einsum('bts,bsd->btd', alpha, slot_values)
            return out @ wo + bo
        key = jax.random.key(seed)
        ks = jax.random.split(key, 24)
        n = lambda k, shp, s=0.02: jax.random.normal(k, shp, dtype=jnp.float32) * s
        return {'x': jax.random.normal(ks[0], (B, T, D), dtype=jnp.float32), 'slot_init': n(ks[1], (NUM_SLOTS, D)), 'w1': n(ks[2], (2 * D, DH)), 'b1': jnp.zeros((DH,)), 'w2': n(ks[3], (DH, NUM_SLOTS)), 'b2': jnp.zeros((NUM_SLOTS,)), 'tau': jnp.ones((1,)), 'Wih': n(ks[4], (3 * D, D)), 'Whh': n(ks[5], (3 * D, D)), 'bih': jnp.zeros((3 * D,)), 'bhh': jnp.zeros((3 * D,)), 'wq': n(ks[6], (D, DQ)), 'bq': jnp.zeros((DQ,)), 'wk': n(ks[7], (D, DQ)), 'bk': jnp.zeros((DQ,)), 'wv': n(ks[8], (D, D)), 'bv': jnp.zeros((D,)), 'ln_g': jnp.ones((D,)), 'ln_b': jnp.zeros((D,)), 'wvp': n(ks[9], (D, D)), 'bvp': jnp.zeros((D,)), 'wo': n(ks[10], (D, D)), 'bo': jnp.zeros((D,))}
    _L0_ffn_all = _L0_ffn_setup()
    _L0_ffn_in = {k: v for k, v in _L0_ffn_all.items() if k in ('slot_init', 'w1', 'b1', 'w2', 'b2', 'tau', 'Wih', 'Whh', 'bih', 'bhh', 'wq', 'bq', 'wk', 'bk', 'wv', 'bv', 'ln_g', 'ln_b', 'wvp', 'bvp', 'wo', 'bo')}
    del _L0_ffn_all

    def _L1_xattn_setup():
        import jax, jax.numpy as jnp
        import numpy as np
        DIM = 512
        HEADS = 16
        DIM_HEAD = 64
        INNER = HEADS * DIM_HEAD
        EPS = 1e-05

        def layernorm(t, g, b):
            mu = jnp.mean(t, axis=-1, keepdims=True)
            var = jnp.var(t, axis=-1, keepdims=True)
            return (t - mu) * jax.lax.rsqrt(var + EPS) * g + b
        key = jax.random.key(seed)
        ks = jax.random.split(key, 8)
        b, n, m = (8, 2048, 64)
        x = jax.random.normal(ks[0], (b, n, DIM), dtype=jnp.float32)
        latents = jax.random.normal(ks[1], (b, m, DIM), dtype=jnp.float32)
        mask = jax.random.randint(ks[2], (b, n), 0, 2).astype(bool)
        s = 0.02
        Wq = jax.random.normal(ks[3], (DIM, INNER), dtype=jnp.float32) * s
        Wkv = jax.random.normal(ks[4], (DIM, 2 * INNER), dtype=jnp.float32) * s
        Wout = jax.random.normal(ks[5], (INNER, DIM), dtype=jnp.float32) * s
        ln_x_g = jnp.ones((DIM,), jnp.float32)
        ln_x_b = jnp.zeros((DIM,), jnp.float32)
        ln_l_g = jnp.ones((DIM,), jnp.float32)
        ln_l_b = jnp.zeros((DIM,), jnp.float32)
        ln_o_g = jnp.ones((DIM,), jnp.float32)
        ln_o_b = jnp.zeros((DIM,), jnp.float32)
        return {'x': x, 'latents': latents, 'mask': mask, 'ln_x_g': ln_x_g, 'ln_x_b': ln_x_b, 'ln_l_g': ln_l_g, 'ln_l_b': ln_l_b, 'Wq': Wq, 'Wkv': Wkv, 'Wout': Wout, 'ln_o_g': ln_o_g, 'ln_o_b': ln_o_b}
    _L1_xattn_all = _L1_xattn_setup()
    _L1_xattn_in = {k: v for k, v in _L1_xattn_all.items() if k in ('ln_x_g', 'ln_x_b', 'ln_l_g', 'ln_l_b', 'Wq', 'Wkv', 'Wout', 'ln_o_g', 'ln_o_b')}
    del _L1_xattn_all

    def _L1_ffn_setup():
        import jax, jax.numpy as jnp
        import numpy as np
        B, T, D, E, H = (8, 1024, 512, 8, 128)
        LN_EPS = 1e-05
        key = jax.random.key(seed)
        ks = jax.random.split(key, 4)
        return {'x': jax.random.normal(ks[0], (B, T, D), dtype=jnp.float32), 'Wg': jax.random.normal(ks[1], (E, D), dtype=jnp.float32) * 0.02, 'ln_scale': jnp.ones((E, D), dtype=jnp.float32), 'ln_bias': jnp.zeros((E, D), dtype=jnp.float32), 'W1': jax.random.normal(ks[2], (E, D, H), dtype=jnp.float32) * 0.02, 'b1': jnp.zeros((E, H), dtype=jnp.float32), 'W2': jax.random.normal(ks[3], (E, H, D), dtype=jnp.float32) * 0.02, 'b2': jnp.zeros((E, D), dtype=jnp.float32)}
    _L1_ffn_all = _L1_ffn_setup()
    _L1_ffn_in = {k: v for k, v in _L1_ffn_all.items() if k in ('Wg', 'ln_scale', 'ln_bias', 'W1', 'b1', 'W2', 'b2')}
    del _L1_ffn_all
    return {'x': x, 'ctx_1024': ctx_1024, 'mask_BxS2_ik0': mask_BxS2_ik0, 'mask_BxS2_bk0': mask_BxS2_bk0, 'L0_xattn_Wq': _L0_xattn_in['Wq'], 'L0_xattn_bq': _L0_xattn_in['bq'], 'L0_xattn_Wk': _L0_xattn_in['Wk'], 'L0_xattn_bk': _L0_xattn_in['bk'], 'L0_xattn_Wv': _L0_xattn_in['Wv'], 'L0_xattn_bv': _L0_xattn_in['bv'], 'L0_xattn_Wo': _L0_xattn_in['Wo'], 'L0_xattn_bo': _L0_xattn_in['bo'], 'L0_ffn_slot_init': _L0_ffn_in['slot_init'], 'L0_ffn_w1': _L0_ffn_in['w1'], 'L0_ffn_b1': _L0_ffn_in['b1'], 'L0_ffn_w2': _L0_ffn_in['w2'], 'L0_ffn_b2': _L0_ffn_in['b2'], 'L0_ffn_tau': _L0_ffn_in['tau'], 'L0_ffn_Wih': _L0_ffn_in['Wih'], 'L0_ffn_Whh': _L0_ffn_in['Whh'], 'L0_ffn_bih': _L0_ffn_in['bih'], 'L0_ffn_bhh': _L0_ffn_in['bhh'], 'L0_ffn_wq': _L0_ffn_in['wq'], 'L0_ffn_bq': _L0_ffn_in['bq'], 'L0_ffn_wk': _L0_ffn_in['wk'], 'L0_ffn_bk': _L0_ffn_in['bk'], 'L0_ffn_wv': _L0_ffn_in['wv'], 'L0_ffn_bv': _L0_ffn_in['bv'], 'L0_ffn_ln_g': _L0_ffn_in['ln_g'], 'L0_ffn_ln_b': _L0_ffn_in['ln_b'], 'L0_ffn_wvp': _L0_ffn_in['wvp'], 'L0_ffn_bvp': _L0_ffn_in['bvp'], 'L0_ffn_wo': _L0_ffn_in['wo'], 'L0_ffn_bo': _L0_ffn_in['bo'], 'L1_xattn_ln_x_g': _L1_xattn_in['ln_x_g'], 'L1_xattn_ln_x_b': _L1_xattn_in['ln_x_b'], 'L1_xattn_ln_l_g': _L1_xattn_in['ln_l_g'], 'L1_xattn_ln_l_b': _L1_xattn_in['ln_l_b'], 'L1_xattn_Wq': _L1_xattn_in['Wq'], 'L1_xattn_Wkv': _L1_xattn_in['Wkv'], 'L1_xattn_Wout': _L1_xattn_in['Wout'], 'L1_xattn_ln_o_g': _L1_xattn_in['ln_o_g'], 'L1_xattn_ln_o_b': _L1_xattn_in['ln_o_b'], 'L1_ffn_Wg': _L1_ffn_in['Wg'], 'L1_ffn_ln_scale': _L1_ffn_in['ln_scale'], 'L1_ffn_ln_bias': _L1_ffn_in['ln_bias'], 'L1_ffn_W1': _L1_ffn_in['W1'], 'L1_ffn_b1': _L1_ffn_in['b1'], 'L1_ffn_W2': _L1_ffn_in['W2'], 'L1_ffn_b2': _L1_ffn_in['b2']}

def reference(x, ctx_1024, mask_BxS2_ik0, mask_BxS2_bk0, L0_xattn_Wq, L0_xattn_bq, L0_xattn_Wk, L0_xattn_bk, L0_xattn_Wv, L0_xattn_bv, L0_xattn_Wo, L0_xattn_bo, L0_ffn_slot_init, L0_ffn_w1, L0_ffn_b1, L0_ffn_w2, L0_ffn_b2, L0_ffn_tau, L0_ffn_Wih, L0_ffn_Whh, L0_ffn_bih, L0_ffn_bhh, L0_ffn_wq, L0_ffn_bq, L0_ffn_wk, L0_ffn_bk, L0_ffn_wv, L0_ffn_bv, L0_ffn_ln_g, L0_ffn_ln_b, L0_ffn_wvp, L0_ffn_bvp, L0_ffn_wo, L0_ffn_bo, L1_xattn_ln_x_g, L1_xattn_ln_x_b, L1_xattn_ln_l_g, L1_xattn_ln_l_b, L1_xattn_Wq, L1_xattn_Wkv, L1_xattn_Wout, L1_xattn_ln_o_g, L1_xattn_ln_o_b, L1_ffn_Wg, L1_ffn_ln_scale, L1_ffn_ln_bias, L1_ffn_W1, L1_ffn_b1, L1_ffn_W2, L1_ffn_b2):
    import jax
    import jax.numpy as jnp

    def _L0_xattn_ref(query, key, value, key_mask, Wq, bq, Wk, bk, Wv, bv, Wo, bo):
        import jax, jax.numpy as jnp
        import numpy as np
        QUERY_DIM = 512
        KEY_DIM = 512
        NUM_HEADS = 16
        HEAD_DIM = QUERY_DIM // NUM_HEADS
        B, Sq, _ = query.shape
        Sk = key.shape[1]
        H, D = (NUM_HEADS, HEAD_DIM)
        scale = 1.0 / np.sqrt(D)
        q = (query @ Wq + bq).reshape(B, Sq, H, D)
        k = (key @ Wk + bk).reshape(B, Sk, H, D)
        v = (value @ Wv + bv).reshape(B, Sk, H, D)
        scores = jnp.einsum('bqhd,bkhd->bhqk', q, k) * scale
        mask = (key_mask == 0)[:, None, None, :]
        scores = jnp.where(mask, jnp.float32(-1000000000.0), scores)
        probs = jax.nn.softmax(scores, axis=-1)
        ctx = jnp.einsum('bhqk,bkhd->bqhd', probs, v).reshape(B, Sq, H * D)
        return ctx @ Wo + bo

    def _L0_ffn_ref(x, slot_init, w1, b1, w2, b2, tau, Wih, Whh, bih, bhh, wq, bq, wk, bk, wv, bv, ln_g, ln_b, wvp, bvp, wo, bo):
        import jax, jax.numpy as jnp
        import numpy as np
        B, T, D = (8, 2048, 512)
        NUM_SLOTS = 64
        TOP_K = 8
        DQ = D // 4
        DH = D // 2

        def _forward(x, slot_init, w1, b1, w2, b2, tau, Wih, Whh, bih, bhh, wq, bq, wk, bk, wv, bv, ln_g, ln_b, wvp, bvp, wo, bo):
            Bx, Tx, Dx = x.shape
            S = jnp.broadcast_to(slot_init[None], (Bx, NUM_SLOTS, Dx)).astype(x.dtype)
            slot_mean = jnp.broadcast_to(S.mean(axis=1, keepdims=True), (Bx, Tx, Dx))
            ctx = jnp.concatenate([x, slot_mean], axis=-1)
            h = jax.nn.gelu(ctx @ w1 + b1, approximate=False)
            route_logits = (h @ w2 + b2) / (jnp.abs(tau) + 0.1)
            topk_vals, topk_idx = jax.lax.top_k(route_logits, TOP_K)
            topk_w = jax.nn.softmax(topk_vals, axis=-1)
            alpha = (jax.nn.one_hot(topk_idx, NUM_SLOTS, dtype=x.dtype) * topk_w[..., None]).sum(axis=-2)
            slot_input = jnp.einsum('bts,btd->bsd', alpha, x)
            denom = alpha.sum(axis=1) + 1e-08
            si = slot_input / denom[..., None]
            gi = si @ Wih.T + bih
            gh = S @ Whh.T + bhh
            i_r, i_z, i_n = jnp.split(gi, 3, axis=-1)
            h_r, h_z, h_n = jnp.split(gh, 3, axis=-1)
            r = jax.nn.sigmoid(i_r + h_r)
            z = jax.nn.sigmoid(i_z + h_z)
            n = jnp.tanh(i_n + r * h_n)
            S_new = (1.0 - z) * n + z * S
            q = S_new @ wq + bq
            k = S_new @ wk + bk
            v = S_new @ wv + bv
            scale = DQ ** (-0.5)
            attn = jax.nn.softmax(jnp.einsum('bsq,btq->bst', q, k) * scale, axis=-1)
            S_comm = jnp.einsum('bst,btd->bsd', attn, v)
            y = S_new + S_comm
            mu = y.mean(axis=-1, keepdims=True)
            var = y.var(axis=-1, keepdims=True)
            y = (y - mu) * jax.lax.rsqrt(var + 1e-05) * ln_g + ln_b
            slot_values = y @ wvp + bvp
            out = jnp.einsum('bts,bsd->btd', alpha, slot_values)
            return out @ wo + bo
        return _forward(x, slot_init, w1, b1, w2, b2, tau, Wih, Whh, bih, bhh, wq, bq, wk, bk, wv, bv, ln_g, ln_b, wvp, bvp, wo, bo)

    def _L1_xattn_ref(x, latents, mask, ln_x_g, ln_x_b, ln_l_g, ln_l_b, Wq, Wkv, Wout, ln_o_g, ln_o_b):
        import jax, jax.numpy as jnp
        import numpy as np
        DIM = 512
        HEADS = 16
        DIM_HEAD = 64
        INNER = HEADS * DIM_HEAD
        EPS = 1e-05

        def layernorm(t, g, b):
            mu = jnp.mean(t, axis=-1, keepdims=True)
            var = jnp.var(t, axis=-1, keepdims=True)
            return (t - mu) * jax.lax.rsqrt(var + EPS) * g + b
        b, n, _ = x.shape
        m = latents.shape[1]
        scale = DIM_HEAD ** (-0.5)
        xn = layernorm(x, ln_x_g, ln_x_b)
        ln = layernorm(latents, ln_l_g, ln_l_b)
        q = ln @ Wq
        kv_input = jnp.concatenate((xn, ln), axis=1)
        kv = kv_input @ Wkv
        k, v = jnp.split(kv, 2, axis=-1)

        def heads(t):
            return t.reshape(t.shape[0], t.shape[1], HEADS, DIM_HEAD).transpose(0, 2, 1, 3)
        q, k, v = (heads(q) * scale, heads(k), heads(v))
        sim = jnp.einsum('bhid,bhjd->bhij', q, k)
        mask_full = jnp.concatenate((mask, jnp.ones((b, m), dtype=bool)), axis=1)
        max_neg = -jnp.finfo(sim.dtype).max
        sim = jnp.where(mask_full[:, None, None, :], sim, max_neg)
        attn = jax.nn.softmax(sim.astype(jnp.float32), axis=-1).astype(sim.dtype)
        out = jnp.einsum('bhij,bhjd->bhid', attn, v)
        out = out.transpose(0, 2, 1, 3).reshape(b, m, INNER)
        out = out @ Wout
        return layernorm(out, ln_o_g, ln_o_b)

    def _L1_ffn_ref(x, Wg, ln_scale, ln_bias, W1, b1, W2, b2):
        import jax, jax.numpy as jnp
        import numpy as np
        B, T, D, E, H = (8, 1024, 512, 8, 128)
        LN_EPS = 1e-05
        Bs, Ts, Ds = x.shape
        xt = x.reshape(Bs * Ts, Ds)
        logits = xt @ Wg.T
        top1 = jnp.argmax(logits, axis=-1)
        mu = jnp.mean(xt, axis=-1, keepdims=True)
        var = jnp.mean(jnp.square(xt - mu), axis=-1, keepdims=True)
        xhat = (xt - mu) * jax.lax.rsqrt(var + LN_EPS)
        n_experts = Wg.shape[0]

        def body(y, p):
            s_e, b_e, w1, bb1, w2, bb2, eid = p
            h = jax.nn.gelu((xhat * s_e + b_e) @ w1 + bb1, approximate=False)
            out = h @ w2 + bb2
            mask = (top1 == eid)[:, None].astype(out.dtype)
            return (y + mask * out, None)
        y0 = jnp.zeros_like(xt)
        y, _ = jax.lax.scan(body, y0, (ln_scale, ln_bias, W1, b1, W2, b2, jnp.arange(n_experts)))
        return y.reshape(Bs, Ts, Ds)
    x = x + _L0_xattn_ref(_layernorm(x, axis=-1), ctx_1024, ctx_1024, mask_BxS2_ik0, L0_xattn_Wq, L0_xattn_bq, L0_xattn_Wk, L0_xattn_bk, L0_xattn_Wv, L0_xattn_bv, L0_xattn_Wo, L0_xattn_bo)
    x = x + _L0_ffn_ref(_layernorm(x, axis=-1), L0_ffn_slot_init, L0_ffn_w1, L0_ffn_b1, L0_ffn_w2, L0_ffn_b2, L0_ffn_tau, L0_ffn_Wih, L0_ffn_Whh, L0_ffn_bih, L0_ffn_bhh, L0_ffn_wq, L0_ffn_bq, L0_ffn_wk, L0_ffn_bk, L0_ffn_wv, L0_ffn_bv, L0_ffn_ln_g, L0_ffn_ln_b, L0_ffn_wvp, L0_ffn_bvp, L0_ffn_wo, L0_ffn_bo)
    x = x + _L1_xattn_ref(ctx_1024, _layernorm(x, axis=-1), mask_BxS2_bk0, L1_xattn_ln_x_g, L1_xattn_ln_x_b, L1_xattn_ln_l_g, L1_xattn_ln_l_b, L1_xattn_Wq, L1_xattn_Wkv, L1_xattn_Wout, L1_xattn_ln_o_g, L1_xattn_ln_o_b)
    x = x + _L1_ffn_ref(_layernorm(x, axis=-1), L1_ffn_Wg, L1_ffn_ln_scale, L1_ffn_ln_bias, L1_ffn_W1, L1_ffn_b1, L1_ffn_W2, L1_ffn_b2)
    return x

_drawn_inputs = setup_inputs


def setup_inputs(seed=0):
    import zlib

    import numpy as np

    out = dict(_drawn_inputs(seed))
    spreads = {'L0_xattn_bq': (0.0, 0.1),
     'L0_xattn_bk': (0.0, 2.0),
     'L0_xattn_bv': (0.0, 0.1),
     'L0_xattn_bo': (0.0, 0.1),
     'L0_ffn_b1': (0.0, 0.761),
     'L0_ffn_b2': (0.0, 1.161),
     'L0_ffn_bih': (0.0, 0.1),
     'L0_ffn_bhh': (0.0, 0.1),
     'L0_ffn_bq': (0.0, 2.0),
     'L0_ffn_bk': (0.0, 2.0),
     'L0_ffn_bv': (0.0, 0.1),
     'L0_ffn_ln_g': (1.0, 0.2),
     'L0_ffn_ln_b': (0.0, 0.316),
     'L0_ffn_bvp': (0.0, 0.1),
     'L0_ffn_bo': (0.0, 0.1),
     'L1_xattn_ln_x_g': (1.0, 0.6),
     'L1_xattn_ln_x_b': (0.0, 0.8),
     'L1_xattn_ln_l_g': (1.0, 0.2),
     'L1_xattn_ln_l_b': (0.0, 0.1),
     'L1_xattn_ln_o_g': (1.0, 0.2),
     'L1_xattn_ln_o_b': (0.0, 0.1),
     'L1_ffn_ln_scale': (1.0, 0.6),
     'L1_ffn_ln_bias': (0.0, 0.8),
     'L1_ffn_b1': (0.0, 0.8),
     'L1_ffn_b2': (0.0, 0.1)}
    factors = {'L0_ffn_slot_init': 6.413,
     'L0_ffn_w1': 5.549,
     'L0_ffn_w2': 5.398,
     'L0_ffn_Whh': 8.0,
     'L0_ffn_wq': 64.0,
     'L0_ffn_wk': 35.1,
     'L1_xattn_Wq': 3.402}
    for name, (base, spread) in spreads.items():
        noise = np.random.default_rng([zlib.crc32(name.encode()), seed]).standard_normal(out[name].shape)
        drawn = base * np.exp(spread * noise) if base else spread * noise
        out[name] = jnp.asarray(drawn.astype(out[name].dtype))
    for name, factor in factors.items():
        out[name] = (out[name] * factor).astype(out[name].dtype)
    return out
```

```python
from contextlib import ExitStack

import numpy as np
import concourse.bass as bass
from concourse import mybir

F32 = mybir.dt.float32
F32R = mybir.dt.float32r
I32 = mybir.dt.int32
U32 = mybir.dt.uint32
ALU = mybir.AluOpType
ACT = mybir.ActivationFunctionType
AX = mybir.AxisListType.X

P = 128
EPS = 1e-5

COLUMNS = ["L0_xattn_bq", "L0_xattn_bk", "L0_xattn_bv", "L0_ffn_b1", "L0_ffn_bih", "L0_ffn_bhh", "L0_ffn_bq",
           "L0_ffn_bk", "L0_ffn_bvp", "L1_xattn_ln_x_g", "L1_xattn_ln_x_b", "L1_xattn_ln_l_g", "L1_xattn_ln_l_b",
           "L1_ffn_ln_scale", "L1_ffn_ln_bias", "L1_ffn_b1"]


class Signal:

    def __init__(self, sem, orders):
        self.sem, self.known, self.order, self.same = sem, orders.get(sem.name), [], {}
        orders[sem.name] = self.order

    @property
    def per(self):
        return len(self.known) if self.known else 1

    def mark(self, *name):
        if name not in self.order:
            self.order.append(name)
        return self.sem, 1

    def alias(self, name, step):
        self.same[name] = step

    def has(self, *name):
        return not self.known or self.same.get(name, name) in self.known

    def ordinal(self, name):
        return self.known.index(self.same.get(name, name)) + 1 if self.known else 1

    def at(self, i, *name):
        return self.sem, i * self.per + (self.per + self.ordinal(name))

    def before(self, i, *name):
        return self.sem, i * self.per + self.ordinal(name)


class Stage:

    def __init__(self, nc, ctx, name, orders):
        self.nc, self.ctx, self.name, self.orders = nc, ctx, name, orders

    def sb(self, name, shape, dt=F32):
        return self.ctx.enter_context(self.nc.sbuf_tensor(f"{self.name}_{name}", shape, dt))

    def ps(self, name, shape):
        return self.ctx.enter_context(self.nc.psum_tensor(f"{self.name}_{name}", shape, F32))

    def sem(self, name):
        return self.ctx.enter_context(self.nc.semaphore(f"{self.name}_{name}"))

    def steps(self, name):
        return Signal(self.sem(name), self.orders)


def wait_apart(engine, step, passed):
    engine.wait_ge(*step)
    engine.sem_inc(passed, 1)


def f32(ap):
    return ap.bitcast(F32)


def product(pe, out, a, b, first, last):
    pe.matmul(out, a[0], b[0], start=first, stop=False)
    pe.matmul(out, a[0], b[1], start=False, stop=False)
    return pe.matmul(out, a[1], b[0], start=False, stop=last)


def make_identity(pool, ident, done):
    pool.memset(ident[:, :], 0.0).then_inc(done, 1)
    pool.wait_ge(done, 1)
    pool.affine_select(out=ident[:, :], in_=ident[:, :], compare_op=ALU.not_equal, fill=1.0,
                       base=0, pattern=[[-1, P]], channel_multiplier=1).then_inc(done, 1)



def load_and_split(st, weights, tag, slots):
    loaded = [st.sem(f"{tag}_w{j}_loaded") for j in range(2)]
    hi_cut, lo_cut = st.sem(f"{tag}_hi_cut"), st.sem(f"{tag}_lo_cut")

    def slot(n):
        _, k, m = weights[n][0].shape
        return slots[n % 2][:, 0:k * m].rearrange("p (k m) -> p k m", k=k)

    def on_sync(sp):
        for n, (src, _, _) in enumerate(weights):
            if n >= 2:
                sp.wait_ge(lo_cut, n - 1)
            sp.dma_start(slot(n), src).then_inc(loaded[n % 2], 16)

    def on_scalar(act):
        for n, (_, hi, _) in enumerate(weights):
            act.wait_ge(loaded[n % 2], 16 * (n // 2 + 1))
            act.activation(hi, slot(n), ACT.Copy).then_inc(hi_cut, 1)

    def on_vector(dve):
        for n, (_, hi, lo) in enumerate(weights):
            dve.wait_ge(hi_cut, n + 1)
            dve.tensor_tensor(lo, slot(n), f32(hi), ALU.subtract).then_inc(lo_cut, 1)

    def cut(engine, n=len(weights)):
        engine.wait_ge(lo_cut, n)

    return on_sync, on_scalar, on_vector, cut


class Banks:

    def __init__(self, tiles, units):
        self.tiles, self.units = tiles, units

    def __getitem__(self, unit):
        return self.tiles[self.units.index(unit) % len(self.tiles)]

    def user_before(self, unit):
        n, r = self.units.index(unit), len(self.tiles)
        if n >= r:
            return self.units[n - r], False
        return self.units[max(m for m in range(len(self.units)) if m % r == n % r)], True


def take(engine, banks, read, i, unit):
    last, earlier = banks.user_before(unit)
    for signal in read:
        if signal.has("read", *last):
            engine.wait_ge(*(signal.before if earlier else signal.at)(i, "read", *last))



def build_layer0(nc, orders, a, x1_s, alphaT_s, si_s):
    B, T, D = a["x"].shape
    SK = a["ctx_1024"].shape[1]
    SKP = SK + SK % 2
    C, NT = D // P, T // P
    H, HD = 16, 32
    HC = P // HD
    DH = a["L0_ffn_w1"].shape[1]
    J = DH // P
    NS = a["L0_ffn_slot_init"].shape[0]
    KTOP = 8
    SCALE = 1.0 / float(np.sqrt(HD))
    MASKED = 1e9 / SCALE

    with ExitStack() as ctx:
        st = Stage(nc, ctx, "l0", orders)
        sb, sem = st.sb, st.sem
        pair = lambda name, shape: (sb(name + "_hi", shape, F32R), sb(name + "_lo", shape, F32R))

        ident = sb("ident", [P, P])
        minus_half = sb("minus_half", [P, NT])
        ones = sb("ones", [P, P])
        ones_r = sb("ones_r", [1, P], F32R)
        Wq, Wk, Wv, Wo = (pair(n, [P, C, D]) for n in ("Wq", "Wk", "Wv", "Wo"))
        W1 = pair("W1", [P, C, DH])
        W2 = pair("W2", [P, J, NS])
        smean = sb("smean", [P, C])
        b1c = sb("b1c", [P, J])
        hbias = sb("hbias", [P, J])
        bq, bk, bv = (sb(n, [P, C]) for n in ("bq", "bk", "bv"))
        bo_bc = sb("bo_bc", [P, D])
        b2_bc = sb("b2_bc", [P, NS])
        tau = sb("tau", [P, 4])

        x = sb("x", [P, NT, D])
        x1 = sb("x1", [P, NT, D])
        cx = sb("cx", [SK, D])
        mask_i = sb("mask_i", [P, SK], I32)
        valid = sb("valid", [P, SKP])
        mrow = sb("mrow", [1, HC, SKP], F32R)
        stats = sb("stats", [P, NT, 6])
        mv = sb("mv", [P, NT, 2])
        ve = sb("ve", [P, NT])
        rstd = sb("rstd", [P, NT])
        xn = sb("xn", [P, NT, D])
        xT = pair("xT", [P, C, T])
        cT = pair("cT", [P, C, SKP])
        Kv = sb("Kv", [P, C, SKP])
        Kd = pair("Kd", [P, C, HC * SKP])
        Vd = pair("Vd", [SK, C, HC * (P + HD)])
        qT = pair("qT", [P, C, T])
        mx = sb("mx", [P, NT, H])
        E = sb("E", [P, NT, H, SK])
        rs = sb("rs", [P, NT, H])
        PT = [pair(f"PT{n}", [SK, T]) for n in range(2)]
        oT = qT
        flat = E[:, :, :, :].rearrange("p t h s -> p (t h s)")
        w1s = flat[:, 0:C * DH].rearrange("p (c n) -> p c n", c=C)
        slots0 = flat[0:NS, C * DH:C * DH + D]
        hT = flat[:, 0:J * T].rearrange("p (j t) -> p j t", j=J)
        hTs = tuple(z[:, 0:J, :] for z in oT)
        L = sb("L", [P, NT, NS])
        top = sb("top", [P, NT, KTOP])
        rest = sb("rest", [P, NT, NS])
        el = sb("el", [P, NT, NS])
        asum = sb("asum", [P, NT])
        alpha = sb("alpha", [P, NT, NS])
        aT = sb("aT", [NS, T])
        den = sb("den", [NS, 1])
        si = sb("si", [NS, D])

        flat_slots = [z[:, :, :].rearrange("p t d -> p (t d)") for z in (x1, xn)]

        bank = [st.ps(f"bank{n}", [P, 512]) for n in range(8)]

        setup = sem("setup")
        passed = sem("passed")
        small = sem("small")
        x_in, cx_in, mask_in = sem("x_in"), sem("cx_in"), sem("mask_in")
        x1_out, aT_out, si_out = sem("x1_out"), sem("aT_out"), sem("si_out")
        consts = sem("consts")
        mean_ps, mean_sb, hb_ps = sem("mean_ps"), sem("mean_sb"), sem("hb_ps")
        hb_ready, tau_ready = sem("hb_ready"), sem("tau_ready")
        pe_s, act_s, dve_s, pool_s = (st.steps(n) for n in ("products", "act", "dve", "rstd"))

        dve_s.alias(("read", "K"), ("Kv",))
        dve_s.alias(("read", "aT"), ("aT",))
        dve_s.alias(("read", "si"), ("si",))
        for t in range(NT):
            for c in range(C):
                dve_s.alias(("read", "S", t, c), ("shifted", t, c))

        rows = lambda w: w.rearrange("(c p) n -> p c n", p=P)
        weights = []
        for name, tile in (("Wk", Wk), ("Wv", Wv), ("Wq", Wq), ("Wo", Wo)):
            weights.append((rows(a["L0_xattn_" + name]), tile[0][:, :, :], tile[1][:, :, :]))
        weights.append((rows(a["L0_ffn_w1"][0:D, :]), W1[0][:, :, :], W1[1][:, :, :]))
        weights.append((rows(a["L0_ffn_w2"]), W2[0][:, :, :], W2[1][:, :, :]))
        w_sync, w_scalar, w_vector, w_cut = load_and_split(st, weights, "w", flat_slots)

        smalls = [(slots0, a["L0_ffn_slot_init"]), (w1s, rows(a["L0_ffn_w1"][D:2 * D, :])),
                  (b1c[:, :], a["L0_ffn_b1"]),
                  (bq[:, :], a["L0_xattn_bq"]), (bk[:, :], a["L0_xattn_bk"]),
                  (bv[:, :], a["L0_xattn_bv"]),
                  (bo_bc[:, :], a["L0_xattn_bo"].partition_broadcast(P)),
                  (b2_bc[:, :], a["L0_ffn_b2"].partition_broadcast(P)),
                  (tau[:, 0:1], a["L0_ffn_tau"].partition_broadcast(P))]

        units = [("xT", c) for c in range(C)] + [("cT",), ("K",), ("V",)]
        units += [("Q", c) for c in range(C)]
        units += [("S", t, c) for t in range(NT) for c in range(C)]
        for c in range(C):
            units += [("PT", c * HC + n) for n in range(HC)] + [("O", c)]
        units += [("Wo", t) for t in range(NT)] + [("fT", c) for c in range(C)]
        units += [("h", j) for j in range(J)] + [("L",), ("aT",), ("si",), ("den",)]
        banks = Banks(bank, units)

        block = ctx.enter_context(nc.Block())

        @block.sync
        def _(sp):
            for out in (x1_out, aT_out, si_out):
                sp.sem_inc(out, 16)
            for dst, src in smalls:
                sp.dma_start(dst, src).then_inc(small, 16)
            w_sync(sp)

            def load(i, last=None):
                one = lambda ap: ap[bass.ds(i, 1)]
                if last is not None:
                    sp.wait_ge(*dve_s.at(last, "res", NT - 1))
                sp.dma_start(x[:, :, :], one(a["x"]).rearrange("b (t p) d -> p (b t) d", p=P)).then_inc(x_in, 16)
                if last is not None:
                    sp.wait_ge(*pe_s.at(last, "cT"))
                sp.dma_start(cx[:, :], one(a["ctx_1024"]).rearrange("b s d -> (b s) d")).then_inc(cx_in, 16)
                if last is not None:
                    sp.wait_ge(*dve_s.at(last, "valid"))
                sp.dma_start(mask_i[:, :], one(a["mask_BxS2_ik0"]).rearrange("b s -> (b s)").partition_broadcast(P)).then_inc(mask_in, 16)

            def store(i):
                one = lambda ap: ap[bass.ds(i, 1)]
                sp.wait_ge(*dve_s.at(i, "aT"))
                sp.dma_start(one(alphaT_s).rearrange("b s t -> (b s) t"), aT[:, :]).then_inc(aT_out, 16)
                sp.wait_ge(*dve_s.at(i, "si"))
                sp.dma_start(one(si_s).rearrange("b s d -> (b s) d"), si[:, :]).then_inc(si_out, 16)

            def store_x1(i):
                sp.wait_ge(*dve_s.at(i, "res", NT - 1))
                sp.dma_start(x1_s[bass.ds(i, 1)].rearrange("b (t p) d -> p (b t) d", p=P), x1[:, :, :]).then_inc(x1_out, 16)

            load(0)
            with sp.Fori(0, B - 1) as i:
                store_x1(i)
                load(i + 1, i)
                store(i)
            store_x1(B - 1)
            store(B - 1)
            for out in (x1_out, aT_out, si_out):
                sp.wait_ge(out, 16 * (B + 1))

        @block.gpsimd
        def _(pool):
            pool.sem_inc(pool_s.sem, pool_s.per)
            make_identity(pool, ident, setup)
            pool.memset(minus_half[:, :], -0.5).then_inc(setup, 1)
            pool.memset(ones[:, :], 1.0).then_inc(setup, 1)
            pool.memset(valid[:, :], 0.0).then_inc(setup, 1)
            for n in range(2):
                pool.memset(cT[n][:, :, :].bitcast(F32), 0.0).then_inc(setup, 1)
                pool.memset(Kd[n][:, :, :].bitcast(F32), 0.0).then_inc(setup, 1)
                pool.memset(Vd[n][:, :, :].bitcast(F32), 0.0).then_inc(setup, 1)
            pool.wait_ge(setup, 11)
            with pool.Fori(0, B) as i:
                for ln in ("ln1", "ln2"):
                    wait_apart(pool, dve_s.at(i, ln, "var"), passed)
                    pool.tensor_scalar(ve[:, :], mv[:, :, 1], EPS, None, ALU.add).then_inc(*pool_s.mark(ln, "ve"))
                    pool.wait_ge(*pool_s.at(i, ln, "ve"))
                    pool.tensor_tensor(rstd[:, :], ve[:, :], minus_half[:, :], ALU.pow).then_inc(*pool_s.mark(ln, "rstd"))

        @block.tensor
        def _(pe):
            pe.sem_inc(pe_s.sem, pe_s.per)
            pe.wait_ge(small, 16 * len(smalls))
            pe.wait_ge(setup, 11)
            for c in range(C):
                m = pe.matmul(bank[0][:, c:c + 1], slots0[:, c * P:(c + 1) * P], ones[0:NS, 0:1], start=True, stop=True)
            m.then_inc(mean_ps, 1)
            pe.wait_ge(mean_sb, 1)
            for j in range(J):
                for c in range(C):
                    m = pe.matmul(bank[1][:, j:j + 1], w1s[:, c, j * P:(j + 1) * P], smean[:, c:c + 1],
                                  start=(c == 0), stop=(c == C - 1))
            m.then_inc(hb_ps, 1)
            w_cut(pe)
            pe.wait_ge(consts, 3)
            pe.wait_ge(hb_ready, 1)
            with pe.Fori(0, B) as i:
                def unit(*name):
                    take(pe, banks, (act_s, dve_s), i, name)
                    return banks[name]

                def project(out, w, m0, m1, x, n0, n1, chunks=C):
                    for k in range(chunks):
                        last = product(pe, out, (w[0][:, k, m0:m1], w[1][:, k, m0:m1]),
                                       (x[0][:, k, n0:n1], x[1][:, k, n0:n1]), k == 0, k == chunks - 1)
                    return last

                def transposes(name, ln):
                    for c in range(C):
                        ps = unit(name, c)
                        for t in range(NT):
                            if c == 0:
                                pe.wait_ge(*dve_s.at(i, ln, "xn", t))
                            m = pe.transpose(ps[:, t * P:(t + 1) * P], xn[:, t, c * P:(c + 1) * P], ident[:, :])
                        m.then_inc(*pe_s.mark(name, c))

                transposes("xT", "ln1")
                ps = unit("cT")
                pe.wait_ge(cx_in, i * 16 + 16)
                for c in range(C):
                    m = pe.transpose(ps[:, c * SK:(c + 1) * SK], cx[:, c * P:(c + 1) * P], ident[0:SK, 0:SK])
                m.then_inc(*pe_s.mark("cT"))
                ps = unit("K")
                pe.wait_ge(*dve_s.at(i, "read", "cT"))
                for c in range(C):
                    m = project(ps[:, c * SKP:(c + 1) * SKP], Wk, c * P, (c + 1) * P, cT, 0, SKP)
                m.then_inc(*pe_s.mark("K"))
                ps = unit("V")
                project(ps[0:SK, :], cT, 0, SK, Wv, 0, D).then_inc(*pe_s.mark("V"))
                for c in range(C):
                    ps = unit("Q", c)
                    pe.wait_ge(*dve_s.at(i, "read", "xT", C - 1))
                    project(ps[:, :], Wq, c * P, (c + 1) * P, xT, 0, T).then_inc(*pe_s.mark("Q", c))
                pe.wait_ge(*dve_s.at(i, "Kd"))
                for t in range(NT):
                    for c in range(C):
                        ps = unit("S", t, c)
                        if t == 0:
                            pe.wait_ge(*dve_s.at(i, "read", "Q", c))
                        q = [z[:, c, t * P:(t + 1) * P] for z in qT]
                        out = ps[:, 0:HC * SKP]
                        product(pe, out, q, [z[:, c, :] for z in Kd], True, False)
                        pe.matmul(out, ones_r[:, :], mrow[:, :, :].rearrange("p h s -> p (h s)"),
                                  start=False, stop=True).then_inc(*pe_s.mark("S", t, c))
                for c in range(C):
                    for n in range(HC):
                        h = c * HC + n
                        ps = unit("PT", h)
                        for t in range(NT):
                            if h == 0:
                                pe.wait_ge(*dve_s.at(i, "probs", t))
                            m = pe.transpose(ps[0:SK, t * P:(t + 1) * P], E[:, t, h, :], ident[:, :])
                        m.then_inc(*pe_s.mark("PT", h))
                    ps = unit("O", c)
                    for n in range(HC):
                        h = c * HC + n
                        pe.wait_ge(*dve_s.at(i, "read", "PT", h))
                        last = product(pe, ps[:, :], [z[:, c, n * P:(n + 1) * P] for z in Vd],
                                       [z[:, :] for z in PT[h % 2]], n == 0, n == HC - 1)
                        last.then_inc(*pe_s.mark("PV", h))
                for t in range(NT):
                    ps = unit("Wo", t)
                    pe.wait_ge(*dve_s.at(i, "read", "O", C - 1))
                    project(ps[:, :], oT, t * P, (t + 1) * P, Wo, 0, D).then_inc(*pe_s.mark("Wo", t))
                transposes("fT", "ln2")
                pe.wait_ge(*dve_s.at(i, "read", "fT", C - 1))
                for j in range(J):
                    ps = unit("h", j)
                    project(ps[:, :], W1, j * P, (j + 1) * P, xT, 0, T).then_inc(*pe_s.mark("h", j))
                ps = unit("L")
                pe.wait_ge(*dve_s.at(i, "hlo", J - 1))
                for t in range(NT):
                    m = project(ps[:, t * NS:(t + 1) * NS], hTs, t * P, (t + 1) * P, W2, 0, NS, J)
                m.then_inc(*pe_s.mark("L"))
                ps = unit("aT")
                wait_apart(pe, dve_s.at(i, "alpha"), passed)
                for t in range(NT):
                    m = pe.transpose(ps[0:NS, t * P:(t + 1) * P], alpha[:, t, :], ident[:, :])
                m.then_inc(*pe_s.mark("aT"))
                ps, ps2 = unit("si"), unit("den")
                for t in range(NT):
                    pe.matmul(ps[0:NS, :], alpha[:, t, :], xn[:, t, :], start=(t == 0), stop=(t == NT - 1))
                    m = pe.matmul(ps2[0:NS, 0:1], alpha[:, t, :], ones[:, 0:1], start=(t == 0), stop=(t == NT - 1))
                m.then_inc(*pe_s.mark("si"))

        @block.scalar
        def _(act):
            act.sem_inc(act_s.sem, act_s.per)
            w_scalar(act)
            act.wait_ge(tau_ready, 1)
            act.wait_ge(hb_ready, 1)
            with act.Fori(0, B) as i:
                def hi(signal_name, out, src, func=ACT.Copy, mark=None, **kw):
                    act.wait_ge(*pe_s.at(i, *signal_name))
                    return act.activation(out, src, func, **kw).then_inc(*act_s.mark("hi", *signal_name))

                for c in range(C):
                    if c == 0:
                        act.wait_ge(*pe_s.before(i, "h", J - 1))
                    hi(("xT", c), xT[0][:, c, :], banks["xT", c][:, :])
                act.wait_ge(*pe_s.before(i, "V"))
                hi(("cT",), cT[0][:, :, 0:SK], banks["cT",][:, 0:C * SK].rearrange("p (c s) -> p c s", c=C))
                act.wait_ge(*dve_s.at(i, "Kv"))
                act.wait_ge(*pe_s.before(i, "S", NT - 1, C - 1))
                for n in range(HC):
                    q = slice(n * HD, (n + 1) * HD)
                    act.activation(Kd[0][q, :, n * SKP:(n + 1) * SKP], Kv[q, :, :], ACT.Copy)\
                       .then_inc(*act_s.mark("Kd", n))
                act.wait_ge(*pe_s.before(i, "PV", H - 1))
                hi(("V",), vdiag(Vd[0], C, HC, P, HD, SK), banks["V",][0:SK, :].rearrange("p (c h d) -> p c h d", c=C, h=HC))
                for c in range(C):
                    hi(("Q", c), qT[0][:, c, :], banks["Q", c][:, :], ACT.Identity, bias=bq[:, c:c + 1])
                for t in range(NT):
                    act.wait_ge(*dve_s.at(i, "shifted", t, C - 1))
                    act.activation(E[:, t, :, :], E[:, t, :, :], ACT.Exp, scale=SCALE).then_inc(*act_s.mark("exp", t))
                for c in range(C):
                    for n in range(HC):
                        h = c * HC + n
                        if h >= 2:
                            act.wait_ge(*pe_s.at(i, "PV", h - 2))
                        hi(("PT", h), PT[h % 2][0][:, :], banks["PT", h][0:SK, :])
                    if c == 0:
                        act.wait_ge(*pe_s.before(i, "Wo", NT - 1))
                    act.wait_ge(*pe_s.at(i, "PV", c * HC + HC - 1))
                    act.activation(oT[0][:, c, :], banks["O", c][:, :], ACT.Identity, bias=bv[:, c:c + 1])\
                       .then_inc(*act_s.mark("hi", "O", c))
                for c in range(C):
                    if c == 0:
                        act.wait_ge(*pe_s.at(i, "Q", C - 1))
                    hi(("fT", c), xT[0][:, c, :], banks["fT", c][:, :])
                act.wait_ge(*dve_s.before(i, "hlo", J - 1))
                act.wait_ge(*pe_s.before(i, "L"))
                for j in range(J):
                    act.wait_ge(*pe_s.at(i, "h", j))
                    act.activation(hT[:, j, :], banks["h", j][:, :], ACT.Gelu, bias=hbias[:, j:j + 1])\
                       .then_inc(*act_s.mark("read", "h", j))
                for j in range(J):
                    act.wait_ge(*act_s.at(i, "read", "h", j))
                    act.activation(hTs[0][:, j, :], hT[:, j, :], ACT.Copy).then_inc(*act_s.mark("hhi", j))
                act.wait_ge(*dve_s.at(i, "lshift"))
                act.activation(el[:, :, :], el[:, :, :], ACT.Exp, scale=tau[:, 3:4]).then_inc(*act_s.mark("lexp"))

        @block.vector
        def _(dve):
            dve.sem_inc(dve_s.sem, dve_s.per)
            dve.wait_ge(small, 16 * len(smalls))
            dve.wait_ge(setup, 11)
            dve.tensor_copy(ones_r[:, :], ones[0:1, :]).then_inc(consts, 1)
            dve.tensor_scalar(tau[:, 1:2], tau[:, 0:1], -1.0, None, ALU.mult).then_inc(consts, 1)
            dve.wait_ge(consts, 2)
            dve.tensor_scalar(tau[:, 2:3], tau[:, 1:2], tau[:, 0:1], 0.1, ALU.max, ALU.add).then_inc(consts, 1)
            dve.wait_ge(consts, 3)
            dve.reciprocal(tau[:, 3:4], tau[:, 2:3]).then_inc(tau_ready, 1)
            dve.wait_ge(mean_ps, 1)
            dve.tensor_scalar(smean[:, :], bank[0][:, 0:C], 1.0 / NS, None, ALU.mult).then_inc(mean_sb, 1)
            dve.wait_ge(hb_ps, 1)
            dve.tensor_tensor(hbias[:, :], bank[1][:, 0:J], b1c[:, :], ALU.add).then_inc(hb_ready, 1)
            w_vector(dve)

            with dve.Fori(0, B) as i:
                def layer_norm(src, ln):
                    for t in range(NT):
                        if ln == "ln2":
                            dve.wait_ge(*dve_s.at(i, "res", t))
                        dve.bn_stats(stats[:, t, :], src[:, t, :]).then_inc(*dve_s.mark(ln, "stats", t))
                    wait_apart(dve, dve_s.at(i, ln, "stats", NT - 1), passed)
                    for t in range(NT):
                        m = dve.bn_aggr(mv[:, t, :], stats[:, t, :])
                    m.then_inc(*dve_s.mark(ln, "var"))
                    dve.wait_ge(*dve_s.at(i, ln, "var"))
                    dve.wait_ge(*pool_s.at(i, ln, "rstd"))
                    for t in range(NT):
                        dve.tensor_scalar(xn[:, t, :], src[:, t, :], mv[:, t, 0:1], rstd[:, t:t + 1],
                                          ALU.subtract, ALU.mult).then_inc(*dve_s.mark(ln, "xn", t))

                def lo(name, out, ps, hi_ap, bias=None):
                    dve.wait_ge(*act_s.at(i, "hi", *name))
                    if bias is None:
                        m = dve.tensor_tensor(out, ps, f32(hi_ap), ALU.subtract)
                    else:
                        m = dve.scalar_tensor_tensor(out, ps, bias, f32(hi_ap), ALU.add, ALU.subtract)
                    return m.then_inc(*dve_s.mark("read", *name))

                dve.wait_ge(x_in, i * 16 + 16)
                dve.wait_ge(*pe_s.before(i, "si"))
                layer_norm(x, "ln1")
                for c in range(C):
                    lo(("xT", c), xT[1][:, c, :], banks["xT", c][:, :], xT[0][:, c, :])
                dve.wait_ge(*act_s.at(i, "hi", "cT"))
                lo(("cT",), cT[1][:, :, 0:SK], banks["cT",][:, 0:C * SK].rearrange("p (c s) -> p c s", c=C), cT[0][:, :, 0:SK])
                dve.wait_ge(mask_in, i * 16 + 16)
                dve.tensor_scalar(valid[:, 0:SK], mask_i[:, :], 0.0, None, ALU.not_equal).then_inc(*dve_s.mark("valid"))
                dve.wait_ge(*dve_s.at(i, "valid"))
                dve.wait_ge(*pe_s.before(i, "S", NT - 1, C - 1))
                dve.tensor_scalar(mrow[:, :, :], valid[0:1, :].unsqueeze(1).to_broadcast([1, HC, SKP]), 1.0, MASKED,
                                  ALU.subtract, ALU.mult).then_inc(*dve_s.mark("mrow"))
                dve.wait_ge(*pe_s.at(i, "K"))
                for c in range(C):
                    m = dve.scalar_tensor_tensor(Kv[:, c, :], banks["K",][:, c * SKP:(c + 1) * SKP], bk[:, c:c + 1],
                                                 valid[:, :], ALU.add, ALU.mult)
                    m.then_inc(*dve_s.mark(*(("Kv",) if c == C - 1 else ("Kv", c))))
                dve.wait_ge(*dve_s.at(i, "Kv"))
                for n in range(HC):
                    q = slice(n * HD, (n + 1) * HD)
                    dve.wait_ge(*act_s.at(i, "Kd", n))
                    m = dve.tensor_tensor(Kd[1][q, :, n * SKP:(n + 1) * SKP], Kv[q, :, :],
                                          f32(Kd[0][q, :, n * SKP:(n + 1) * SKP]), ALU.subtract)
                    m.then_inc(*dve_s.mark(*(("Kd",) if n == HC - 1 else ("Kd", n))))
                lo(("V",), vdiag(Vd[1], C, HC, P, HD, SK), banks["V",][0:SK, :].rearrange("p (c h d) -> p c h d", c=C, h=HC),
                   vdiag(Vd[0], C, HC, P, HD, SK))
                for c in range(C):
                    lo(("Q", c), qT[1][:, c, :], banks["Q", c][:, :], qT[0][:, c, :], bq[:, c:c + 1])

                def softmax_end(t):
                    dve.wait_ge(*act_s.at(i, "exp", t))
                    dve.reduce_sum(rs[:, t, :], E[:, t, :, :], AX).then_inc(*dve_s.mark("sum", t))
                    dve.wait_ge(*dve_s.at(i, "sum", t))
                    dve.reciprocal(rs[:, t, :], rs[:, t, :]).then_inc(*dve_s.mark("rsum", t))
                    dve.wait_ge(*dve_s.at(i, "rsum", t))
                    dve.tensor_tensor(E[:, t, :, :], E[:, t, :, :], rs[:, t, :].unsqueeze(2).to_broadcast([P, H, SK]),
                                      ALU.mult).then_inc(*dve_s.mark("probs", t))

                for t in range(NT):
                    for c in range(C):
                        s = banks["S", t, c][:, 0:HC * SKP].rearrange("p (h s) -> p h s", h=HC)[:, :, 0:SK]
                        hs = slice(c * HC, (c + 1) * HC)
                        dve.wait_ge(*pe_s.at(i, "S", t, c))
                        dve.reduce_max(mx[:, t, hs], s, AX).then_inc(*dve_s.mark("max", t, c))
                        dve.wait_ge(*dve_s.at(i, "max", t, c))
                        dve.tensor_tensor(E[:, t, hs, :], s, mx[:, t, hs].unsqueeze(2).to_broadcast([P, HC, SK]),
                                          ALU.subtract).then_inc(*dve_s.mark("shifted", t, c))
                    if t:
                        softmax_end(t - 1)
                softmax_end(NT - 1)
                for c in range(C):
                    for n in range(HC):
                        h = c * HC + n
                        lo(("PT", h), PT[h % 2][1][:, :], banks["PT", h][0:SK, :], PT[h % 2][0][:, :])
                    lo(("O", c), oT[1][:, c, :], banks["O", c][:, :], oT[0][:, c, :], bv[:, c:c + 1])
                dve.wait_ge(x1_out, i * 16 + 16)
                for t in range(NT):
                    dve.wait_ge(*pe_s.at(i, "Wo", t))
                    dve.tensor_tensor(x1[:, t, :], banks["Wo", t][:, :], x[:, t, :], ALU.add).then_inc(*dve_s.mark("read", "Wo", t))
                    dve.wait_ge(*dve_s.at(i, "read", "Wo", t))
                    dve.tensor_tensor(x1[:, t, :], x1[:, t, :], bo_bc[:, :], ALU.add).then_inc(*dve_s.mark("res", t))
                dve.wait_ge(*pe_s.at(i, "xT", C - 1))
                layer_norm(x1, "ln2")
                for c in range(C):
                    lo(("fT", c), xT[1][:, c, :], banks["fT", c][:, :], xT[0][:, c, :])
                for j in range(J):
                    dve.wait_ge(*act_s.at(i, "hhi", j))
                    dve.tensor_tensor(hTs[1][:, j, :], hT[:, j, :], f32(hTs[0][:, j, :]), ALU.subtract)\
                       .then_inc(*dve_s.mark("hlo", j))
                dve.wait_ge(*pe_s.at(i, "L"))
                dve.tensor_tensor(L[:, :, :], banks["L",][:, 0:NT * NS].rearrange("p (t s) -> p t s", t=NT),
                                  b2_bc[:, :].unsqueeze(1).to_broadcast([P, NT, NS]), ALU.add)\
                   .then_inc(*dve_s.mark("read", "L"))
                wait_apart(dve, dve_s.at(i, "read", "L"), passed)
                for t in range(NT):
                    dve.max(top[:, t, :], L[:, t, :]).then_inc(*dve_s.mark("top", t))
                wait_apart(dve, dve_s.at(i, "top", NT - 1), passed)
                for t in range(NT):
                    dve.match_replace(rest[:, t, :], top[:, t, :], L[:, t, :], -3e38).then_inc(*dve_s.mark("rest", t))
                dve.tensor_tensor(el[:, :, :], L[:, :, :], top[:, :, 0:1].to_broadcast([P, NT, NS]), ALU.subtract)\
                   .then_inc(*dve_s.mark("lshift"))
                dve.wait_ge(*dve_s.at(i, "rest", NT - 1))
                dve.tensor_tensor(rest[:, :, :], rest[:, :, :], L[:, :, :], ALU.not_equal).then_inc(*dve_s.mark("chosen"))
                dve.wait_ge(*dve_s.at(i, "chosen"))
                dve.wait_ge(*act_s.at(i, "lexp"))
                dve.tensor_tensor(el[:, :, :], el[:, :, :], rest[:, :, :], ALU.mult).then_inc(*dve_s.mark("kept"))
                dve.wait_ge(*dve_s.at(i, "kept"))
                dve.reduce_sum(asum[:, :], el[:, :, :], AX).then_inc(*dve_s.mark("asum"))
                dve.wait_ge(*dve_s.at(i, "asum"))
                dve.reciprocal(asum[:, :], asum[:, :]).then_inc(*dve_s.mark("rasum"))
                dve.wait_ge(*dve_s.at(i, "rasum"))
                dve.wait_ge(*pe_s.before(i, "si"))
                dve.tensor_tensor(alpha[:, :, :], el[:, :, :], asum[:, :].unsqueeze(2).to_broadcast([P, NT, NS]), ALU.mult)\
                   .then_inc(*dve_s.mark("alpha"))
                dve.wait_ge(*pe_s.at(i, "aT"))
                dve.wait_ge(aT_out, i * 16 + 16)
                dve.tensor_copy(aT[:, :], banks["aT",][0:NS, :]).then_inc(*dve_s.mark("aT"))
                dve.wait_ge(*pe_s.at(i, "si"))
                dve.tensor_scalar(den[:, :], banks["den",][0:NS, 0:1], 1e-8, None, ALU.add).then_inc(*dve_s.mark("read", "den"))
                dve.wait_ge(*dve_s.at(i, "read", "den"))
                dve.reciprocal(den[:, :], den[:, :]).then_inc(*dve_s.mark("rden"))
                dve.wait_ge(*dve_s.at(i, "rden"))
                dve.wait_ge(si_out, i * 16 + 16)
                dve.tensor_scalar(si[:, :], banks["si",][0:NS, :], den[:, :], None, ALU.mult).then_inc(*dve_s.mark("si"))


def vdiag(tile, C, HC, p, hd, sk):
    return tile[0:sk, :, :].rearrange("k c (h w) -> k c h w", h=HC)[:, :, :, 0:hd]



def build_slots(nc, orders, a, si_s, vo_s):
    B = si_s.shape[0]
    NS, D = a["L0_ffn_slot_init"].shape
    DQ = a["L0_ffn_wq"].shape[1]
    C = D // P
    BS = B * NS
    NP = BS // P
    SCALE = float(DQ) ** -0.5

    with ExitStack() as ctx:
        st = Stage(nc, ctx, "sl", orders)
        sb, sem = st.sb, st.sem
        ident = sb("ident", [P, P])
        minus_half = sb("minus_half", [P, NP])
        WihT = sb("WihT", [P, C, 3 * D])
        WhhT = sb("WhhT", [P, C, 3 * D])
        wq, wk = sb("wq", [P, C, DQ]), sb("wk", [P, C, DQ])
        wv, wvp, wo = (sb(n, [P, C, D]) for n in ("wv", "wvp", "wo"))
        S0T = sb("S0T", [P, C, NS])
        bih, bhh = sb("bih", [P, 3 * C]), sb("bhh", [P, 3 * C])
        bq, bk, bvp = sb("bq", [P, 1]), sb("bk", [P, 1]), sb("bvp", [P, C])
        bv_bc, g_bc, b_bc = (sb(n, [P, D]) for n in ("bv_bc", "g_bc", "b_bc"))
        si = sb("si", [P, NP, D])
        siT = sb("siT", [P, C, BS])
        gh = sb("gh", [P, 3 * C, NS])
        gate = [sb(f"gate{n}", [P, BS]) for n in range(3)]
        SnT = sb("SnT", [P, C, BS])
        qT, kT = sb("qT", [P, BS]), sb("kT", [P, BS])
        v = si
        A = sb("A", [P, NP, P])
        AT = sb("AT", [P, NP, P])
        amx, asum = sb("amx", [P, NP]), sb("asum", [P, NP])
        y = sb("y", [P, NP, D])
        stats, mv = sb("stats", [P, NP, 6]), sb("mv", [P, NP, 2])
        rstd = sb("rstd", [P, NP])
        yT = siT
        svT = SnT
        vo = y

        bank = [st.ps(f"bank{n}", [P, 512]) for n in range(8)]
        setup, small, si_in, out = sem("setup"), sem("small"), sem("si_in"), sem("out")
        w_in = {n: sem(n + "_in") for n in ("WihT", "WhhT", "wqk", "wv", "wvp", "wo")}
        pe_s, act_s, dve_s, pool_s = (st.steps(n) for n in ("products", "act", "dve", "rstd"))
        rows = lambda w: w.rearrange("(c p) n -> p c n", p=P)

        units = [("siT", c) for c in range(C)] + [("gh", n) for n in range(3)]
        units += [("gi", c, n) for c in range(C) for n in range(3)]
        units += [("q",), ("k",)] + [("v", j) for j in range(NP)]
        for j in range(NP):
            units += [("A", j), ("AT", j), ("y", j)]
        units += [("yT", c) for c in range(C)] + [("sv", c) for c in range(C)] + [("vo", j) for j in range(NP)]
        banks = Banks(bank, units)
        dve_s.alias(("read", "q"), ("q",))
        dve_s.alias(("read", "k"), ("k",))
        for j in range(NP):
            dve_s.alias(("read", "v", j), ("v", j))
            dve_s.alias(("read", "y", j), ("y+bv", j))
            dve_s.alias(("read", "AT", j), ("AT", j))
            dve_s.alias(("read", "vo", j), ("vo", j))
            act_s.alias(("read", "A", j), ("A", j, 1))
        for c in range(C):
            dve_s.alias(("read", "siT", c), ("siT", c))
            dve_s.alias(("read", "gi", c, 0), ("r in", c))
            dve_s.alias(("read", "gi", c, 1), ("z in", c))
            dve_s.alias(("read", "gi", c, 2), ("n in", c))
            dve_s.alias(("read", "yT", c), ("yT", c))
            dve_s.alias(("read", "sv", c), ("sv", c))
        for n in range(3):
            dve_s.alias(("read", "gh", n), ("gh", n, C - 1))

        block = ctx.enter_context(nc.Block())

        smalls = [(S0T[:, :, :], rows(a["slot_init_T"])), (bih[:, :], a["L0_ffn_bih"]), (bhh[:, :], a["L0_ffn_bhh"]),
                  (bq[:, :], a["L0_ffn_bq"]), (bk[:, :], a["L0_ffn_bk"]), (bvp[:, :], a["L0_ffn_bvp"]),
                  (bv_bc[:, :], a["L0_ffn_bv"].partition_broadcast(P)),
                  (g_bc[:, :], a["L0_ffn_ln_g"].partition_broadcast(P)),
                  (b_bc[:, :], a["L0_ffn_ln_b"].partition_broadcast(P))]

        @block.sync
        def _(sp):
            sp.dma_start(si[:, :, :], si_s.rearrange("(j b) s d -> (b s) j d", j=NP)).then_inc(si_in, 16)
            sp.dma_start(WhhT[:, :, :], rows(a["Whh_T"])).then_inc(w_in["WhhT"], 16)
            sp.dma_start(WihT[:, :, :], rows(a["Wih_T"])).then_inc(w_in["WihT"], 16)
            sp.dma_start(wq[:, :, :], rows(a["L0_ffn_wq"])).then_inc(w_in["wqk"], 16)
            sp.dma_start(wk[:, :, :], rows(a["L0_ffn_wk"])).then_inc(w_in["wqk"], 16)
            for n, t in (("wv", wv), ("wvp", wvp), ("wo", wo)):
                sp.dma_start(t[:, :, :], rows(a["L0_ffn_" + n])).then_inc(w_in[n], 16)
            for j in range(NP):
                sp.wait_ge(*dve_s.at(0, "vo", j))
                sp.dma_start(vo_s[2 * j:2 * j + 2].rearrange("b s d -> (b s) d"), vo[:, j, :]).then_inc(out, 16)
            sp.wait_ge(out, 16 * NP)

        @block.gpsimd
        def _(pool):
            pool.sem_inc(pool_s.sem, pool_s.per)
            make_identity(pool, ident, setup)
            pool.memset(minus_half[:, :], -0.5).then_inc(setup, 1)
            pool.memset(A[:, :, :], 0.0).then_inc(setup, 1)
            pool.wait_ge(*dve_s.at(0, "var"))
            pool.tensor_scalar(rstd[:, :], mv[:, :, 1], EPS, None, ALU.add).then_inc(*pool_s.mark("ve"))
            pool.wait_ge(*pool_s.at(0, "ve"))
            pool.tensor_tensor(rstd[:, :], rstd[:, :], minus_half[:, :], ALU.pow).then_inc(*pool_s.mark("rstd"))

        @block.tensor
        def _(pe):
            pe.sem_inc(pe_s.sem, pe_s.per)
            pe.wait_ge(setup, 4)
            pe.wait_ge(si_in, 16)

            def unit(*name):
                if banks.user_before(name)[1] is False:
                    take(pe, banks, (act_s, dve_s), 0, name)
                return banks[name]

            def matmuls(out, w, m0, m1, x, n0, n1):
                for k in range(C):
                    last = pe.matmul(out, w[:, k, m0:m1], x[:, k, n0:n1], start=(k == 0), stop=(k == C - 1))
                return last

            for c in range(C):
                ps = unit("siT", c)
                for j in range(NP):
                    m = pe.transpose(ps[:, j * P:(j + 1) * P], si[:, j, c * P:(c + 1) * P], ident[:, :])
                m.then_inc(*pe_s.mark("siT", c))
            pe.wait_ge(small, 16 * len(smalls))
            pe.wait_ge(w_in["WhhT"], 16)
            for n in range(3):
                ps = unit("gh", n)
                for c in range(C):
                    m = matmuls(ps[:, c * NS:(c + 1) * NS], WhhT, n * D + c * P, n * D + (c + 1) * P, S0T, 0, NS)
                m.then_inc(*pe_s.mark("gh", n))
            pe.wait_ge(w_in["WihT"], 16)
            pe.wait_ge(*dve_s.at(0, "siT", C - 1))
            for c in range(C):
                for n in range(3):
                    ps = unit("gi", c, n)
                    matmuls(ps[:, :], WihT, n * D + c * P, n * D + (c + 1) * P, siT, 0, BS).then_inc(*pe_s.mark("gi", c, n))
            pe.wait_ge(w_in["wqk"], 32)
            pe.wait_ge(*dve_s.at(0, "S", C - 1))
            for name, w in (("q", wq), ("k", wk)):
                ps = unit(name)
                matmuls(ps[:, :], w, 0, DQ, SnT, 0, BS).then_inc(*pe_s.mark(name))
            pe.wait_ge(w_in["wv"], 16)
            for j in range(NP):
                ps = unit("v", j)
                matmuls(ps[:, :], SnT, j * P, (j + 1) * P, wv, 0, D).then_inc(*pe_s.mark("v", j))
            for j in range(NP):
                ps = unit("A", j)
                pe.wait_ge(*dve_s.at(0, "k"))
                pe.matmul(ps[:, 0:P], qT[:, j * P:(j + 1) * P], kT[:, j * P:(j + 1) * P], start=True, stop=True)\
                  .then_inc(*pe_s.mark("A", j))
                ps = unit("AT", j)
                pe.wait_ge(*dve_s.at(0, "A", j))
                pe.transpose(ps[:, 0:P], A[:, j, :], ident[:, :]).then_inc(*pe_s.mark("AT", j))
                ps = unit("y", j)
                pe.wait_ge(*dve_s.at(0, "AT", j))
                for c in range(C):
                    cols = slice(c * P, (c + 1) * P)
                    pe.matmul(ps[:, cols], AT[:, j, :], v[:, j, cols], start=True, stop=False)
                    m = pe.matmul(ps[:, cols], SnT[:, c, j * P:(j + 1) * P], ident[:, :], start=False, stop=True)
                m.then_inc(*pe_s.mark("y", j))
            for c in range(C):
                ps = unit("yT", c)
                for j in range(NP):
                    pe.wait_ge(*dve_s.at(0, "yn", j))
                    m = pe.transpose(ps[:, j * P:(j + 1) * P], y[:, j, c * P:(c + 1) * P], ident[:, :])
                m.then_inc(*pe_s.mark("yT", c))
            pe.wait_ge(w_in["wvp"], 16)
            pe.wait_ge(*dve_s.at(0, "yT", C - 1))
            for c in range(C):
                ps = unit("sv", c)
                matmuls(ps[:, :], wvp, c * P, (c + 1) * P, yT, 0, BS).then_inc(*pe_s.mark("sv", c))
            pe.wait_ge(w_in["wo"], 16)
            pe.wait_ge(*dve_s.at(0, "sv", C - 1))
            for j in range(NP):
                ps = unit("vo", j)
                matmuls(ps[:, :], svT, j * P, (j + 1) * P, wo, 0, D).then_inc(*pe_s.mark("vo", j))

        @block.scalar
        def _(act):
            act.sem_inc(act_s.sem, act_s.per)
            for dst, src in smalls:
                act.dma_start(dst, src).then_inc(small, 16)
            act.wait_ge(small, 16 * len(smalls))
            for c in range(C):
                for n, (name, func) in enumerate((("r", ACT.Sigmoid), ("z", ACT.Sigmoid), ("n", ACT.Tanh))):
                    act.wait_ge(*dve_s.at(0, name + " in", c))
                    if name == "n":
                        act.wait_ge(*dve_s.at(0, "r*h", c))
                        act.activation(gate[n][:, :], gate[n][:, :], func, bias=bih[:, 2 * C + c:2 * C + c + 1])\
                           .then_inc(*act_s.mark(name, c))
                    else:
                        act.activation(gate[n][:, :], gate[n][:, :], func).then_inc(*act_s.mark(name, c))
            for j in range(NP):
                act.wait_ge(*dve_s.at(0, "amx", j))
                for b in range(2):
                    s = slice(b * NS, (b + 1) * NS)
                    act.activation(A[s, j, s], banks["A", j][s, s], ACT.Exp, scale=SCALE, bias=amx[s, j:j + 1],
                                   accum_out=asum[s, j:j + 1]).then_inc(*act_s.mark("A", j, b))

        @block.vector
        def _(dve):
            dve.sem_inc(dve_s.sem, dve_s.per)
            dve.wait_ge(setup, 4)
            dve.wait_ge(small, 16 * len(smalls))

            def copy(name, dst, *bias):
                dve.wait_ge(*pe_s.at(0, *name))
                if bias:
                    m = dve.tensor_scalar(dst, banks[name][:, :], bias[0], None, ALU.add)
                else:
                    m = dve.tensor_copy(dst, banks[name][:, 0:dst.shape[-1]])
                return m.then_inc(*dve_s.mark(*name))

            for c in range(C):
                copy(("siT", c), siT[:, c, :])
            dve.tensor_tensor(bhh[:, 0:2 * C], bhh[:, 0:2 * C], bih[:, 0:2 * C], ALU.add).then_inc(*dve_s.mark("b"))
            dve.wait_ge(*dve_s.at(0, "b"))
            for n in range(3):
                dve.wait_ge(*pe_s.at(0, "gh", n))
                for c in range(C):
                    g = n * C + c
                    dve.tensor_scalar(gh[:, g, :], banks["gh", n][:, c * NS:(c + 1) * NS], bhh[:, g:g + 1], None, ALU.add)\
                       .then_inc(*dve_s.mark("gh", n, c))
            dve.wait_ge(*dve_s.at(0, "gh", 2, C - 1))
            by_batch = lambda t: t.rearrange("p (b s) -> p b s", b=B)
            same = lambda t: t.unsqueeze(1).to_broadcast([P, B, NS])
            for c in range(C):
                r, z, n = (by_batch(g[:, :]) for g in gate)
                gi = [by_batch(banks["gi", c, m][:, :]) for m in range(3)]
                if c:
                    dve.wait_ge(*dve_s.at(0, "S", c - 1))
                dve.wait_ge(*pe_s.at(0, "gi", c, 0))
                dve.tensor_tensor(r, gi[0], same(gh[:, c, :]), ALU.add).then_inc(*dve_s.mark("r in", c))
                dve.wait_ge(*pe_s.at(0, "gi", c, 1))
                dve.tensor_tensor(z, gi[1], same(gh[:, C + c, :]), ALU.add).then_inc(*dve_s.mark("z in", c))
                dve.wait_ge(*act_s.at(0, "r", c))
                dve.tensor_tensor(r, r, same(gh[:, 2 * C + c, :]), ALU.mult).then_inc(*dve_s.mark("r*h", c))
                dve.wait_ge(*dve_s.at(0, "r*h", c))
                dve.wait_ge(*pe_s.at(0, "gi", c, 2))
                dve.tensor_tensor(n, gi[2], r, ALU.add).then_inc(*dve_s.mark("n in", c))
                dve.wait_ge(*act_s.at(0, "n", c))
                dve.tensor_tensor(r, same(S0T[:, c, :]), n, ALU.subtract).then_inc(*dve_s.mark("S0-n", c))
                dve.wait_ge(*dve_s.at(0, "S0-n", c))
                dve.tensor_tensor(r, r, z, ALU.mult).then_inc(*dve_s.mark("z*", c))
                dve.wait_ge(*dve_s.at(0, "z*", c))
                dve.tensor_tensor(by_batch(SnT[:, c, :]), r, n, ALU.add).then_inc(*dve_s.mark("S", c))
            copy(("q",), qT[:, :], bq[:, 0:1])
            copy(("k",), kT[:, :], bk[:, 0:1])
            for j in range(NP):
                copy(("v", j), v[:, j, :])
            for j in range(NP):
                dve.wait_ge(*pe_s.at(0, "A", j))
                for b in range(2):
                    s = slice(b * NS, (b + 1) * NS)
                    m = dve.reduce_max(amx[s, j:j + 1], banks["A", j][s, s], AX)
                m.then_inc(*dve_s.mark("max", j))
                dve.wait_ge(*dve_s.at(0, "max", j))
                dve.tensor_scalar(amx[:, j:j + 1], amx[:, j:j + 1], -SCALE, None, ALU.mult).then_inc(*dve_s.mark("amx", j))
                dve.wait_ge(*act_s.at(0, "A", j, 1))
                dve.reciprocal(asum[:, j:j + 1], asum[:, j:j + 1]).then_inc(*dve_s.mark("rsum", j))
                dve.wait_ge(*dve_s.at(0, "rsum", j))
                dve.tensor_scalar(A[:, j, :], A[:, j, :], asum[:, j:j + 1], None, ALU.mult).then_inc(*dve_s.mark("A", j))
                copy(("AT", j), AT[:, j, :])
                dve.wait_ge(*pe_s.at(0, "y", j))
                dve.tensor_tensor(y[:, j, :], banks["y", j][:, :], bv_bc[:, :], ALU.add).then_inc(*dve_s.mark("y+bv", j))
                dve.wait_ge(*dve_s.at(0, "y+bv", j))
                dve.bn_stats(stats[:, j, :], y[:, j, :]).then_inc(*dve_s.mark("stats", j))
                dve.wait_ge(*dve_s.at(0, "stats", j))
                m = dve.bn_aggr(mv[:, j, :], stats[:, j, :])
            m.then_inc(*dve_s.mark("var"))
            dve.wait_ge(*dve_s.at(0, "var"))
            dve.wait_ge(*pool_s.at(0, "rstd"))
            for j in range(NP):
                dve.tensor_scalar(y[:, j, :], y[:, j, :], mv[:, j, 0:1], rstd[:, j:j + 1], ALU.subtract, ALU.mult)\
                   .then_inc(*dve_s.mark("normed", j))
                dve.wait_ge(*dve_s.at(0, "normed", j))
                dve.tensor_tensor(y[:, j, :], y[:, j, :], g_bc[:, :], ALU.mult).then_inc(*dve_s.mark("*g", j))
                dve.wait_ge(*dve_s.at(0, "*g", j))
                dve.tensor_tensor(y[:, j, :], y[:, j, :], b_bc[:, :], ALU.add).then_inc(*dve_s.mark("yn", j))
            for c in range(C):
                copy(("yT", c), yT[:, c, :])
            for c in range(C):
                copy(("sv", c), svT[:, c, :], bvp[:, c:c + 1])
            for j in range(NP):
                copy(("vo", j), vo[:, j, :])



def build_latents(nc, orders, a, x1_s, alphaT_s, vo_s, x2_s, z_s):
    B, T, D = x1_s.shape
    SK = a["ctx_1024"].shape[1]
    Z = z_s[0].shape[3]
    C, NT = D // P, T // P
    NS = vo_s.shape[1]
    NL = NT + 1

    with ExitStack() as ctx:
        st = Stage(nc, ctx, "la", orders)
        sb, sem = st.sb, st.sem
        two = lambda name, shape, dt=F32: [sb(f"{name}{n}", shape, dt) for n in range(2)]
        ident = sb("ident", [P, P])
        minus_half = sb("minus_half", [P, NL])
        ones = sb("ones", [1, P])
        bo = sb("bo", [1, D])
        gain = {n: (sb(n + "g", [P, C]), sb(n + "b", [P, C])) for n in ("x", "l")}
        x1, x2 = two("x1", [P, NT, D]), two("x2", [P, NT, D])
        aT, vo, cx = two("aT", [NS, T]), two("vo", [NS, D]), two("cx", [SK, D])
        stats, mv = two("stats", [P, NL, 6]), two("mv", [P, NL, 2])
        ve, rstd = two("ve", [P, NL]), two("rstd", [P, NL])
        xn, cn = two("xn", [P, NT, D]), two("cn", [SK, D])
        full = two("full", [P, C, Z])
        z_hi, z_lo = two("z_hi", [P, C, Z], F32R), two("z_lo", [P, C, Z], F32R)
        bank = [st.ps(f"bank{n}", [P, 512]) for n in range(8)]

        setup, small = sem("setup"), sem("small")
        passed = sem("passed")
        ins = [{n: sem(f"{n}_in{m}") for n in ("x1", "aT", "vo", "cx")} for m in range(2)]
        x2_out, z_out = [sem(f"x2_out{m}") for m in range(2)], [sem(f"z_out{m}") for m in range(2)]
        pe_s, act_s, dve_s, pool_s = (st.steps(n) for n in ("products", "act", "dve", "rstd"))

        units = []
        for m in range(2):
            units += [("x2", m, t) for t in range(NT)] + [("zT", m, c) for c in range(C)] + [("cT", m)]
        banks = Banks(bank, units)
        for m in range(2):
            for t in range(NT):
                dve_s.alias(("read", "x2", m, t), ("x2", m, t))
            for c in range(C):
                act_s.alias(("read", "zT", m, c), ("full", m, c))
            act_s.alias(("read", "cT", m), ("full", m, C, C - 1))

        smalls = [(bo[:, :], a["L0_ffn_bo"].rearrange("(o n) -> o n", o=1))]
        for n in gain:
            smalls += [(gain[n][0][:, :], a[f"L1_xattn_ln_{n}_g"]), (gain[n][1][:, :], a[f"L1_xattn_ln_{n}_b"])]
        PAIRS = B // 2
        block = ctx.enter_context(nc.Block())

        @block.sync
        def _(sp):
            for dst, src in smalls:
                sp.dma_start(dst, src).then_inc(small, 16)
            with sp.Fori(0, PAIRS) as i:
                for m in range(2):
                    one = lambda ap: ap[bass.ds(2 * i + m, 1)]
                    sp.wait_ge(*dve_s.before(i, "x2", m, NT - 1))
                    sp.dma_start(x1[m][:, :, :], one(x1_s).rearrange("b (t p) d -> p (b t) d", p=P)).then_inc(ins[m]["x1"], 16)
                    sp.dma_start(aT[m][:, :], one(alphaT_s).rearrange("b s t -> (b s) t")).then_inc(ins[m]["aT"], 16)
                    sp.dma_start(vo[m][:, :], one(vo_s).rearrange("b s d -> (b s) d")).then_inc(ins[m]["vo"], 16)
                    sp.wait_ge(*dve_s.before(i, "cn", m))
                    sp.dma_start(cx[m][:, :], one(a["ctx_1024"]).rearrange("b s d -> (b s) d")).then_inc(ins[m]["cx"], 16)

        @block.gpsimd
        def _(pool):
            pool.sem_inc(pool_s.sem, pool_s.per)
            make_identity(pool, ident, setup)
            pool.memset(minus_half[:, :], -0.5).then_inc(setup, 1)
            pool.memset(ones[:, :], 1.0).then_inc(setup, 1)
            for m in range(2):
                pool.memset(mv[m][:, :, :], 1.0).then_inc(setup, 1)
                pool.memset(full[m][:, :, :], 0.0).then_inc(setup, 1)
            with pool.Fori(0, PAIRS) as i:
                for m in range(2):
                    wait_apart(pool, dve_s.at(i, "var", m), passed)
                    pool.tensor_scalar(ve[m][:, 0:NT], mv[m][:, 0:NT, 1], 1.0 + EPS, EPS * EPS, ALU.mult, ALU.add)\
                        .then_inc(*pool_s.mark("ve", m))
                    pool.tensor_scalar(ve[m][:, NT:NL], mv[m][:, NT:NL, 1], EPS, None, ALU.add).then_inc(*pool_s.mark("vc", m))
                    pool.wait_ge(*pool_s.at(i, "vc", m))
                    pool.tensor_tensor(rstd[m][:, :], ve[m][:, :], minus_half[:, :], ALU.pow).then_inc(*pool_s.mark("rstd", m))

        @block.tensor
        def _(pe):
            pe.sem_inc(pe_s.sem, pe_s.per)
            pe.wait_ge(setup, 8)
            pe.wait_ge(small, 16 * len(smalls))
            with pe.Fori(0, PAIRS) as i:
                def unit(*name):
                    take(pe, banks, (act_s, dve_s), i, name)
                    return banks[name]

                for m in range(2):
                    pe.wait_ge(ins[m]["aT"], i * 16 + 16)
                    pe.wait_ge(ins[m]["vo"], i * 16 + 16)
                    for t in range(NT):
                        ps = unit("x2", m, t)
                        pe.matmul(ps[:, :], ones[:, :], bo[:, :], start=True, stop=False)
                        pe.matmul(ps[:, :], aT[m][:, t * P:(t + 1) * P], vo[m][:, :], start=False, stop=True)\
                          .then_inc(*pe_s.mark("x2", m, t))
                    for c in range(C):
                        ps = unit("zT", m, c)
                        for t in range(NT):
                            if c == 0:
                                pe.wait_ge(*dve_s.at(i, "xn", m, t))
                            tr = pe.transpose(ps[:, t * P:(t + 1) * P], xn[m][:, t, c * P:(c + 1) * P], ident[:, :])
                        tr.then_inc(*pe_s.mark("zT", m, c))
                    ps = unit("cT", m)
                    pe.wait_ge(*dve_s.at(i, "cn", m))
                    for c in range(C):
                        tr = pe.transpose(ps[:, c * SK:(c + 1) * SK], cn[m][:, c * P:(c + 1) * P], ident[0:SK, 0:SK])
                    tr.then_inc(*pe_s.mark("cT", m))

        @block.scalar
        def _(act):
            act.sem_inc(act_s.sem, act_s.per)
            for m in range(2):
                act.sem_inc(x2_out[m], 16)
                act.sem_inc(z_out[m], 32)
            act.wait_ge(small, 16 * len(smalls))
            act.wait_ge(setup, 8)
            with act.Fori(0, PAIRS) as i:
                for m in range(2):
                    act.wait_ge(*dve_s.before(i, "lo", m, C - 1))
                    act.wait_ge(z_out[m], i * 32 + 32)
                    for c in range(C):
                        act.wait_ge(*pe_s.at(i, "zT", m, c))
                        act.activation(full[m][:, c, 0:T], banks["zT", m, c][:, :], ACT.Identity,
                                       scale=gain["l"][0][:, c:c + 1], bias=gain["l"][1][:, c:c + 1])\
                           .then_inc(*act_s.mark("full", m, c))
                    act.wait_ge(*pe_s.at(i, "cT", m))
                    for c in range(C):
                        act.activation(full[m][:, c, T:T + SK], banks["cT", m][:, c * SK:(c + 1) * SK], ACT.Identity,
                                       scale=gain["x"][0][:, c:c + 1], bias=gain["x"][1][:, c:c + 1])\
                           .then_inc(*act_s.mark("full", m, C, c))
                    for c in range(C):
                        act.wait_ge(*act_s.at(i, "full", m, C, C - 1))
                        act.activation(z_hi[m][:, c, :], full[m][:, c, :], ACT.Copy).then_inc(*act_s.mark("hi", m, c))
                    act.wait_ge(*dve_s.at(i, "x2", m, NT - 1))
                    act.dma_start(x2_s[bass.ds(2 * i + m, 1)].rearrange("b (t p) d -> p (b t) d", p=P), x2[m][:, :, :])\
                       .then_inc(x2_out[m], 16)
                    act.wait_ge(*dve_s.at(i, "lo", m, C - 1))
                    act.dma_start(z_s[0][bass.ds(2 * i + m, 1)].rearrange("b p c z -> p (b c) z"), f32(z_hi[m][:, :, :])).then_inc(z_out[m], 16)
                    act.dma_start(z_s[1][bass.ds(2 * i + m, 1)].rearrange("b p c z -> p (b c) z"), f32(z_lo[m][:, :, :])).then_inc(z_out[m], 16)
            for m in range(2):
                act.wait_ge(x2_out[m], 16 * (PAIRS + 1))
                act.wait_ge(z_out[m], 32 * (PAIRS + 1))

        @block.vector
        def _(dve):
            dve.sem_inc(dve_s.sem, dve_s.per)
            dve.wait_ge(setup, 8)
            with dve.Fori(0, PAIRS) as i:
                for m in range(2):
                    dve.wait_ge(ins[m]["x1"], i * 16 + 16)
                    dve.wait_ge(x2_out[m], i * 16 + 16)
                    for t in range(NT):
                        dve.wait_ge(*pe_s.at(i, "x2", m, t))
                        dve.tensor_tensor(x2[m][:, t, :], banks["x2", m, t][:, :], x1[m][:, t, :], ALU.add)\
                           .then_inc(*dve_s.mark("x2", m, t))
                        dve.wait_ge(*dve_s.at(i, "x2", m, t))
                        dve.bn_stats(stats[m][:, t, :], x2[m][:, t, :]).then_inc(*dve_s.mark("stats", m, t))
                    dve.wait_ge(ins[m]["cx"], i * 16 + 16)
                    dve.bn_stats(stats[m][0:SK, NT, :], cx[m][:, :]).then_inc(*dve_s.mark("stats", m, NT))
                    wait_apart(dve, dve_s.at(i, "stats", m, NT), passed)
                    for t in range(NL):
                        rows = slice(0, SK if t == NT else P)
                        last = dve.bn_aggr(mv[m][rows, t, :], stats[m][rows, t, :])
                    last.then_inc(*dve_s.mark("var", m))
                    dve.wait_ge(*dve_s.at(i, "var", m))
                    dve.wait_ge(*pool_s.at(i, "rstd", m))
                    dve.wait_ge(*pe_s.before(i, "cT", m))
                    for t in range(NT):
                        dve.tensor_scalar(xn[m][:, t, :], x2[m][:, t, :], mv[m][:, t, 0:1], rstd[m][:, t:t + 1],
                                          ALU.subtract, ALU.mult).then_inc(*dve_s.mark("xn", m, t))
                    dve.tensor_scalar(cn[m][:, :], cx[m][:, :], mv[m][0:SK, NT, 0:1], rstd[m][0:SK, NT:NL],
                                      ALU.subtract, ALU.mult).then_inc(*dve_s.mark("cn", m))
                    for c in range(C):
                        dve.wait_ge(*act_s.at(i, "hi", m, c))
                        dve.tensor_tensor(z_lo[m][:, c, :], full[m][:, c, :], f32(z_hi[m][:, c, :]), ALU.subtract)\
                           .then_inc(*dve_s.mark("lo", m, c))



class Claims:

    def __init__(self, name, orders):
        self.known, self.order = orders.get(name), []
        orders[name] = self.order

    def before(self, bank, unit):
        self.order.append((bank, unit))
        if not self.known:
            return unit, True
        n = len(self.order) - 1
        earlier = [u for b, u in self.known[:n] if b == bank]
        if earlier:
            return earlier[-1], False
        return [u for b, u in self.known if b == bank][-1], True


def build_perceiver(nc, orders, a, z_s, o_s):
    B = z_s[0].shape[0]
    C, Z = z_s[0].shape[2], z_s[0].shape[3]
    INNER = a["L1_xattn_Wq"].shape[1]
    SK = a["ctx_1024"].shape[1]
    T = a["x"].shape[1]
    SKP = Z - T
    NK = T + SK
    NT = T // P
    HD, H = 64, INNER // 64
    NPAIR = H // 2
    NC = NT + 1
    QH = 4
    SCALE = HD ** -0.5
    MASKED = 2.0 ** 126
    KEYS = [P] * NT + [SK]

    with ExitStack() as ctx:
        st = Stage(nc, ctx, "pa", orders)
        sb, sem = st.sb, st.sem
        two = lambda name, shape, dt=F32: [sb(f"{name}{n}", shape, dt) for n in range(2)]
        pair = lambda name, shape: (sb(name + "_hi", shape, F32R), sb(name + "_lo", shape, F32R))
        ident = sb("ident", [P, P])
        one_row = sb("one_row", [1, P])
        ones = sb("ones", [1, P], F32R)
        mask_words = sb("mask_words", [1, B * SK // 4], I32)
        mask_u = mask_words[:, :].bitcast(mybir.dt.uint8)
        mrow = sb("mrow", [1, B, SKP], F32R)
        z = pair("z", [P, C, Z])
        Wq = pair("Wq", [P, C, INNER])
        Wkv = pair("Wkv", [P, C, 2 * INNER])
        U = [two(f"U{m}", [P, T], F32R) for m in range(2)]
        Uc = two("Uc", [P, NPAIR, SKP], F32R)
        Qh = [two(f"Qh{m}", [P, T], F32R) for m in range(2)]
        Ql = [two(f"Ql{m}", [P, T], F32R) for m in range(2)]
        V = two("V", [P, NC, QH, P], F32R)
        Pr = two("Pr", [P, NT, NK + 1])
        RING = 4
        PTh, PTl = (sb(n, [P, RING, T], F32R) for n in ("PTh", "PTl"))
        low = sb("low", [HD, T])
        O = sb("O_pair", [P, T])
        mx, nb, rs = (sb(n, [P, 2, NT]) for n in ("mx", "nb", "rs"))

        S = [st.ps(f"S{n}", [P, 1024]) for n in range(2)]
        bank = {n: st.ps(n, [P, 512]) for n in ("T0", "T1", "O", "J")}

        setup, mask_in, consts = sem("setup"), sem("mask_in"), sem("consts")
        z_in = sem("z_in")
        dup = [sem(f"dup{m}") for m in range(2)]
        o_out = sem("o_out")
        pe_s, act_s, dve_s = (st.steps(n) for n in ("products", "act", "dve"))
        claims = Claims("pa_banks", orders)
        for h in range(H):
            dve_s.alias(("read", "O", h), ("O", h))

        rows = lambda w: w.rearrange("(c p) n -> p c n", p=P)
        weights = []
        half = lambda w, n: w[:, :, n * 512:(n + 1) * 512]
        for n in (2, 3, 0, 1):
            weights.append((half(rows(a["L1_xattn_Wkv"]), n), half(Wkv[0], n), half(Wkv[1], n)))
        for n in range(2):
            weights.append((half(rows(a["L1_xattn_Wq"]), n), half(Wq[0], n), half(Wq[1], n)))
        slots = [t[:, :, :].rearrange("p t k -> p (t k)")[:, 0:2048] for t in Pr]
        w_sync, w_scalar, w_vector, w_cut = load_and_split(st, weights, "w", slots)

        work = [("Kc", 0), ("Kc", 1), ("Q", 0), ("K", 0)] + [("V", 0, j) for j in range(NC)]
        extra = {}
        for p in range(NPAIR - 1):
            extra[2 * p, 0], extra[2 * p, 1] = ("Q", p + 1), ("K", p + 1)
        for q in range(H // QH - 1):
            for j in range(NC):
                extra[QH * q + (1 if j < 3 else 3), j % 3] = ("V", q + 1, j)
        for h in range(H + 1):
            for t in range(NT):
                if h < H:
                    work.append(("S", h, t))
                if h:
                    work.append(("T", h - 1, t))
                    if t:
                        work.append(("PV", h - 1, t - 1))
                if (h, t) in extra:
                    work.append(extra[h, t])
            if h:
                work += [("T", h - 1, NT), ("PV", h - 1, NT - 1), ("PV", h - 1, NT), ("O", h - 1)]
        lead = iter(["T0", "T1", "O", "J"] * 3)
        lead_bank = {u: next(lead) for u in work[:4 + NC]}

        def bank_of(u):
            if u in lead_bank:
                return lead_bank[u]
            if u[0] == "T":
                return "T%d" % ((u[1] * NC + u[2]) % 2)
            return "O" if u[0] == "PV" else "J"

        last_projection = [u for u in work if u[0] in ("Kc", "Q", "K", "V")][-1]
        ring = lambda h, c: (h * NC + c) % RING

        def wait(engine, signal, i, earlier, *name):
            engine.wait_ge(*(signal.before if earlier else signal.at)(i, *name))

        block = ctx.enter_context(nc.Block())

        @block.sync
        def _(sp):
            sp.dma_start(mask_words[:, :], a["mask_BxS2_bk0"]).then_inc(mask_in, 16)
            w_sync(sp)
            with sp.Fori(0, B) as i:
                sp.wait_ge(*pe_s.before(i, *last_projection))
                for n in range(2):
                    sp.dma_start(f32(z[n][:, :, :]), z_s[n][bass.ds(i, 1)].rearrange("b p c z -> p (b c) z")).then_inc(z_in, 16)
                for p in range(NPAIR):
                    m = p % 2
                    sp.wait_ge(*act_s.at(i, "hi", "Q", p, 0))
                    sp.dma_start(f32(Qh[m][0][HD:P, :]), f32(Qh[m][0][0:HD, :])).then_inc(dup[m], 16)
                    sp.wait_ge(*act_s.at(i, "hi", "Q", p, 1))
                    sp.dma_start(f32(Qh[m][1][0:HD, :]), f32(Qh[m][1][HD:P, :])).then_inc(dup[m], 16)

        @block.gpsimd
        def _(pool):
            make_identity(pool, ident, setup)
            pool.memset(one_row[:, :], 1.0).then_inc(setup, 1)
            pool.memset(f32(mrow[:, :, :]), 0.0).then_inc(setup, 1)
            for m in range(2):
                for x in range(2):
                    pool.memset(f32(Ql[m][x][:, :]), 0.0).then_inc(setup, 1)

        @block.tensor
        def _(pe):
            pe.sem_inc(pe_s.sem, pe_s.per)
            pe.wait_ge(setup, 8)
            pe.wait_ge(consts, 2)
            w_cut(pe)
            with pe.Fori(0, B) as i:
                def claim(u, b):
                    last, earlier = claims.before(b, u)
                    for s in (act_s, dve_s):
                        if s.has("read", *last):
                            wait(pe, s, i, earlier, "read", *last)
                    return bank[b] if b in bank else S[int(b[1])]

                for u in work:
                    kind = u[0]
                    if kind == "Kc":
                        if u[1] == 0:
                            pe.wait_ge(z_in, i * 32 + 32)
                        ps = claim(u, bank_of(u))
                        for n in range(NPAIR // 2):
                            p = u[1] * (NPAIR // 2) + n
                            for k in range(C):
                                last = product(pe, ps[:, n * SKP:(n + 1) * SKP], [w[:, k, p * P:(p + 1) * P] for w in Wkv],
                                               [x[:, k, T:Z] for x in z], k == 0, k == C - 1)
                        last.then_inc(*pe_s.mark(*u))
                    elif kind in ("Q", "K"):
                        ps = claim(u, bank_of(u))
                        for k in range(C):
                            last = product(pe, ps[:, :], [w[:, k, u[1] * P:(u[1] + 1) * P] for w in (Wq if kind == "Q" else Wkv)],
                                           [x[:, k, 0:T] for x in z], k == 0, k == C - 1)
                        last.then_inc(*pe_s.mark(*u))
                    elif kind == "V":
                        _, q, j = u
                        ps = claim(u, bank_of(u))
                        n0 = INNER + q * QH * HD
                        for k in range(C):
                            last = product(pe, ps[0:KEYS[j], 0:QH * HD], [x[:, k, j * P:j * P + KEYS[j]] for x in z],
                                           [w[:, k, n0:n0 + QH * HD] for w in Wkv], k == 0, k == C - 1)
                        last.then_inc(*pe_s.mark(*u))
                    elif kind == "S":
                        _, h, t = u
                        p, x = h // 2, h % 2
                        if t == 0 and x == 0:
                            pe.wait_ge(dup[p % 2], (i * (NPAIR // 2) + (p // 2 + 1)) * 32)
                            pe.wait_ge(*dve_s.at(i, "read", "K", p))
                        ps = claim(u, "S%d" % (t % 2))
                        cols = slice(t * P, (t + 1) * P)
                        qh, ql = Qh[p % 2][x][:, cols], Ql[p % 2][x][:, cols]
                        pe.matmul(ps[:, 0:T], qh, U[p % 2][x][:, :], start=True, stop=False)
                        pe.matmul(ps[:, 0:T], ql, U[p % 2][x][:, :], start=False, stop=True)
                        out = ps[:, T:Z]
                        pe.matmul(out, qh, Uc[x][:, p, :], start=True, stop=False)
                        pe.matmul(out, ql, Uc[x][:, p, :], start=False, stop=False)
                        pe.matmul(out, ones[:, :], mrow[:, bass.ds(i, 1), :].rearrange("o b s -> o (b s)"),
                                  start=False, stop=True).then_inc(*pe_s.mark(*u))
                    elif kind == "T":
                        _, h, c = u
                        if c == 0:
                            claims.before(bank_of(u), u)
                            ps = bank[bank_of(u)]
                            pe.wait_ge(*dve_s.at(i, "probs", h, NT - 1))
                        else:
                            ps = claim(u, bank_of(u))
                        for t in range(NT):
                            m = pe.transpose(ps[0:KEYS[c], t * P:(t + 1) * P], Pr[h % 2][:, t, c * P:c * P + KEYS[c]], ident[:, :])
                        m.then_inc(*pe_s.mark(*u))
                    elif kind == "PV":
                        _, h, c = u
                        if c == 0:
                            claims.before("O", ("O", h))
                        ps, r, n = bank["O"], ring(h, c), KEYS[c]
                        v = V[(h // QH) % 2][0:n, c, h % QH, :]
                        pe.wait_ge(*dve_s.at(i, "read", "T", h, c))
                        pe.matmul(ps[:, :], v, PTh[0:n, r, :], start=(c == 0), stop=False)
                        pe.matmul(ps[:, :], v, PTl[0:n, r, :], start=False, stop=(c == NC - 1)).then_inc(*pe_s.mark(*u))

        @block.scalar
        def _(act):
            act.sem_inc(act_s.sem, act_s.per)
            act.sem_inc(o_out, 16)
            w_scalar(act)
            with act.Fori(0, B) as i:
                def copy(out, src, *name):
                    act.activation(out, src, ACT.Copy).then_inc(*act_s.mark(*name))

                def store(p):
                    act.wait_ge(*dve_s.at(i, "O", 2 * p + 1))
                    act.dma_start(o_s[bass.ds(i, 1), p].rearrange("b p t -> (b p) t"), O[:, :]).then_inc(o_out, 16)

                for u in work:
                    kind = u[0]
                    if kind in ("Kc", "Q", "K", "V", "T"):
                        act.wait_ge(*pe_s.at(i, *u))
                    ps = None if kind in ("S", "O", "PV") else bank[bank_of(u)]
                    if kind == "Kc":
                        for x in range(2):
                            r = slice(x * HD, (x + 1) * HD)
                            g = slice(u[1] * (NPAIR // 2), (u[1] + 1) * (NPAIR // 2))
                            copy(Uc[x][r, g, :], ps[r, 0:(NPAIR // 2) * SKP].rearrange("p (g s) -> p g s", s=SKP), "hi", *u, x)
                    elif kind in ("Q", "K"):
                        p = u[1]
                        for x in range(2):
                            r = slice(x * HD, (x + 1) * HD)
                            copy((Qh if kind == "Q" else U)[p % 2][x][r, :], ps[r, :], "hi", *u, x)
                    elif kind == "V":
                        _, q, j = u
                        n = KEYS[j]
                        copy(V[q % 2][0:n, j, :, 0:HD], ps[0:n, 0:QH * HD].rearrange("p (h d) -> p h d", d=HD), "hi", *u)
                    elif kind == "S":
                        _, h, t = u
                        if t == 1 and h % 2 and h >= 3:
                            store((h - 3) // 2)
                        act.wait_ge(*dve_s.at(i, "bias", h, t))
                        act.activation(Pr[h % 2][:, t, 0:NK], S[t % 2][:, 0:NK], ACT.Exp, scale=SCALE,
                                       bias=nb[:, h % 2, t:t + 1], accum_out=rs[:, h % 2, t:t + 1])\
                           .then_inc(*act_s.mark("read", *u))
                    elif kind == "T":
                        _, h, c = u
                        copy(PTh[0:KEYS[c], ring(h, c), :], ps[0:KEYS[c], :], "hi", *u)
                    elif kind == "O":
                        h = u[1]
                        act.wait_ge(*pe_s.at(i, "PV", h, NC - 1))
                        copy(low[:, :], bank["O"][HD:P, :], "low", h)
                store(NPAIR - 1)
            act.wait_ge(o_out, 16 * (B * NPAIR + 1))

        @block.vector
        def _(dve):
            dve.sem_inc(dve_s.sem, dve_s.per)
            dve.wait_ge(setup, 8)
            dve.tensor_copy(ones[:, :], one_row[:, :]).then_inc(consts, 1)
            dve.wait_ge(mask_in, 16)
            dve.tensor_scalar(mrow[:, :, 0:SK], mask_u.rearrange("o (b s) -> o b s", b=B), 1.0, MASKED,
                              ALU.subtract, ALU.mult).then_inc(consts, 1)
            w_vector(dve)
            with dve.Fori(0, B) as i:
                def lo(out, src, hi_ap, *name):
                    dve.tensor_tensor(out, src, f32(hi_ap), ALU.subtract).then_inc(*dve_s.mark(*name))

                def normalise(h, t):
                    dve.wait_ge(*act_s.at(i, "read", "S", h, t))
                    r = rs[:, h % 2, t:t + 1]
                    dve.reciprocal(r, r).then_inc(*dve_s.mark("rsum", h, t))
                    dve.wait_ge(*dve_s.at(i, "rsum", h, t))
                    p = Pr[h % 2][:, t, 0:NK]
                    dve.tensor_scalar(p, p, r, None, ALU.mult).then_inc(*dve_s.mark("probs", h, t))

                pending = []
                for u in work:
                    kind = u[0]
                    ps = None if kind in ("S", "O", "PV") else bank[bank_of(u)]
                    if kind == "Kc":
                        for x in range(2):
                            r, o = slice(x * HD, (x + 1) * HD), slice((1 - x) * HD, (2 - x) * HD)
                            g = slice(u[1] * (NPAIR // 2), (u[1] + 1) * (NPAIR // 2))
                            dve.wait_ge(*act_s.at(i, "hi", *u, x))
                            lo(Uc[x][o, g, :], ps[r, 0:(NPAIR // 2) * SKP].rearrange("p (g s) -> p g s", s=SKP), Uc[x][r, g, :],
                               *(("read", *u) if x else ("lo", *u)))
                    elif kind in ("Q", "K"):
                        p = u[1]
                        for x in range(2):
                            r, o = slice(x * HD, (x + 1) * HD), slice((1 - x) * HD, (2 - x) * HD)
                            dve.wait_ge(*act_s.at(i, "hi", *u, x))
                            hi_ap = (Qh if kind == "Q" else U)[p % 2][x][r, :]
                            out = Ql[p % 2][x][r, :] if kind == "Q" else U[p % 2][x][o, :]
                            lo(out, ps[r, :], hi_ap, *(("read", *u) if x else ("lo", *u)))
                    elif kind == "V":
                        _, q, j = u
                        n = KEYS[j]
                        dve.wait_ge(*act_s.at(i, "hi", *u))
                        lo(V[q % 2][0:n, j, :, HD:P], ps[0:n, 0:QH * HD].rearrange("p (h d) -> p h d", d=HD),
                           V[q % 2][0:n, j, :, 0:HD], "read", *u)
                    elif kind == "S":
                        _, h, t = u
                        dve.wait_ge(*pe_s.at(i, *u))
                        m = mx[:, h % 2, t:t + 1]
                        dve.reduce_max(m, S[t % 2][:, 0:NK], AX).then_inc(*dve_s.mark("max", h, t))
                        dve.wait_ge(*dve_s.at(i, "max", h, t))
                        dve.tensor_scalar(nb[:, h % 2, t:t + 1], m, -SCALE, None, ALU.mult).then_inc(*dve_s.mark("bias", h, t))
                        for e in pending:
                            normalise(*e)
                        pending = [(h, t)]
                    elif kind == "T":
                        for e in pending:
                            if e[0] == u[1]:
                                normalise(*e)
                        pending = [e for e in pending if e[0] != u[1]]
                        _, h, c = u
                        dve.wait_ge(*act_s.at(i, "hi", *u))
                        n, r = KEYS[c], ring(h, c)
                        lo(PTl[0:n, r, :], ps[0:n, :], PTh[0:n, r, :], "read", *u)
                    elif kind == "O":
                        h = u[1]
                        p = h // 2
                        dve.wait_ge(*act_s.at(i, "low", h))
                        if h % 2 == 0:
                            dve.wait_ge(o_out, (i * NPAIR + (p + 1)) * 16)
                        dve.tensor_tensor(O[(h % 2) * HD:(h % 2 + 1) * HD, :], bank["O"][0:HD, :], low[:, :], ALU.add)\
                           .then_inc(*dve_s.mark("O", h))



def build_experts(nc, orders, a, o_s, x2_s, out):
    B, T, D = a["x"].shape
    C, NT = D // P, T // P
    K = a["L1_xattn_Wout"].shape[0] // P
    E, _, HE = a["L1_ffn_W1"].shape
    RING = 4

    with ExitStack() as ctx:
        st = Stage(nc, ctx, "ex", orders)
        sb, sem = st.sb, st.sem
        pair = lambda name, shape: (sb(name + "_hi", shape, F32R), sb(name + "_lo", shape, F32R))
        ident = sb("ident", [P, P])
        eight = sb("eight", [P, E])
        minus_half = sb("minus_half", [P, NT])
        sel_f = sb("sel_f", [E, E, P])
        sel = sb("sel", [E, E, P], F32R)
        Wout = pair("Wout", [P, K, D])
        W1 = pair("W1", [HE, E * C, HE])
        W2 = pair("W2", [HE, E, D])
        Wg = pair("Wg", [P, C, E])
        Wg_raw = sb("Wg_raw", [P, C, E])
        b2 = pair("b2", [E, D])
        b2_raw = sel_f[:, :, :].rearrange("k e p -> k (e p)")[:, 0:D]
        g_bc, b_bc = sb("g_bc", [P, D]), sb("b_bc", [P, D])
        gain, shift = sb("gain", [P, E * C]), sb("shift", [P, E * C])
        b1 = sb("b1", [P, E])
        b1x = sb("b1x", [P, E])
        o_raw = sb("o_raw", [P, K, T])
        o = pair("o", [P, RING, T])
        x = sb("x", [P, NT, D])
        xh = sb("xh", [P, NT, D])
        stats, mv = sb("stats", [P, NT, 6]), sb("mv", [P, NT, 2])
        ve, rstd = sb("ve", [P, NT]), sb("rstd", [P, NT])
        xT = pair("xT", [P, C, T])
        L = sb("L", [P, NT, E])
        top = sb("top", [P, NT, E])
        idx = sb("idx", [P, NT, E], U32)
        idx_f = sb("idx_f", [P, NT])
        hot = sb("hot", [P, NT, E])
        hotT = sb("hotT", [E, T], F32R)
        g = [sb(f"g{n}", [P, T]) for n in range(2)]
        h = [pair(f"h{n}", [P, T]) for n in range(2)]

        acc = [st.ps(f"acc{n}", [P, 512]) for n in range(4)]
        bank = {n: st.ps(n, [P, 512]) for n in "ABCD"}

        setup, small, w1_in, b2_in = sem("setup"), sem("small"), sem("w1_in"), sem("b2_in")
        passed = sem("passed")
        consts, bias_ps, w1_ready, w1_hi = sem("consts"), sem("bias_ps"), sem("w1_ready"), sem("w1_hi")
        small_cut = sem("small_cut")
        o_in, x_in, stored = sem("o_in"), sem("x_in"), sem("stored")
        pe_s, act_s, dve_s, pool_s = (st.steps(n) for n in ("products", "act", "dve", "pool"))
        claims = Claims("ex_banks", orders)
        pe_s.alias(("Wk", K - 1), ("Wout", NT - 1))
        for t in range(NT):
            dve_s.alias(("read", "Wout", t), ("y", t))
            dve_s.alias(("read", "out", t), ("x4", t))
        dve_s.alias(("read", "hotT"), ("hotT",))

        rows = lambda w: w.rearrange("(c p) n -> p c n", p=P)
        w1_slots = [t[:, :, :].rearrange("p t d -> p (t d)") for t in (x, xh)]
        EH = E // 2
        w1_raw = [s.rearrange("p (k n) -> p k n", n=HE) for s in w1_slots]
        weights = []
        for n in range(2):
            s = slice(n * K // 2, (n + 1) * K // 2)
            weights.append((rows(a["L1_xattn_Wout"])[:, s, :], Wout[0][:, s, :], Wout[1][:, s, :]))
        for n in range(2):
            s = slice(n * EH, (n + 1) * EH)
            weights.append((a["L1_ffn_W2"].rearrange("e h d -> h e d")[:, s, :], W2[0][:, s, :], W2[1][:, s, :]))
        flat = o_raw[:, :, :].rearrange("p k t -> p (k t)")
        w_sync, w_scalar, w_vector, w_cut = load_and_split(st, weights, "w", [flat[:, 0:2048], flat[:, 2048:4096]])

        smalls = [(gain[:, :], a["L1_ffn_ln_scale"]), (shift[:, :], a["L1_ffn_ln_bias"]), (b1[:, :], a["L1_ffn_b1"]),
                  (Wg_raw[:, :, :], rows(a["Wg_T"])),
                  (g_bc[:, :], a["L1_xattn_ln_o_g"].partition_broadcast(P)),
                  (b_bc[:, :], a["L1_xattn_ln_o_b"].partition_broadcast(P))]
        one = lambda ap, i: ap[bass.ds(i, 1)].rearrange("b (t p) d -> p (b t) d", p=P)
        block = ctx.enter_context(nc.Block())

        @block.sync
        def _(sp):
            for dst, src in smalls:
                sp.dma_start(dst, src).then_inc(small, 16)
            for n in range(2):
                src = a["L1_ffn_W1"][n * EH:(n + 1) * EH].rearrange("e (c p) h -> p (e c) h", p=P)
                sp.dma_start(w1_raw[n], src).then_inc(w1_in, 16)
            sp.wait_ge(consts, 1)
            sp.dma_start(b2_raw, a["L1_ffn_b2"]).then_inc(b2_in, 16)
            w_sync(sp)
            w_cut(sp)
            sp.wait_ge(small_cut, 3)
            with sp.Fori(0, B) as i:
                sp.wait_ge(*dve_s.before(i, "olo", K - 1))
                sp.dma_start(o_raw[:, :, :], o_s[bass.ds(i, 1)].rearrange("b k p t -> p (b k) t")).then_inc(o_in, 16)
                sp.wait_ge(*dve_s.before(i, "x4", NT - 1))
                sp.dma_start(x[:, :, :], one(x2_s, i)).then_inc(x_in, 16)

        @block.gpsimd
        def _(pool):
            pool.sem_inc(pool_s.sem, pool_s.per)
            make_identity(pool, ident, setup)
            pool.memset(minus_half[:, :], -0.5).then_inc(setup, 1)
            pool.iota(eight[:, :], pattern=[[1, E]], base=0, channel_multiplier=0,
                      allow_small_or_imprecise_dtypes=True).then_inc(setup, 1)
            pool.memset(sel_f[:, :, :], 0.0).then_inc(setup, 1)
            pool.wait_ge(setup, 5)
            pool.affine_select(out=sel_f[:, :, :], in_=sel_f[:, :, :], compare_op=ALU.not_equal, fill=1.0,
                               base=0, pattern=[[-1, E], [0, P]], channel_multiplier=1).then_inc(setup, 1)
            with pool.Fori(0, B) as i:
                for ln, scale, eps in (("ln_o", 1.0, EPS), ("ln", 1.0 + EPS, EPS * EPS)):
                    wait_apart(pool, dve_s.at(i, ln, "var"), passed)
                    pool.tensor_scalar(ve[:, :], mv[:, :, 1], scale, eps, ALU.mult, ALU.add).then_inc(*pool_s.mark(ln, "ve"))
                    pool.wait_ge(*pool_s.at(i, ln, "ve"))
                    pool.tensor_tensor(rstd[:, :], ve[:, :], minus_half[:, :], ALU.pow).then_inc(*pool_s.mark(ln, "rstd"))

        @block.tensor
        def _(pe):
            pe.sem_inc(pe_s.sem, pe_s.per)
            pe.wait_ge(small, 16 * len(smalls))
            pe.wait_ge(w1_in, 32)
            for e in range(E):
                for c in range(C):
                    m = pe.matmul(bank["A"][:, e:e + 1], w1_raw[e // EH][:, (e % EH) * C + c, :],
                                  shift[:, e * C + c:e * C + c + 1], start=(c == 0), stop=(c == C - 1))
            m.then_inc(bias_ps, 1)
            pe.wait_ge(setup, 6)
            pe.wait_ge(consts, 1)
            pe.wait_ge(small_cut, 3)
            w_cut(pe)
            with pe.Fori(0, B) as i:
                def claim(ps, b, *u):
                    last, earlier = claims.before(b, u)
                    for s in (act_s, dve_s):
                        if s.has("read", *last):
                            pe.wait_ge(*(s.before if earlier else s.at)(i, "read", *last))
                    return ps

                on = lambda b, *u: claim(bank[b], b, *u)

                for k in range(K):
                    pe.wait_ge(*dve_s.at(i, "olo", k))
                    for t in range(NT):
                        if k == 0:
                            claim(acc[t], t, "Wout", t)
                        m = product(pe, acc[t][:, :], [z[:, k % RING, t * P:(t + 1) * P] for z in o],
                                    [w[:, k, :] for w in Wout], k == 0, k == K - 1)
                        if k == K - 1:
                            m.then_inc(*pe_s.mark("Wout", t))
                    if k < K - 1:
                        m.then_inc(*pe_s.mark("Wk", k))
                for c in range(C):
                    ps = on("ABCD"[c], "xT", c)
                    for t in range(NT):
                        if c == 0:
                            pe.wait_ge(*dve_s.at(i, "xh", t))
                        m = pe.transpose(ps[:, t * P:(t + 1) * P], xh[:, t, c * P:(c + 1) * P], ident[:, :])
                    m.then_inc(*pe_s.mark("xT", c))

                ps = on("C", "L")
                pe.wait_ge(*dve_s.at(i, "read", "xT", C - 1))
                for t in range(NT):
                    for c in range(C):
                        m = product(pe, ps[:, t * E:(t + 1) * E], [z[:, c, t * P:(t + 1) * P] for z in xT],
                                    [w[:, c, :] for w in Wg], c == 0, c == C - 1)
                m.then_inc(*pe_s.mark("L"))

                def hidden(e):
                    ps = on("AB"[e % 2], "h", e)
                    for c in range(C):
                        m = product(pe, ps[:, :], [w[:, e * C + c, :] for w in W1], [z[:, c, :] for z in xT], c == 0, c == C - 1)
                    m.then_inc(*pe_s.mark("h", e))

                def mask(e):
                    ps = on("CD"[e % 2], "M", e)
                    pe.matmul(ps[:, :], sel[:, e, :], hotT[:, :], start=True, stop=True).then_inc(*pe_s.mark("M", e))

                for e in range(2):
                    hidden(e)
                ps = on("D", "hotT")
                pe.wait_ge(*dve_s.at(i, "hot"))
                for t in range(NT):
                    m = pe.transpose(ps[0:E, t * P:(t + 1) * P], hot[:, t, :], ident[:, :])
                m.then_inc(*pe_s.mark("hotT"))
                pe.wait_ge(*dve_s.at(i, "hotT"))
                for e in range(2):
                    mask(e)
                for t in range(NT):
                    claim(acc[t], t, "out", t)
                    for n in range(2):
                        pe.matmul(acc[t][:, :], hotT[:, t * P:(t + 1) * P], b2[n][:, :], start=(n == 0), stop=False)
                for e in range(E):
                    pe.wait_ge(*dve_s.at(i, "lo", e))
                    for t in range(NT):
                        m = product(pe, acc[t][:, :], [z[:, t * P:(t + 1) * P] for z in h[e % 2]],
                                    [w[:, e, :] for w in W2], False, e == E - 1)
                        if e == E - 1:
                            m.then_inc(*pe_s.mark("out", t))
                    if e < E - 1:
                        m.then_inc(*pe_s.mark("used", e))
                    if e + 2 < E:
                        hidden(e + 2)
                        mask(e + 2)

        @block.scalar
        def _(act):
            act.sem_inc(act_s.sem, act_s.per)
            act.sem_inc(stored, 16)
            for n in range(2):
                act.wait_ge(w1_ready, n + 1)
                s = slice(n * EH * C, (n + 1) * EH * C)
                act.activation(W1[0][:, s, :], w1_raw[n], ACT.Copy).then_inc(w1_hi, 1)
            w_scalar(act)
            with act.Fori(0, B) as i:
                act.wait_ge(o_in, i * 16 + 16)
                for k in range(K):
                    if k < RING:
                        act.wait_ge(*pe_s.before(i, "Wk", k + RING))
                    else:
                        act.wait_ge(*pe_s.at(i, "Wk", k - RING))
                    act.activation(o[0][:, k % RING, :], o_raw[:, k, :], ACT.Copy).then_inc(*act_s.mark("ohi", k))
                for c in range(C):
                    act.wait_ge(*pe_s.at(i, "xT", c))
                    act.activation(xT[0][:, c, :], bank["ABCD"[c]][:, :], ACT.Copy).then_inc(*act_s.mark("hi", "xT", c))

                def gelu(e):
                    act.wait_ge(*pe_s.at(i, "h", e))
                    if e < 2:
                        act.wait_ge(*dve_s.before(i, "lo", e + E - 2))
                    else:
                        act.wait_ge(*dve_s.at(i, "lo", e - 2))
                    act.activation(g[e % 2][:, :], bank["AB"[e % 2]][:, :], ACT.Gelu, bias=b1x[:, e:e + 1])\
                       .then_inc(*act_s.mark("read", "h", e))

                gelu(0)
                for e in range(E):
                    if e + 1 < E:
                        gelu(e + 1)
                    act.wait_ge(*dve_s.at(i, "read", "M", e))
                    if e >= 2:
                        act.wait_ge(*pe_s.at(i, "used", e - 2))
                    else:
                        act.wait_ge(*pe_s.before(i, "out", NT - 1))
                    act.activation(h[e % 2][0][:, :], g[e % 2][:, :], ACT.Copy).then_inc(*act_s.mark("hhi", e))
                act.wait_ge(*dve_s.at(i, "x4", NT - 1))
                act.dma_start(one(out, i), xh[:, :, :]).then_inc(stored, 16)
            act.wait_ge(stored, 16 * (B + 1))

        @block.vector
        def _(dve):
            dve.sem_inc(dve_s.sem, dve_s.per)
            dve.wait_ge(setup, 6)
            dve.tensor_copy(sel[:, :, :], sel_f[:, :, :]).then_inc(consts, 1)
            dve.wait_ge(bias_ps, 1)
            dve.tensor_tensor(b1x[:, :], bank["A"][:, 0:E], b1[:, :], ALU.add).then_inc(small_cut, 1)
            for n in range(2):
                s = slice(n * EH * C, (n + 1) * EH * C)
                dve.tensor_tensor(w1_raw[n], w1_raw[n], gain[:, s].unsqueeze(2).to_broadcast([P, EH * C, HE]), ALU.mult)\
                   .then_inc(w1_ready, 1)
            for n in range(2):
                s = slice(n * EH * C, (n + 1) * EH * C)
                dve.wait_ge(w1_hi, n + 1)
                dve.tensor_tensor(W1[1][:, s, :], w1_raw[n], f32(W1[0][:, s, :]), ALU.subtract).then_inc(w1_ready, 1)
            for raw, cut, loaded in ((Wg_raw[:, :, :], [w[:, :, :] for w in Wg], None),
                                     (b2_raw, [w[:, :] for w in b2], b2_in)):
                if loaded is not None:
                    dve.wait_ge(loaded, 16)
                dve.tensor_copy(cut[0], raw).then_inc(consts, 1)
                dve.wait_ge(consts, 2 if loaded is None else 3)
                dve.tensor_tensor(cut[1], raw, f32(cut[0]), ALU.subtract).then_inc(small_cut, 1)
            dve.wait_ge(w1_ready, 4)
            w_vector(dve)
            with dve.Fori(0, B) as i:
                def moments(ln, t, src):
                    dve.bn_stats(stats[:, t, :], src).then_inc(*dve_s.mark(ln, "stats", t))

                def aggregate(ln):
                    wait_apart(dve, dve_s.at(i, ln, "stats", NT - 1), passed)
                    for t in range(NT):
                        m = dve.bn_aggr(mv[:, t, :], stats[:, t, :])
                    m.then_inc(*dve_s.mark(ln, "var"))
                    dve.wait_ge(*dve_s.at(i, ln, "var"))
                    dve.wait_ge(*pool_s.at(i, ln, "rstd"))

                for k in range(K):
                    dve.wait_ge(*act_s.at(i, "ohi", k))
                    dve.tensor_tensor(o[1][:, k % RING, :], o_raw[:, k, :], f32(o[0][:, k % RING, :]), ALU.subtract)\
                       .then_inc(*dve_s.mark("olo", k))
                dve.wait_ge(x_in, i * 16 + 16)
                dve.tensor_tensor(x[:, :, :], x[:, :, :], b_bc[:, :].unsqueeze(1).to_broadcast([P, NT, D]), ALU.add)\
                   .then_inc(*dve_s.mark("x+b"))
                for t in range(NT):
                    dve.wait_ge(*pe_s.at(i, "Wout", t))
                    moments("ln_o", t, acc[t][:, :])
                aggregate("ln_o")
                dve.wait_ge(stored, i * 16 + 16)
                for t in range(NT):
                    dve.scalar_tensor_tensor(xh[:, t, :], acc[t][:, :], mv[:, t, 0:1], g_bc[:, :], ALU.subtract, ALU.mult)\
                       .then_inc(*dve_s.mark("y", t))
                for t in range(NT):
                    dve.wait_ge(*dve_s.at(i, "y", t))
                    dve.scalar_tensor_tensor(x[:, t, :], xh[:, t, :], rstd[:, t:t + 1], x[:, t, :], ALU.mult, ALU.add)\
                       .then_inc(*dve_s.mark("x3", t))
                for t in range(NT):
                    dve.wait_ge(*dve_s.at(i, "x3", t))
                    moments("ln", t, x[:, t, :])
                aggregate("ln")
                for t in range(NT):
                    dve.tensor_scalar(xh[:, t, :], x[:, t, :], mv[:, t, 0:1], rstd[:, t:t + 1], ALU.subtract, ALU.mult)\
                       .then_inc(*dve_s.mark("xh", t))
                for c in range(C):
                    dve.wait_ge(*act_s.at(i, "hi", "xT", c))
                    dve.tensor_tensor(xT[1][:, c, :], bank["ABCD"[c]][:, :], f32(xT[0][:, c, :]), ALU.subtract)\
                       .then_inc(*dve_s.mark("read", "xT", c))
                dve.wait_ge(*pe_s.at(i, "L"))
                dve.tensor_copy(L[:, :, :], bank["C"][:, 0:NT * E].rearrange("p (t e) -> p t e", e=E)).then_inc(*dve_s.mark("read", "L"))
                wait_apart(dve, dve_s.at(i, "read", "L"), passed)
                for t in range(NT):
                    dve.max(top[:, t, :], L[:, t, :]).then_inc(*dve_s.mark("top", t))
                wait_apart(dve, dve_s.at(i, "top", NT - 1), passed)
                for t in range(NT):
                    dve.max_index(idx[:, t, :], top[:, t, :], L[:, t, :]).then_inc(*dve_s.mark("idx", t))
                dve.wait_ge(*dve_s.at(i, "idx", NT - 1))
                dve.tensor_copy(idx_f[:, :], idx[:, :, 0]).then_inc(*dve_s.mark("idx_f"))
                dve.wait_ge(*dve_s.at(i, "idx_f"))
                dve.tensor_tensor(hot[:, :, :], idx_f[:, :].unsqueeze(2).to_broadcast([P, NT, E]),
                                  eight[:, :].unsqueeze(1).to_broadcast([P, NT, E]), ALU.is_equal).then_inc(*dve_s.mark("hot"))
                dve.wait_ge(*pe_s.at(i, "hotT"))
                dve.tensor_copy(hotT[:, :], bank["D"][0:E, :]).then_inc(*dve_s.mark("hotT"))

                def masked(e):
                    dve.wait_ge(*pe_s.at(i, "M", e))
                    dve.wait_ge(*act_s.at(i, "read", "h", e))
                    dve.tensor_tensor(g[e % 2][:, :], g[e % 2][:, :], bank["CD"[e % 2]][:, :], ALU.mult)\
                       .then_inc(*dve_s.mark("read", "M", e))

                masked(0)
                for e in range(E):
                    if e + 1 < E:
                        masked(e + 1)
                    dve.wait_ge(*act_s.at(i, "hhi", e))
                    dve.tensor_tensor(h[e % 2][1][:, :], g[e % 2][:, :], f32(h[e % 2][0][:, :]), ALU.subtract)\
                       .then_inc(*dve_s.mark("lo", e))
                for t in range(NT):
                    dve.wait_ge(*pe_s.at(i, "out", t))
                    dve.tensor_tensor(xh[:, t, :], acc[t][:, :], x[:, t, :], ALU.add).then_inc(*dve_s.mark("x4", t))



INPUTS = ["x", "ctx_1024", "mask_BxS2_ik0", "mask_BxS2_bk0",
          "L0_xattn_Wq", "L0_xattn_bq", "L0_xattn_Wk", "L0_xattn_bk", "L0_xattn_Wv", "L0_xattn_bv",
          "L0_xattn_Wo", "L0_xattn_bo",
          "L0_ffn_slot_init", "L0_ffn_w1", "L0_ffn_b1", "L0_ffn_w2", "L0_ffn_b2", "L0_ffn_tau",
          "L0_ffn_bih", "L0_ffn_bhh", "L0_ffn_wq", "L0_ffn_bq", "L0_ffn_wk", "L0_ffn_bk",
          "L0_ffn_wv", "L0_ffn_bv", "L0_ffn_ln_g", "L0_ffn_ln_b", "L0_ffn_wvp", "L0_ffn_bvp", "L0_ffn_wo", "L0_ffn_bo",
          "L1_xattn_ln_x_g", "L1_xattn_ln_x_b", "L1_xattn_ln_l_g", "L1_xattn_ln_l_b",
          "L1_xattn_Wq", "L1_xattn_Wkv", "L1_xattn_Wout", "L1_xattn_ln_o_g", "L1_xattn_ln_o_b",
          "L1_ffn_ln_scale", "L1_ffn_ln_bias", "L1_ffn_W1", "L1_ffn_b1", "L1_ffn_W2", "L1_ffn_b2",
          "Wih_T", "Whh_T", "slot_init_T", "Wg_T"]
TRANSPOSED = {"Wih_T": "L0_ffn_Wih", "Whh_T": "L0_ffn_Whh", "slot_init_T": "L0_ffn_slot_init", "Wg_T": "L1_ffn_Wg"}


def two_layers(nc, orders, a, out):
    B, T, D = a["x"].shape
    SK = a["ctx_1024"].shape[1]
    NS = a["L0_ffn_slot_init"].shape[0]
    INNER = a["L1_xattn_Wq"].shape[1]
    Z = T + SK + SK % 2

    def scratch(name, *shape):
        return nc.dram_tensor(name, shape, F32, kind="Internal").ap()

    x1_s, x2_s = scratch("x1_s", B, T, D), scratch("x2_s", B, T, D)
    alphaT_s = scratch("alphaT_s", B, NS, T)
    si_s, vo_s = scratch("si_s", B, NS, D), scratch("vo_s", B, NS, D)
    z_s = [scratch(f"z{n}_s", B, P, D // P, Z) for n in range(2)]
    o_s = scratch("o_s", B, INNER // P, P, T)

    build_layer0(nc, orders, a, x1_s, alphaT_s, si_s)
    build_slots(nc, orders, a, si_s, vo_s)
    build_latents(nc, orders, a, x1_s, alphaT_s, vo_s, x2_s, z_s)
    build_perceiver(nc, orders, a, z_s, o_s)
    build_experts(nc, orders, a, o_s, x2_s, out)


def kernel(**inputs):
    import concourse.bacc as bacc
    from concourse.bass_utils import run_bass_kernel_spmd

    arrays = {}
    for name in INPUTS:
        v = np.asarray(inputs[TRANSPOSED.get(name, name)])
        if name in TRANSPOSED:
            v = v.T
        elif name in COLUMNS:
            v = v.reshape(-1, P).T
        v = np.ascontiguousarray(v)
        if v.dtype == np.bool_:
            v = v.reshape(1, -1).view(np.int32)
        arrays[name] = v

    def program(orders):
        nc = bacc.Bacc("TRN2", target_bir_lowering=False, num_devices=1)
        a = {n: nc.dram_tensor(n, v.shape, mybir.dt.from_np(v.dtype), kind="ExternalInput").ap()
             for n, v in arrays.items()}
        out = nc.dram_tensor("out", arrays["x"].shape, F32, kind="ExternalOutput").ap()
        two_layers(nc, orders, a, out)
        return nc

    orders = {}
    program(orders)
    r = run_bass_kernel_spmd(program(orders), [arrays], core_ids=[0])
    return r.results[0]["out"]
```

```python
from contextlib import ExitStack

import numpy as np
import concourse.bass as bass
from concourse import mybir

F32 = mybir.dt.float32
F32R = mybir.dt.float32r
I32 = mybir.dt.int32
U32 = mybir.dt.uint32
ALU = mybir.AluOpType
ACT = mybir.ActivationFunctionType
AX = mybir.AxisListType.X

P = 128
EPS = 1e-5

COLUMNS = ["L0_xattn_bq", "L0_xattn_bk", "L0_xattn_bv", "L0_ffn_b1", "L0_ffn_bih", "L0_ffn_bhh", "L0_ffn_bq",
           "L0_ffn_bk", "L0_ffn_bvp", "L1_xattn_ln_x_g", "L1_xattn_ln_x_b", "L1_xattn_ln_l_g", "L1_xattn_ln_l_b",
           "L1_ffn_ln_scale", "L1_ffn_ln_bias", "L1_ffn_b1"]


class Signal:

    def __init__(self, sem, orders):
        self.sem, self.known, self.order, self.same = sem, orders.get(sem.name), [], {}
        self.lead, self.reached = False, 0
        orders[sem.name] = self.order

    @property
    def per(self):
        return len(self.known) if self.known else 1

    def mark(self, *name):
        if name not in self.order and not self.lead:
            self.order.append(name)
        return self.sem, 1

    def start(self, engine):
        engine.sem_inc(self.sem, self.per)

    def lead_up(self, engine, *name):
        until = self.ordinal(name) - 1 if name else self.per
        if self.reached:
            engine.wait_ge(self.sem, self.reached)
        if until > self.reached:
            engine.sem_inc(self.sem, until - self.reached)
        self.reached = until + 1

    def alias(self, name, step):
        self.same[name] = step

    def has(self, *name):
        return not self.known or self.same.get(name, name) in self.known

    def ordinal(self, name):
        return self.known.index(self.same.get(name, name)) + 1 if self.known else 1

    def at(self, i, *name):
        return self.sem, i * self.per + (self.per + self.ordinal(name))

    def before(self, i, *name):
        return self.sem, i * self.per + self.ordinal(name)


class Stage:

    def __init__(self, nc, ctx, name, orders):
        self.nc, self.ctx, self.name, self.orders = nc, ctx, name, orders

    def sb(self, name, shape, dt=F32):
        return self.ctx.enter_context(self.nc.sbuf_tensor(f"{self.name}_{name}", shape, dt))

    def ps(self, name, shape):
        return self.ctx.enter_context(self.nc.psum_tensor(f"{self.name}_{name}", shape, F32))

    def sem(self, name):
        return self.ctx.enter_context(self.nc.semaphore(f"{self.name}_{name}"))

    def steps(self, name):
        return Signal(self.sem(name), self.orders)


def wait_apart(engine, step, passed):
    engine.wait_ge(*step)
    engine.sem_inc(passed, 1)


def f32(ap):
    return ap.bitcast(F32)


def product(pe, out, a, b, first, last):
    pe.matmul(out, a[0], b[0], start=first, stop=False)
    pe.matmul(out, a[0], b[1], start=False, stop=False)
    return pe.matmul(out, a[1], b[0], start=False, stop=last)


def make_identity(pool, ident, done):
    pool.memset(ident[:, :], 0.0).then_inc(done, 1)
    pool.wait_ge(done, 1)
    pool.affine_select(out=ident[:, :], in_=ident[:, :], compare_op=ALU.not_equal, fill=1.0,
                       base=0, pattern=[[-1, P]], channel_multiplier=1).then_inc(done, 1)



def load_and_split(st, weights, tag, slots):
    loaded = [st.sem(f"{tag}_w{j}_loaded") for j in range(2)]
    hi_cut, lo_cut = st.sem(f"{tag}_hi_cut"), st.sem(f"{tag}_lo_cut")

    def slot(n):
        _, k, m = weights[n][0].shape
        return slots[n % 2][:, 0:k * m].rearrange("p (k m) -> p k m", k=k)

    def on_sync(sp):
        for n, (src, _, _) in enumerate(weights):
            if n >= 2:
                sp.wait_ge(lo_cut, n - 1)
            sp.dma_start(slot(n), src).then_inc(loaded[n % 2], 16)

    def on_scalar(act):
        for n, (_, hi, _) in enumerate(weights):
            act.wait_ge(loaded[n % 2], 16 * (n // 2 + 1))
            act.activation(hi, slot(n), ACT.Copy).then_inc(hi_cut, 1)

    def on_vector(dve):
        for n, (_, hi, lo) in enumerate(weights):
            dve.wait_ge(hi_cut, n + 1)
            dve.tensor_tensor(lo, slot(n), f32(hi), ALU.subtract).then_inc(lo_cut, 1)

    def cut(engine, n=len(weights)):
        engine.wait_ge(lo_cut, n)

    return on_sync, on_scalar, on_vector, cut


class Banks:

    def __init__(self, tiles, units):
        self.tiles, self.units = tiles, units

    def __getitem__(self, unit):
        return self.tiles[self.units.index(unit) % len(self.tiles)]

    def user_before(self, unit):
        n, r = self.units.index(unit), len(self.tiles)
        if n >= r:
            return self.units[n - r], False
        return self.units[max(m for m in range(len(self.units)) if m % r == n % r)], True


def take(engine, banks, read, i, unit):
    last, earlier = banks.user_before(unit)
    for signal in read:
        if signal.has("read", *last):
            engine.wait_ge(*(signal.before if earlier else signal.at)(i, "read", *last))



def build_layer0(nc, orders, a, x1_s, alphaT_s, si_s):
    B, T, D = a["x"].shape
    SK = a["ctx_1024"].shape[1]
    SKP = SK + SK % 2
    C, NT = D // P, T // P
    H, HD = 16, 32
    HC = P // HD
    DH = a["L0_ffn_w1"].shape[1]
    J = DH // P
    NS = a["L0_ffn_slot_init"].shape[0]
    KTOP = 8
    SCALE = 1.0 / float(np.sqrt(HD))
    MASKED = 1e9 / SCALE

    with ExitStack() as ctx:
        st = Stage(nc, ctx, "l0", orders)
        sb, sem = st.sb, st.sem
        pair = lambda name, shape: (sb(name + "_hi", shape, F32R), sb(name + "_lo", shape, F32R))

        ident = sb("ident", [P, P])
        minus_half = sb("minus_half", [P, NT])
        ones = sb("ones", [P, P])
        ones_r = sb("ones_r", [1, P], F32R)
        Wq, Wk, Wv, Wo = (pair(n, [P, C, D]) for n in ("Wq", "Wk", "Wv", "Wo"))
        W1 = pair("W1", [P, C, DH])
        W2 = pair("W2", [P, J, NS])
        smean = sb("smean", [P, C])
        b1c = sb("b1c", [P, J])
        hbias = sb("hbias", [P, J])
        bq, bk, bv = (sb(n, [P, C]) for n in ("bq", "bk", "bv"))
        bo_bc = sb("bo_bc", [P, D])
        b2_bc = sb("b2_bc", [P, NS])
        tau = sb("tau", [P, 4])

        x = sb("x", [P, NT, D])
        x1 = sb("x1", [P, NT, D])
        cx = sb("cx", [SK, D])
        mask_i = sb("mask_i", [P, SK], I32)
        valid = sb("valid", [P, SKP])
        mrow = sb("mrow", [1, HC, SKP], F32R)
        stats = sb("stats", [P, NT, 6])
        mv = sb("mv", [P, NT, 2])
        ve = sb("ve", [P, NT])
        rstd = sb("rstd", [P, NT])
        xn = sb("xn", [P, NT, D])
        xT = pair("xT", [P, C, T])
        cT = pair("cT", [P, C, SKP])
        Kv = sb("Kv", [P, C, SKP])
        Kd = pair("Kd", [P, C, HC * SKP])
        Vd = pair("Vd", [SK, C, HC * (P + HD)])
        qT = pair("qT", [P, C, T])
        mx = sb("mx", [P, NT, H])
        E = sb("E", [P, NT, H, SK])
        rs = sb("rs", [P, NT, H])
        PT = [pair(f"PT{n}", [SK, T]) for n in range(2)]
        oT = qT
        flat = E[:, :, :, :].rearrange("p t h s -> p (t h s)")
        w1s = flat[:, 0:C * DH].rearrange("p (c n) -> p c n", c=C)
        slots0 = flat[0:NS, C * DH:C * DH + D]
        hT = flat[:, 0:J * T].rearrange("p (j t) -> p j t", j=J)
        hTs = tuple(z[:, 0:J, :] for z in oT)
        L = sb("L", [P, NT, NS])
        top = sb("top", [P, NT, KTOP])
        rest = sb("rest", [P, NT, NS])
        el = sb("el", [P, NT, NS])
        asum = sb("asum", [P, NT])
        alpha = sb("alpha", [P, NT, NS])
        aT = sb("aT", [NS, T])
        den = sb("den", [NS, 1])
        si = sb("si", [NS, D])

        flat_slots = [z[:, :, :].rearrange("p t d -> p (t d)") for z in (x1, xn)]

        bank = [st.ps(f"bank{n}", [P, 512]) for n in range(8)]

        setup = sem("setup")
        passed = sem("passed")
        small = sem("small")
        x_in, cx_in, mask_in = sem("x_in"), sem("cx_in"), sem("mask_in")
        x1_out, aT_out, si_out = sem("x1_out"), sem("aT_out"), sem("si_out")
        consts = sem("consts")
        mean_ps, mean_sb, hb_ps = sem("mean_ps"), sem("mean_sb"), sem("hb_ps")
        hb_ready, tau_ready = sem("hb_ready"), sem("tau_ready")
        pe_s, act_s, dve_s, pool_s = (st.steps(n) for n in ("products", "act", "dve", "rstd"))

        dve_s.alias(("read", "K"), ("Kv",))
        dve_s.alias(("read", "aT"), ("aT",))
        dve_s.alias(("read", "si"), ("si",))
        for t in range(NT):
            for c in range(C):
                dve_s.alias(("read", "S", t, c), ("shifted", t, c))

        rows = lambda w: w.rearrange("(c p) n -> p c n", p=P)
        weights = []
        for name, tile in (("Wk", Wk), ("Wv", Wv), ("Wq", Wq), ("Wo", Wo)):
            weights.append((rows(a["L0_xattn_" + name]), tile[0][:, :, :], tile[1][:, :, :]))
        weights.append((rows(a["L0_ffn_w1"][0:D, :]), W1[0][:, :, :], W1[1][:, :, :]))
        weights.append((rows(a["L0_ffn_w2"]), W2[0][:, :, :], W2[1][:, :, :]))
        w_sync, w_scalar, w_vector, w_cut = load_and_split(st, weights, "w", flat_slots)

        smalls = [(slots0, a["L0_ffn_slot_init"]), (w1s, rows(a["L0_ffn_w1"][D:2 * D, :])),
                  (b1c[:, :], a["L0_ffn_b1"]),
                  (bq[:, :], a["L0_xattn_bq"]), (bk[:, :], a["L0_xattn_bk"]),
                  (bv[:, :], a["L0_xattn_bv"]),
                  (bo_bc[:, :], a["L0_xattn_bo"].partition_broadcast(P)),
                  (b2_bc[:, :], a["L0_ffn_b2"].partition_broadcast(P)),
                  (tau[:, 0:1], a["L0_ffn_tau"].partition_broadcast(P))]

        units = [("xT", c) for c in range(C)] + [("cT",), ("K",), ("V",)]
        units += [("Q", c) for c in range(C)]
        units += [("S", t, c) for t in range(NT) for c in range(C)]
        for c in range(C):
            units += [("PT", c * HC + n) for n in range(HC)] + [("O", c)]
        units += [("Wo", t) for t in range(NT)] + [("fT", c) for c in range(C)]
        units += [("h", j) for j in range(J)] + [("L",), ("aT",), ("si",), ("den",)]
        banks = Banks(bank, units)

        block = ctx.enter_context(nc.Block())

        @block.sync
        def _(sp):
            for out in (x1_out, aT_out, si_out):
                sp.sem_inc(out, 16)
            for dst, src in smalls:
                sp.dma_start(dst, src).then_inc(small, 16)
            w_sync(sp)

            def load(i, last=None):
                one = lambda ap: ap[bass.ds(i, 1)]
                if last is not None:
                    sp.wait_ge(*dve_s.at(last, "res", NT - 1))
                sp.dma_start(x[:, :, :], one(a["x"]).rearrange("b (t p) d -> p (b t) d", p=P)).then_inc(x_in, 16)
                if last is not None:
                    sp.wait_ge(*pe_s.at(last, "cT"))
                sp.dma_start(cx[:, :], one(a["ctx_1024"]).rearrange("b s d -> (b s) d")).then_inc(cx_in, 16)
                if last is not None:
                    sp.wait_ge(*dve_s.at(last, "valid"))
                sp.dma_start(mask_i[:, :], one(a["mask_BxS2_ik0"]).rearrange("b s -> (b s)").partition_broadcast(P)).then_inc(mask_in, 16)

            def store(i):
                one = lambda ap: ap[bass.ds(i, 1)]
                sp.wait_ge(*dve_s.at(i, "aT"))
                sp.dma_start(one(alphaT_s).rearrange("b s t -> (b s) t"), aT[:, :]).then_inc(aT_out, 16)
                sp.wait_ge(*dve_s.at(i, "si"))
                sp.dma_start(one(si_s).rearrange("b s d -> (b s) d"), si[:, :]).then_inc(si_out, 16)

            def store_x1(i):
                sp.wait_ge(*dve_s.at(i, "res", NT - 1))
                sp.dma_start(x1_s[bass.ds(i, 1)].rearrange("b (t p) d -> p (b t) d", p=P), x1[:, :, :]).then_inc(x1_out, 16)

            load(0)
            with sp.Fori(0, B - 1) as i:
                store_x1(i)
                load(i + 1, i)
                store(i)
            store_x1(B - 1)
            store(B - 1)
            for out in (x1_out, aT_out, si_out):
                sp.wait_ge(out, 16 * (B + 1))

        @block.gpsimd
        def _(pool):
            pool.sem_inc(pool_s.sem, pool_s.per)
            make_identity(pool, ident, setup)
            pool.memset(minus_half[:, :], -0.5).then_inc(setup, 1)
            pool.memset(ones[:, :], 1.0).then_inc(setup, 1)
            pool.memset(valid[:, :], 0.0).then_inc(setup, 1)
            for n in range(2):
                pool.memset(cT[n][:, :, :].bitcast(F32), 0.0).then_inc(setup, 1)
                pool.memset(Kd[n][:, :, :].bitcast(F32), 0.0).then_inc(setup, 1)
                pool.memset(Vd[n][:, :, :].bitcast(F32), 0.0).then_inc(setup, 1)
            pool.wait_ge(setup, 11)
            with pool.Fori(0, B) as i:
                for ln in ("ln1", "ln2"):
                    wait_apart(pool, dve_s.at(i, ln, "var"), passed)
                    pool.tensor_scalar(ve[:, :], mv[:, :, 1], EPS, None, ALU.add).then_inc(*pool_s.mark(ln, "ve"))
                    pool.wait_ge(*pool_s.at(i, ln, "ve"))
                    pool.tensor_tensor(rstd[:, :], ve[:, :], minus_half[:, :], ALU.pow).then_inc(*pool_s.mark(ln, "rstd"))

        @block.tensor
        def _(pe):
            pe.sem_inc(pe_s.sem, pe_s.per)
            pe.wait_ge(small, 16 * len(smalls))
            pe.wait_ge(setup, 11)
            for c in range(C):
                m = pe.matmul(bank[0][:, c:c + 1], slots0[:, c * P:(c + 1) * P], ones[0:NS, 0:1], start=True, stop=True)
            m.then_inc(mean_ps, 1)
            pe.wait_ge(mean_sb, 1)
            for j in range(J):
                for c in range(C):
                    m = pe.matmul(bank[1][:, j:j + 1], w1s[:, c, j * P:(j + 1) * P], smean[:, c:c + 1],
                                  start=(c == 0), stop=(c == C - 1))
            m.then_inc(hb_ps, 1)
            w_cut(pe)
            pe.wait_ge(consts, 3)
            pe.wait_ge(hb_ready, 1)
            with pe.Fori(0, B) as i:
                def unit(*name):
                    take(pe, banks, (act_s, dve_s), i, name)
                    return banks[name]

                def project(out, w, m0, m1, x, n0, n1, chunks=C):
                    for k in range(chunks):
                        last = product(pe, out, (w[0][:, k, m0:m1], w[1][:, k, m0:m1]),
                                       (x[0][:, k, n0:n1], x[1][:, k, n0:n1]), k == 0, k == chunks - 1)
                    return last

                def transposes(name, ln):
                    for c in range(C):
                        ps = unit(name, c)
                        for t in range(NT):
                            if c == 0:
                                pe.wait_ge(*dve_s.at(i, ln, "xn", t))
                            m = pe.transpose(ps[:, t * P:(t + 1) * P], xn[:, t, c * P:(c + 1) * P], ident[:, :])
                        m.then_inc(*pe_s.mark(name, c))

                transposes("xT", "ln1")
                ps = unit("cT")
                pe.wait_ge(cx_in, i * 16 + 16)
                for c in range(C):
                    m = pe.transpose(ps[:, c * SK:(c + 1) * SK], cx[:, c * P:(c + 1) * P], ident[0:SK, 0:SK])
                m.then_inc(*pe_s.mark("cT"))
                ps = unit("K")
                pe.wait_ge(*dve_s.at(i, "read", "cT"))
                for c in range(C):
                    m = project(ps[:, c * SKP:(c + 1) * SKP], Wk, c * P, (c + 1) * P, cT, 0, SKP)
                m.then_inc(*pe_s.mark("K"))
                ps = unit("V")
                project(ps[0:SK, :], cT, 0, SK, Wv, 0, D).then_inc(*pe_s.mark("V"))
                for c in range(C):
                    ps = unit("Q", c)
                    pe.wait_ge(*dve_s.at(i, "read", "xT", C - 1))
                    project(ps[:, :], Wq, c * P, (c + 1) * P, xT, 0, T).then_inc(*pe_s.mark("Q", c))
                pe.wait_ge(*dve_s.at(i, "Kd"))
                for t in range(NT):
                    for c in range(C):
                        ps = unit("S", t, c)
                        if t == 0:
                            pe.wait_ge(*dve_s.at(i, "read", "Q", c))
                        q = [z[:, c, t * P:(t + 1) * P] for z in qT]
                        out = ps[:, 0:HC * SKP]
                        product(pe, out, q, [z[:, c, :] for z in Kd], True, False)
                        pe.matmul(out, ones_r[:, :], mrow[:, :, :].rearrange("p h s -> p (h s)"),
                                  start=False, stop=True).then_inc(*pe_s.mark("S", t, c))
                for c in range(C):
                    for n in range(HC):
                        h = c * HC + n
                        ps = unit("PT", h)
                        for t in range(NT):
                            if h == 0:
                                pe.wait_ge(*dve_s.at(i, "probs", t))
                            m = pe.transpose(ps[0:SK, t * P:(t + 1) * P], E[:, t, h, :], ident[:, :])
                        m.then_inc(*pe_s.mark("PT", h))
                    ps = unit("O", c)
                    for n in range(HC):
                        h = c * HC + n
                        pe.wait_ge(*dve_s.at(i, "read", "PT", h))
                        last = product(pe, ps[:, :], [z[:, c, n * P:(n + 1) * P] for z in Vd],
                                       [z[:, :] for z in PT[h % 2]], n == 0, n == HC - 1)
                        last.then_inc(*pe_s.mark("PV", h))
                for t in range(NT):
                    ps = unit("Wo", t)
                    pe.wait_ge(*dve_s.at(i, "read", "O", C - 1))
                    project(ps[:, :], oT, t * P, (t + 1) * P, Wo, 0, D).then_inc(*pe_s.mark("Wo", t))
                transposes("fT", "ln2")
                pe.wait_ge(*dve_s.at(i, "read", "fT", C - 1))
                for j in range(J):
                    ps = unit("h", j)
                    project(ps[:, :], W1, j * P, (j + 1) * P, xT, 0, T).then_inc(*pe_s.mark("h", j))
                ps = unit("L")
                pe.wait_ge(*dve_s.at(i, "hlo", J - 1))
                for t in range(NT):
                    m = project(ps[:, t * NS:(t + 1) * NS], hTs, t * P, (t + 1) * P, W2, 0, NS, J)
                m.then_inc(*pe_s.mark("L"))
                ps = unit("aT")
                wait_apart(pe, dve_s.at(i, "alpha"), passed)
                for t in range(NT):
                    m = pe.transpose(ps[0:NS, t * P:(t + 1) * P], alpha[:, t, :], ident[:, :])
                m.then_inc(*pe_s.mark("aT"))
                ps, ps2 = unit("si"), unit("den")
                for t in range(NT):
                    pe.matmul(ps[0:NS, :], alpha[:, t, :], xn[:, t, :], start=(t == 0), stop=(t == NT - 1))
                    m = pe.matmul(ps2[0:NS, 0:1], alpha[:, t, :], ones[:, 0:1], start=(t == 0), stop=(t == NT - 1))
                m.then_inc(*pe_s.mark("si"))

        @block.scalar
        def _(act):
            act.sem_inc(act_s.sem, act_s.per)
            w_scalar(act)
            act.wait_ge(tau_ready, 1)
            act.wait_ge(hb_ready, 1)
            with act.Fori(0, B) as i:
                def hi(signal_name, out, src, func=ACT.Copy, mark=None, **kw):
                    act.wait_ge(*pe_s.at(i, *signal_name))
                    return act.activation(out, src, func, **kw).then_inc(*act_s.mark("hi", *signal_name))

                for c in range(C):
                    if c == 0:
                        act.wait_ge(*pe_s.before(i, "h", J - 1))
                    hi(("xT", c), xT[0][:, c, :], banks["xT", c][:, :])
                act.wait_ge(*pe_s.before(i, "V"))
                hi(("cT",), cT[0][:, :, 0:SK], banks["cT",][:, 0:C * SK].rearrange("p (c s) -> p c s", c=C))
                act.wait_ge(*dve_s.at(i, "Kv"))
                act.wait_ge(*pe_s.before(i, "S", NT - 1, C - 1))
                for n in range(HC):
                    q = slice(n * HD, (n + 1) * HD)
                    act.activation(Kd[0][q, :, n * SKP:(n + 1) * SKP], Kv[q, :, :], ACT.Copy)\
                       .then_inc(*act_s.mark("Kd", n))
                act.wait_ge(*pe_s.before(i, "PV", H - 1))
                hi(("V",), vdiag(Vd[0], C, HC, P, HD, SK), banks["V",][0:SK, :].rearrange("p (c h d) -> p c h d", c=C, h=HC))
                for c in range(C):
                    hi(("Q", c), qT[0][:, c, :], banks["Q", c][:, :], ACT.Identity, bias=bq[:, c:c + 1])
                for t in range(NT):
                    act.wait_ge(*dve_s.at(i, "shifted", t, C - 1))
                    act.activation(E[:, t, :, :], E[:, t, :, :], ACT.Exp, scale=SCALE).then_inc(*act_s.mark("exp", t))
                for c in range(C):
                    for n in range(HC):
                        h = c * HC + n
                        if h >= 2:
                            act.wait_ge(*pe_s.at(i, "PV", h - 2))
                        hi(("PT", h), PT[h % 2][0][:, :], banks["PT", h][0:SK, :])
                    if c == 0:
                        act.wait_ge(*pe_s.before(i, "Wo", NT - 1))
                    act.wait_ge(*pe_s.at(i, "PV", c * HC + HC - 1))
                    act.activation(oT[0][:, c, :], banks["O", c][:, :], ACT.Identity, bias=bv[:, c:c + 1])\
                       .then_inc(*act_s.mark("hi", "O", c))
                for c in range(C):
                    if c == 0:
                        act.wait_ge(*pe_s.at(i, "Q", C - 1))
                    hi(("fT", c), xT[0][:, c, :], banks["fT", c][:, :])
                act.wait_ge(*dve_s.before(i, "hlo", J - 1))
                act.wait_ge(*pe_s.before(i, "L"))
                for j in range(J):
                    act.wait_ge(*pe_s.at(i, "h", j))
                    act.activation(hT[:, j, :], banks["h", j][:, :], ACT.Gelu, bias=hbias[:, j:j + 1])\
                       .then_inc(*act_s.mark("read", "h", j))
                for j in range(J):
                    act.wait_ge(*act_s.at(i, "read", "h", j))
                    act.activation(hTs[0][:, j, :], hT[:, j, :], ACT.Copy).then_inc(*act_s.mark("hhi", j))
                act.wait_ge(*dve_s.at(i, "lshift"))
                act.activation(el[:, :, :], el[:, :, :], ACT.Exp, scale=tau[:, 3:4]).then_inc(*act_s.mark("lexp"))

        @block.vector
        def _(dve):
            dve.sem_inc(dve_s.sem, dve_s.per)
            dve.wait_ge(small, 16 * len(smalls))
            dve.wait_ge(setup, 11)
            dve.tensor_copy(ones_r[:, :], ones[0:1, :]).then_inc(consts, 1)
            dve.tensor_scalar(tau[:, 1:2], tau[:, 0:1], -1.0, None, ALU.mult).then_inc(consts, 1)
            dve.wait_ge(consts, 2)
            dve.tensor_scalar(tau[:, 2:3], tau[:, 1:2], tau[:, 0:1], 0.1, ALU.max, ALU.add).then_inc(consts, 1)
            dve.wait_ge(consts, 3)
            dve.reciprocal(tau[:, 3:4], tau[:, 2:3]).then_inc(tau_ready, 1)
            dve.wait_ge(mean_ps, 1)
            dve.tensor_scalar(smean[:, :], bank[0][:, 0:C], 1.0 / NS, None, ALU.mult).then_inc(mean_sb, 1)
            dve.wait_ge(hb_ps, 1)
            dve.tensor_tensor(hbias[:, :], bank[1][:, 0:J], b1c[:, :], ALU.add).then_inc(hb_ready, 1)
            w_vector(dve)

            with dve.Fori(0, B) as i:
                def layer_norm(src, ln):
                    for t in range(NT):
                        if ln == "ln2":
                            dve.wait_ge(*dve_s.at(i, "res", t))
                        dve.bn_stats(stats[:, t, :], src[:, t, :]).then_inc(*dve_s.mark(ln, "stats", t))
                    wait_apart(dve, dve_s.at(i, ln, "stats", NT - 1), passed)
                    for t in range(NT):
                        m = dve.bn_aggr(mv[:, t, :], stats[:, t, :])
                    m.then_inc(*dve_s.mark(ln, "var"))
                    dve.wait_ge(*dve_s.at(i, ln, "var"))
                    dve.wait_ge(*pool_s.at(i, ln, "rstd"))
                    for t in range(NT):
                        dve.tensor_scalar(xn[:, t, :], src[:, t, :], mv[:, t, 0:1], rstd[:, t:t + 1],
                                          ALU.subtract, ALU.mult).then_inc(*dve_s.mark(ln, "xn", t))

                def lo(name, out, ps, hi_ap, bias=None):
                    dve.wait_ge(*act_s.at(i, "hi", *name))
                    if bias is None:
                        m = dve.tensor_tensor(out, ps, f32(hi_ap), ALU.subtract)
                    else:
                        m = dve.scalar_tensor_tensor(out, ps, bias, f32(hi_ap), ALU.add, ALU.subtract)
                    return m.then_inc(*dve_s.mark("read", *name))

                dve.wait_ge(x_in, i * 16 + 16)
                dve.wait_ge(*pe_s.before(i, "si"))
                layer_norm(x, "ln1")
                for c in range(C):
                    lo(("xT", c), xT[1][:, c, :], banks["xT", c][:, :], xT[0][:, c, :])
                dve.wait_ge(*act_s.at(i, "hi", "cT"))
                lo(("cT",), cT[1][:, :, 0:SK], banks["cT",][:, 0:C * SK].rearrange("p (c s) -> p c s", c=C), cT[0][:, :, 0:SK])
                dve.wait_ge(mask_in, i * 16 + 16)
                dve.tensor_scalar(valid[:, 0:SK], mask_i[:, :], 0.0, None, ALU.not_equal).then_inc(*dve_s.mark("valid"))
                dve.wait_ge(*dve_s.at(i, "valid"))
                dve.wait_ge(*pe_s.before(i, "S", NT - 1, C - 1))
                dve.tensor_scalar(mrow[:, :, :], valid[0:1, :].unsqueeze(1).to_broadcast([1, HC, SKP]), 1.0, MASKED,
                                  ALU.subtract, ALU.mult).then_inc(*dve_s.mark("mrow"))
                dve.wait_ge(*pe_s.at(i, "K"))
                for c in range(C):
                    m = dve.scalar_tensor_tensor(Kv[:, c, :], banks["K",][:, c * SKP:(c + 1) * SKP], bk[:, c:c + 1],
                                                 valid[:, :], ALU.add, ALU.mult)
                    m.then_inc(*dve_s.mark(*(("Kv",) if c == C - 1 else ("Kv", c))))
                dve.wait_ge(*dve_s.at(i, "Kv"))
                for n in range(HC):
                    q = slice(n * HD, (n + 1) * HD)
                    dve.wait_ge(*act_s.at(i, "Kd", n))
                    m = dve.tensor_tensor(Kd[1][q, :, n * SKP:(n + 1) * SKP], Kv[q, :, :],
                                          f32(Kd[0][q, :, n * SKP:(n + 1) * SKP]), ALU.subtract)
                    m.then_inc(*dve_s.mark(*(("Kd",) if n == HC - 1 else ("Kd", n))))
                lo(("V",), vdiag(Vd[1], C, HC, P, HD, SK), banks["V",][0:SK, :].rearrange("p (c h d) -> p c h d", c=C, h=HC),
                   vdiag(Vd[0], C, HC, P, HD, SK))
                for c in range(C):
                    lo(("Q", c), qT[1][:, c, :], banks["Q", c][:, :], qT[0][:, c, :], bq[:, c:c + 1])

                def softmax_end(t):
                    dve.wait_ge(*act_s.at(i, "exp", t))
                    dve.reduce_sum(rs[:, t, :], E[:, t, :, :], AX).then_inc(*dve_s.mark("sum", t))
                    dve.wait_ge(*dve_s.at(i, "sum", t))
                    dve.reciprocal(rs[:, t, :], rs[:, t, :]).then_inc(*dve_s.mark("rsum", t))
                    dve.wait_ge(*dve_s.at(i, "rsum", t))
                    dve.tensor_tensor(E[:, t, :, :], E[:, t, :, :], rs[:, t, :].unsqueeze(2).to_broadcast([P, H, SK]),
                                      ALU.mult).then_inc(*dve_s.mark("probs", t))

                for t in range(NT):
                    for c in range(C):
                        s = banks["S", t, c][:, 0:HC * SKP].rearrange("p (h s) -> p h s", h=HC)[:, :, 0:SK]
                        hs = slice(c * HC, (c + 1) * HC)
                        dve.wait_ge(*pe_s.at(i, "S", t, c))
                        dve.reduce_max(mx[:, t, hs], s, AX).then_inc(*dve_s.mark("max", t, c))
                        dve.wait_ge(*dve_s.at(i, "max", t, c))
                        dve.tensor_tensor(E[:, t, hs, :], s, mx[:, t, hs].unsqueeze(2).to_broadcast([P, HC, SK]),
                                          ALU.subtract).then_inc(*dve_s.mark("shifted", t, c))
                    if t:
                        softmax_end(t - 1)
                softmax_end(NT - 1)
                for c in range(C):
                    for n in range(HC):
                        h = c * HC + n
                        lo(("PT", h), PT[h % 2][1][:, :], banks["PT", h][0:SK, :], PT[h % 2][0][:, :])
                    lo(("O", c), oT[1][:, c, :], banks["O", c][:, :], oT[0][:, c, :], bv[:, c:c + 1])
                dve.wait_ge(x1_out, i * 16 + 16)
                for t in range(NT):
                    dve.wait_ge(*pe_s.at(i, "Wo", t))
                    dve.tensor_tensor(x1[:, t, :], banks["Wo", t][:, :], x[:, t, :], ALU.add).then_inc(*dve_s.mark("read", "Wo", t))
                    dve.wait_ge(*dve_s.at(i, "read", "Wo", t))
                    dve.tensor_tensor(x1[:, t, :], x1[:, t, :], bo_bc[:, :], ALU.add).then_inc(*dve_s.mark("res", t))
                dve.wait_ge(*pe_s.at(i, "xT", C - 1))
                layer_norm(x1, "ln2")
                for c in range(C):
                    lo(("fT", c), xT[1][:, c, :], banks["fT", c][:, :], xT[0][:, c, :])
                for j in range(J):
                    dve.wait_ge(*act_s.at(i, "hhi", j))
                    dve.tensor_tensor(hTs[1][:, j, :], hT[:, j, :], f32(hTs[0][:, j, :]), ALU.subtract)\
                       .then_inc(*dve_s.mark("hlo", j))
                dve.wait_ge(*pe_s.at(i, "L"))
                dve.tensor_tensor(L[:, :, :], banks["L",][:, 0:NT * NS].rearrange("p (t s) -> p t s", t=NT),
                                  b2_bc[:, :].unsqueeze(1).to_broadcast([P, NT, NS]), ALU.add)\
                   .then_inc(*dve_s.mark("read", "L"))
                wait_apart(dve, dve_s.at(i, "read", "L"), passed)
                for t in range(NT):
                    dve.max(top[:, t, :], L[:, t, :]).then_inc(*dve_s.mark("top", t))
                wait_apart(dve, dve_s.at(i, "top", NT - 1), passed)
                for t in range(NT):
                    dve.match_replace(rest[:, t, :], top[:, t, :], L[:, t, :], -3e38).then_inc(*dve_s.mark("rest", t))
                dve.tensor_tensor(el[:, :, :], L[:, :, :], top[:, :, 0:1].to_broadcast([P, NT, NS]), ALU.subtract)\
                   .then_inc(*dve_s.mark("lshift"))
                dve.wait_ge(*dve_s.at(i, "rest", NT - 1))
                dve.tensor_tensor(rest[:, :, :], rest[:, :, :], L[:, :, :], ALU.not_equal).then_inc(*dve_s.mark("chosen"))
                dve.wait_ge(*dve_s.at(i, "chosen"))
                dve.wait_ge(*act_s.at(i, "lexp"))
                dve.tensor_tensor(el[:, :, :], el[:, :, :], rest[:, :, :], ALU.mult).then_inc(*dve_s.mark("kept"))
                dve.wait_ge(*dve_s.at(i, "kept"))
                dve.reduce_sum(asum[:, :], el[:, :, :], AX).then_inc(*dve_s.mark("asum"))
                dve.wait_ge(*dve_s.at(i, "asum"))
                dve.reciprocal(asum[:, :], asum[:, :]).then_inc(*dve_s.mark("rasum"))
                dve.wait_ge(*dve_s.at(i, "rasum"))
                dve.wait_ge(*pe_s.before(i, "si"))
                dve.tensor_tensor(alpha[:, :, :], el[:, :, :], asum[:, :].unsqueeze(2).to_broadcast([P, NT, NS]), ALU.mult)\
                   .then_inc(*dve_s.mark("alpha"))
                dve.wait_ge(*pe_s.at(i, "aT"))
                dve.wait_ge(aT_out, i * 16 + 16)
                dve.tensor_copy(aT[:, :], banks["aT",][0:NS, :]).then_inc(*dve_s.mark("aT"))
                dve.wait_ge(*pe_s.at(i, "si"))
                dve.tensor_scalar(den[:, :], banks["den",][0:NS, 0:1], 1e-8, None, ALU.add).then_inc(*dve_s.mark("read", "den"))
                dve.wait_ge(*dve_s.at(i, "read", "den"))
                dve.reciprocal(den[:, :], den[:, :]).then_inc(*dve_s.mark("rden"))
                dve.wait_ge(*dve_s.at(i, "rden"))
                dve.wait_ge(si_out, i * 16 + 16)
                dve.tensor_scalar(si[:, :], banks["si",][0:NS, :], den[:, :], None, ALU.mult).then_inc(*dve_s.mark("si"))


def vdiag(tile, C, HC, p, hd, sk):
    return tile[0:sk, :, :].rearrange("k c (h w) -> k c h w", h=HC)[:, :, :, 0:hd]



def build_slots(nc, orders, a, si_s, vo_s):
    B = si_s.shape[0]
    NS, D = a["L0_ffn_slot_init"].shape
    DQ = a["L0_ffn_wq"].shape[1]
    C = D // P
    BS = B * NS
    NP = BS // P
    SCALE = float(DQ) ** -0.5

    with ExitStack() as ctx:
        st = Stage(nc, ctx, "sl", orders)
        sb, sem = st.sb, st.sem
        ident = sb("ident", [P, P])
        minus_half = sb("minus_half", [P, NP])
        WihT = sb("WihT", [P, C, 3 * D])
        WhhT = sb("WhhT", [P, C, 3 * D])
        wq, wk = sb("wq", [P, C, DQ]), sb("wk", [P, C, DQ])
        wv, wvp, wo = (sb(n, [P, C, D]) for n in ("wv", "wvp", "wo"))
        S0T = sb("S0T", [P, C, NS])
        bih, bhh = sb("bih", [P, 3 * C]), sb("bhh", [P, 3 * C])
        bq, bk, bvp = sb("bq", [P, 1]), sb("bk", [P, 1]), sb("bvp", [P, C])
        bv_bc, g_bc, b_bc = (sb(n, [P, D]) for n in ("bv_bc", "g_bc", "b_bc"))
        si = sb("si", [P, NP, D])
        siT = sb("siT", [P, C, BS])
        gh = sb("gh", [P, 3 * C, NS])
        gate = [sb(f"gate{n}", [P, BS]) for n in range(3)]
        SnT = sb("SnT", [P, C, BS])
        qT, kT = sb("qT", [P, BS]), sb("kT", [P, BS])
        v = si
        A = sb("A", [P, NP, P])
        AT = sb("AT", [P, NP, P])
        amx, asum = sb("amx", [P, NP]), sb("asum", [P, NP])
        y = sb("y", [P, NP, D])
        stats, mv = sb("stats", [P, NP, 6]), sb("mv", [P, NP, 2])
        rstd = sb("rstd", [P, NP])
        yT = siT
        svT = SnT
        vo = y

        bank = [st.ps(f"bank{n}", [P, 512]) for n in range(8)]
        setup, small, si_in, out = sem("setup"), sem("small"), sem("si_in"), sem("out")
        w_in = {n: sem(n + "_in") for n in ("WihT", "WhhT", "wqk", "wv", "wvp", "wo")}
        pe_s, act_s, dve_s, pool_s = (st.steps(n) for n in ("products", "act", "dve", "rstd"))
        rows = lambda w: w.rearrange("(c p) n -> p c n", p=P)

        units = [("siT", c) for c in range(C)] + [("gh", n) for n in range(3)]
        units += [("gi", c, n) for c in range(C) for n in range(3)]
        units += [("q",), ("k",)] + [("v", j) for j in range(NP)]
        for j in range(NP):
            units += [("A", j), ("AT", j), ("y", j)]
        units += [("yT", c) for c in range(C)] + [("sv", c) for c in range(C)] + [("vo", j) for j in range(NP)]
        banks = Banks(bank, units)
        dve_s.alias(("read", "q"), ("q",))
        dve_s.alias(("read", "k"), ("k",))
        for j in range(NP):
            dve_s.alias(("read", "v", j), ("v", j))
            dve_s.alias(("read", "y", j), ("y+bv", j))
            dve_s.alias(("read", "AT", j), ("AT", j))
            dve_s.alias(("read", "vo", j), ("vo", j))
            act_s.alias(("read", "A", j), ("A", j, 1))
        for c in range(C):
            dve_s.alias(("read", "siT", c), ("siT", c))
            dve_s.alias(("read", "gi", c, 0), ("r in", c))
            dve_s.alias(("read", "gi", c, 1), ("z in", c))
            dve_s.alias(("read", "gi", c, 2), ("n in", c))
            dve_s.alias(("read", "yT", c), ("yT", c))
            dve_s.alias(("read", "sv", c), ("sv", c))
        for n in range(3):
            dve_s.alias(("read", "gh", n), ("gh", n, C - 1))

        block = ctx.enter_context(nc.Block())

        smalls = [(S0T[:, :, :], rows(a["slot_init_T"])), (bih[:, :], a["L0_ffn_bih"]), (bhh[:, :], a["L0_ffn_bhh"]),
                  (bq[:, :], a["L0_ffn_bq"]), (bk[:, :], a["L0_ffn_bk"]), (bvp[:, :], a["L0_ffn_bvp"]),
                  (bv_bc[:, :], a["L0_ffn_bv"].partition_broadcast(P)),
                  (g_bc[:, :], a["L0_ffn_ln_g"].partition_broadcast(P)),
                  (b_bc[:, :], a["L0_ffn_ln_b"].partition_broadcast(P))]

        @block.sync
        def _(sp):
            sp.dma_start(si[:, :, :], si_s.rearrange("(j b) s d -> (b s) j d", j=NP)).then_inc(si_in, 16)
            sp.dma_start(WhhT[:, :, :], rows(a["Whh_T"])).then_inc(w_in["WhhT"], 16)
            sp.dma_start(WihT[:, :, :], rows(a["Wih_T"])).then_inc(w_in["WihT"], 16)
            sp.dma_start(wq[:, :, :], rows(a["L0_ffn_wq"])).then_inc(w_in["wqk"], 16)
            sp.dma_start(wk[:, :, :], rows(a["L0_ffn_wk"])).then_inc(w_in["wqk"], 16)
            for n, t in (("wv", wv), ("wvp", wvp), ("wo", wo)):
                sp.dma_start(t[:, :, :], rows(a["L0_ffn_" + n])).then_inc(w_in[n], 16)
            for j in range(NP):
                sp.wait_ge(*dve_s.at(0, "vo", j))
                sp.dma_start(vo_s[2 * j:2 * j + 2].rearrange("b s d -> (b s) d"), vo[:, j, :]).then_inc(out, 16)
            sp.wait_ge(out, 16 * NP)

        @block.gpsimd
        def _(pool):
            pool.sem_inc(pool_s.sem, pool_s.per)
            make_identity(pool, ident, setup)
            pool.memset(minus_half[:, :], -0.5).then_inc(setup, 1)
            pool.memset(A[:, :, :], 0.0).then_inc(setup, 1)
            pool.wait_ge(*dve_s.at(0, "var"))
            pool.tensor_scalar(rstd[:, :], mv[:, :, 1], EPS, None, ALU.add).then_inc(*pool_s.mark("ve"))
            pool.wait_ge(*pool_s.at(0, "ve"))
            pool.tensor_tensor(rstd[:, :], rstd[:, :], minus_half[:, :], ALU.pow).then_inc(*pool_s.mark("rstd"))

        @block.tensor
        def _(pe):
            pe.sem_inc(pe_s.sem, pe_s.per)
            pe.wait_ge(setup, 4)
            pe.wait_ge(si_in, 16)

            def unit(*name):
                if banks.user_before(name)[1] is False:
                    take(pe, banks, (act_s, dve_s), 0, name)
                return banks[name]

            def matmuls(out, w, m0, m1, x, n0, n1):
                for k in range(C):
                    last = pe.matmul(out, w[:, k, m0:m1], x[:, k, n0:n1], start=(k == 0), stop=(k == C - 1))
                return last

            for c in range(C):
                ps = unit("siT", c)
                for j in range(NP):
                    m = pe.transpose(ps[:, j * P:(j + 1) * P], si[:, j, c * P:(c + 1) * P], ident[:, :])
                m.then_inc(*pe_s.mark("siT", c))
            pe.wait_ge(small, 16 * len(smalls))
            pe.wait_ge(w_in["WhhT"], 16)
            for n in range(3):
                ps = unit("gh", n)
                for c in range(C):
                    m = matmuls(ps[:, c * NS:(c + 1) * NS], WhhT, n * D + c * P, n * D + (c + 1) * P, S0T, 0, NS)
                m.then_inc(*pe_s.mark("gh", n))
            pe.wait_ge(w_in["WihT"], 16)
            pe.wait_ge(*dve_s.at(0, "siT", C - 1))
            for c in range(C):
                for n in range(3):
                    ps = unit("gi", c, n)
                    matmuls(ps[:, :], WihT, n * D + c * P, n * D + (c + 1) * P, siT, 0, BS).then_inc(*pe_s.mark("gi", c, n))
            pe.wait_ge(w_in["wqk"], 32)
            pe.wait_ge(*dve_s.at(0, "S", C - 1))
            for name, w in (("q", wq), ("k", wk)):
                ps = unit(name)
                matmuls(ps[:, :], w, 0, DQ, SnT, 0, BS).then_inc(*pe_s.mark(name))
            pe.wait_ge(w_in["wv"], 16)
            for j in range(NP):
                ps = unit("v", j)
                matmuls(ps[:, :], SnT, j * P, (j + 1) * P, wv, 0, D).then_inc(*pe_s.mark("v", j))
            for j in range(NP):
                ps = unit("A", j)
                pe.wait_ge(*dve_s.at(0, "k"))
                pe.matmul(ps[:, 0:P], qT[:, j * P:(j + 1) * P], kT[:, j * P:(j + 1) * P], start=True, stop=True)\
                  .then_inc(*pe_s.mark("A", j))
                ps = unit("AT", j)
                pe.wait_ge(*dve_s.at(0, "A", j))
                pe.transpose(ps[:, 0:P], A[:, j, :], ident[:, :]).then_inc(*pe_s.mark("AT", j))
                ps = unit("y", j)
                pe.wait_ge(*dve_s.at(0, "AT", j))
                for c in range(C):
                    cols = slice(c * P, (c + 1) * P)
                    pe.matmul(ps[:, cols], AT[:, j, :], v[:, j, cols], start=True, stop=False)
                    m = pe.matmul(ps[:, cols], SnT[:, c, j * P:(j + 1) * P], ident[:, :], start=False, stop=True)
                m.then_inc(*pe_s.mark("y", j))
            for c in range(C):
                ps = unit("yT", c)
                for j in range(NP):
                    pe.wait_ge(*dve_s.at(0, "yn", j))
                    m = pe.transpose(ps[:, j * P:(j + 1) * P], y[:, j, c * P:(c + 1) * P], ident[:, :])
                m.then_inc(*pe_s.mark("yT", c))
            pe.wait_ge(w_in["wvp"], 16)
            pe.wait_ge(*dve_s.at(0, "yT", C - 1))
            for c in range(C):
                ps = unit("sv", c)
                matmuls(ps[:, :], wvp, c * P, (c + 1) * P, yT, 0, BS).then_inc(*pe_s.mark("sv", c))
            pe.wait_ge(w_in["wo"], 16)
            pe.wait_ge(*dve_s.at(0, "sv", C - 1))
            for j in range(NP):
                ps = unit("vo", j)
                matmuls(ps[:, :], svT, j * P, (j + 1) * P, wo, 0, D).then_inc(*pe_s.mark("vo", j))

        @block.scalar
        def _(act):
            act.sem_inc(act_s.sem, act_s.per)
            for dst, src in smalls:
                act.dma_start(dst, src).then_inc(small, 16)
            act.wait_ge(small, 16 * len(smalls))
            for c in range(C):
                for n, (name, func) in enumerate((("r", ACT.Sigmoid), ("z", ACT.Sigmoid), ("n", ACT.Tanh))):
                    act.wait_ge(*dve_s.at(0, name + " in", c))
                    if name == "n":
                        act.wait_ge(*dve_s.at(0, "r*h", c))
                        act.activation(gate[n][:, :], gate[n][:, :], func, bias=bih[:, 2 * C + c:2 * C + c + 1])\
                           .then_inc(*act_s.mark(name, c))
                    else:
                        act.activation(gate[n][:, :], gate[n][:, :], func).then_inc(*act_s.mark(name, c))
            for j in range(NP):
                act.wait_ge(*dve_s.at(0, "amx", j))
                for b in range(2):
                    s = slice(b * NS, (b + 1) * NS)
                    act.activation(A[s, j, s], banks["A", j][s, s], ACT.Exp, scale=SCALE, bias=amx[s, j:j + 1],
                                   accum_out=asum[s, j:j + 1]).then_inc(*act_s.mark("A", j, b))

        @block.vector
        def _(dve):
            dve.sem_inc(dve_s.sem, dve_s.per)
            dve.wait_ge(setup, 4)
            dve.wait_ge(small, 16 * len(smalls))

            def copy(name, dst, *bias):
                dve.wait_ge(*pe_s.at(0, *name))
                if bias:
                    m = dve.tensor_scalar(dst, banks[name][:, :], bias[0], None, ALU.add)
                else:
                    m = dve.tensor_copy(dst, banks[name][:, 0:dst.shape[-1]])
                return m.then_inc(*dve_s.mark(*name))

            for c in range(C):
                copy(("siT", c), siT[:, c, :])
            dve.tensor_tensor(bhh[:, 0:2 * C], bhh[:, 0:2 * C], bih[:, 0:2 * C], ALU.add).then_inc(*dve_s.mark("b"))
            dve.wait_ge(*dve_s.at(0, "b"))
            for n in range(3):
                dve.wait_ge(*pe_s.at(0, "gh", n))
                for c in range(C):
                    g = n * C + c
                    dve.tensor_scalar(gh[:, g, :], banks["gh", n][:, c * NS:(c + 1) * NS], bhh[:, g:g + 1], None, ALU.add)\
                       .then_inc(*dve_s.mark("gh", n, c))
            dve.wait_ge(*dve_s.at(0, "gh", 2, C - 1))
            by_batch = lambda t: t.rearrange("p (b s) -> p b s", b=B)
            same = lambda t: t.unsqueeze(1).to_broadcast([P, B, NS])
            for c in range(C):
                r, z, n = (by_batch(g[:, :]) for g in gate)
                gi = [by_batch(banks["gi", c, m][:, :]) for m in range(3)]
                if c:
                    dve.wait_ge(*dve_s.at(0, "S", c - 1))
                dve.wait_ge(*pe_s.at(0, "gi", c, 0))
                dve.tensor_tensor(r, gi[0], same(gh[:, c, :]), ALU.add).then_inc(*dve_s.mark("r in", c))
                dve.wait_ge(*pe_s.at(0, "gi", c, 1))
                dve.tensor_tensor(z, gi[1], same(gh[:, C + c, :]), ALU.add).then_inc(*dve_s.mark("z in", c))
                dve.wait_ge(*act_s.at(0, "r", c))
                dve.tensor_tensor(r, r, same(gh[:, 2 * C + c, :]), ALU.mult).then_inc(*dve_s.mark("r*h", c))
                dve.wait_ge(*dve_s.at(0, "r*h", c))
                dve.wait_ge(*pe_s.at(0, "gi", c, 2))
                dve.tensor_tensor(n, gi[2], r, ALU.add).then_inc(*dve_s.mark("n in", c))
                dve.wait_ge(*act_s.at(0, "n", c))
                dve.tensor_tensor(r, same(S0T[:, c, :]), n, ALU.subtract).then_inc(*dve_s.mark("S0-n", c))
                dve.wait_ge(*dve_s.at(0, "S0-n", c))
                dve.tensor_tensor(r, r, z, ALU.mult).then_inc(*dve_s.mark("z*", c))
                dve.wait_ge(*dve_s.at(0, "z*", c))
                dve.tensor_tensor(by_batch(SnT[:, c, :]), r, n, ALU.add).then_inc(*dve_s.mark("S", c))
            copy(("q",), qT[:, :], bq[:, 0:1])
            copy(("k",), kT[:, :], bk[:, 0:1])
            for j in range(NP):
                copy(("v", j), v[:, j, :])
            for j in range(NP):
                dve.wait_ge(*pe_s.at(0, "A", j))
                for b in range(2):
                    s = slice(b * NS, (b + 1) * NS)
                    m = dve.reduce_max(amx[s, j:j + 1], banks["A", j][s, s], AX)
                m.then_inc(*dve_s.mark("max", j))
                dve.wait_ge(*dve_s.at(0, "max", j))
                dve.tensor_scalar(amx[:, j:j + 1], amx[:, j:j + 1], -SCALE, None, ALU.mult).then_inc(*dve_s.mark("amx", j))
                dve.wait_ge(*act_s.at(0, "A", j, 1))
                dve.reciprocal(asum[:, j:j + 1], asum[:, j:j + 1]).then_inc(*dve_s.mark("rsum", j))
                dve.wait_ge(*dve_s.at(0, "rsum", j))
                dve.tensor_scalar(A[:, j, :], A[:, j, :], asum[:, j:j + 1], None, ALU.mult).then_inc(*dve_s.mark("A", j))
                copy(("AT", j), AT[:, j, :])
                dve.wait_ge(*pe_s.at(0, "y", j))
                dve.tensor_tensor(y[:, j, :], banks["y", j][:, :], bv_bc[:, :], ALU.add).then_inc(*dve_s.mark("y+bv", j))
                dve.wait_ge(*dve_s.at(0, "y+bv", j))
                dve.bn_stats(stats[:, j, :], y[:, j, :]).then_inc(*dve_s.mark("stats", j))
                dve.wait_ge(*dve_s.at(0, "stats", j))
                m = dve.bn_aggr(mv[:, j, :], stats[:, j, :])
            m.then_inc(*dve_s.mark("var"))
            dve.wait_ge(*dve_s.at(0, "var"))
            dve.wait_ge(*pool_s.at(0, "rstd"))
            for j in range(NP):
                dve.tensor_scalar(y[:, j, :], y[:, j, :], mv[:, j, 0:1], rstd[:, j:j + 1], ALU.subtract, ALU.mult)\
                   .then_inc(*dve_s.mark("normed", j))
                dve.wait_ge(*dve_s.at(0, "normed", j))
                dve.tensor_tensor(y[:, j, :], y[:, j, :], g_bc[:, :], ALU.mult).then_inc(*dve_s.mark("*g", j))
                dve.wait_ge(*dve_s.at(0, "*g", j))
                dve.tensor_tensor(y[:, j, :], y[:, j, :], b_bc[:, :], ALU.add).then_inc(*dve_s.mark("yn", j))
            for c in range(C):
                copy(("yT", c), yT[:, c, :])
            for c in range(C):
                copy(("sv", c), svT[:, c, :], bvp[:, c:c + 1])
            for j in range(NP):
                copy(("vo", j), vo[:, j, :])



def build_latents(nc, orders, a, x1_s, alphaT_s, vo_s, x2_s, z_s):
    B, T, D = x1_s.shape
    SK = a["ctx_1024"].shape[1]
    Z = z_s[0].shape[3]
    C, NT = D // P, T // P
    NS = vo_s.shape[1]
    NL = NT + 1

    with ExitStack() as ctx:
        st = Stage(nc, ctx, "la", orders)
        sb, sem = st.sb, st.sem
        two = lambda name, shape, dt=F32: [sb(f"{name}{n}", shape, dt) for n in range(2)]
        ident = sb("ident", [P, P])
        minus_half = sb("minus_half", [P, NL])
        ones = sb("ones", [1, P])
        bo = sb("bo", [1, D])
        gain = {n: (sb(n + "g", [P, C]), sb(n + "b", [P, C])) for n in ("x", "l")}
        x1, x2 = two("x1", [P, NT, D]), two("x2", [P, NT, D])
        aT, vo, cx = two("aT", [NS, T]), two("vo", [NS, D]), two("cx", [SK, D])
        stats, mv = two("stats", [P, NL, 6]), two("mv", [P, NL, 2])
        ve, rstd = two("ve", [P, NL]), two("rstd", [P, NL])
        xn, cn = two("xn", [P, NT, D]), two("cn", [SK, D])
        full = two("full", [P, C, Z])
        z_hi, z_lo = two("z_hi", [P, C, Z], F32R), two("z_lo", [P, C, Z], F32R)
        bank = [st.ps(f"bank{n}", [P, 512]) for n in range(8)]

        setup, small = sem("setup"), sem("small")
        passed = sem("passed")
        ins = [{n: sem(f"{n}_in{m}") for n in ("x1", "aT", "vo", "cx")} for m in range(2)]
        x2_out, z_out = [sem(f"x2_out{m}") for m in range(2)], [sem(f"z_out{m}") for m in range(2)]
        pe_s, act_s, dve_s, pool_s = (st.steps(n) for n in ("products", "act", "dve", "rstd"))

        units = []
        for m in range(2):
            units += [("x2", m, t) for t in range(NT)] + [("zT", m, c) for c in range(C)] + [("cT", m)]
        banks = Banks(bank, units)
        for m in range(2):
            for t in range(NT):
                dve_s.alias(("read", "x2", m, t), ("x2", m, t))
            for c in range(C):
                act_s.alias(("read", "zT", m, c), ("full", m, c))
            act_s.alias(("read", "cT", m), ("full", m, C, C - 1))

        smalls = [(bo[:, :], a["L0_ffn_bo"].rearrange("(o n) -> o n", o=1))]
        for n in gain:
            smalls += [(gain[n][0][:, :], a[f"L1_xattn_ln_{n}_g"]), (gain[n][1][:, :], a[f"L1_xattn_ln_{n}_b"])]
        PAIRS = B // 2
        block = ctx.enter_context(nc.Block())

        @block.sync
        def _(sp):
            for dst, src in smalls:
                sp.dma_start(dst, src).then_inc(small, 16)
            with sp.Fori(0, PAIRS) as i:
                for m in range(2):
                    one = lambda ap: ap[bass.ds(2 * i + m, 1)]
                    sp.wait_ge(*dve_s.before(i, "x2", m, NT - 1))
                    sp.dma_start(x1[m][:, :, :], one(x1_s).rearrange("b (t p) d -> p (b t) d", p=P)).then_inc(ins[m]["x1"], 16)
                    sp.dma_start(aT[m][:, :], one(alphaT_s).rearrange("b s t -> (b s) t")).then_inc(ins[m]["aT"], 16)
                    sp.dma_start(vo[m][:, :], one(vo_s).rearrange("b s d -> (b s) d")).then_inc(ins[m]["vo"], 16)
                    sp.wait_ge(*dve_s.before(i, "cn", m))
                    sp.dma_start(cx[m][:, :], one(a["ctx_1024"]).rearrange("b s d -> (b s) d")).then_inc(ins[m]["cx"], 16)

        @block.gpsimd
        def _(pool):
            pool.sem_inc(pool_s.sem, pool_s.per)
            make_identity(pool, ident, setup)
            pool.memset(minus_half[:, :], -0.5).then_inc(setup, 1)
            pool.memset(ones[:, :], 1.0).then_inc(setup, 1)
            for m in range(2):
                pool.memset(mv[m][:, :, :], 1.0).then_inc(setup, 1)
                pool.memset(full[m][:, :, :], 0.0).then_inc(setup, 1)
            with pool.Fori(0, PAIRS) as i:
                for m in range(2):
                    wait_apart(pool, dve_s.at(i, "var", m), passed)
                    pool.tensor_scalar(ve[m][:, 0:NT], mv[m][:, 0:NT, 1], 1.0 + EPS, EPS * EPS, ALU.mult, ALU.add)\
                        .then_inc(*pool_s.mark("ve", m))
                    pool.tensor_scalar(ve[m][:, NT:NL], mv[m][:, NT:NL, 1], EPS, None, ALU.add).then_inc(*pool_s.mark("vc", m))
                    pool.wait_ge(*pool_s.at(i, "vc", m))
                    pool.tensor_tensor(rstd[m][:, :], ve[m][:, :], minus_half[:, :], ALU.pow).then_inc(*pool_s.mark("rstd", m))

        @block.tensor
        def _(pe):
            pe.sem_inc(pe_s.sem, pe_s.per)
            pe.wait_ge(setup, 8)
            pe.wait_ge(small, 16 * len(smalls))
            with pe.Fori(0, PAIRS) as i:
                def unit(*name):
                    take(pe, banks, (act_s, dve_s), i, name)
                    return banks[name]

                for m in range(2):
                    pe.wait_ge(ins[m]["aT"], i * 16 + 16)
                    pe.wait_ge(ins[m]["vo"], i * 16 + 16)
                    for t in range(NT):
                        ps = unit("x2", m, t)
                        pe.matmul(ps[:, :], ones[:, :], bo[:, :], start=True, stop=False)
                        pe.matmul(ps[:, :], aT[m][:, t * P:(t + 1) * P], vo[m][:, :], start=False, stop=True)\
                          .then_inc(*pe_s.mark("x2", m, t))
                    for c in range(C):
                        ps = unit("zT", m, c)
                        for t in range(NT):
                            if c == 0:
                                pe.wait_ge(*dve_s.at(i, "xn", m, t))
                            tr = pe.transpose(ps[:, t * P:(t + 1) * P], xn[m][:, t, c * P:(c + 1) * P], ident[:, :])
                        tr.then_inc(*pe_s.mark("zT", m, c))
                    ps = unit("cT", m)
                    pe.wait_ge(*dve_s.at(i, "cn", m))
                    for c in range(C):
                        tr = pe.transpose(ps[:, c * SK:(c + 1) * SK], cn[m][:, c * P:(c + 1) * P], ident[0:SK, 0:SK])
                    tr.then_inc(*pe_s.mark("cT", m))

        @block.scalar
        def _(act):
            act.sem_inc(act_s.sem, act_s.per)
            for m in range(2):
                act.sem_inc(x2_out[m], 16)
                act.sem_inc(z_out[m], 32)
            act.wait_ge(small, 16 * len(smalls))
            act.wait_ge(setup, 8)
            with act.Fori(0, PAIRS) as i:
                for m in range(2):
                    act.wait_ge(*dve_s.before(i, "lo", m, C - 1))
                    act.wait_ge(z_out[m], i * 32 + 32)
                    for c in range(C):
                        act.wait_ge(*pe_s.at(i, "zT", m, c))
                        act.activation(full[m][:, c, 0:T], banks["zT", m, c][:, :], ACT.Identity,
                                       scale=gain["l"][0][:, c:c + 1], bias=gain["l"][1][:, c:c + 1])\
                           .then_inc(*act_s.mark("full", m, c))
                    act.wait_ge(*pe_s.at(i, "cT", m))
                    for c in range(C):
                        act.activation(full[m][:, c, T:T + SK], banks["cT", m][:, c * SK:(c + 1) * SK], ACT.Identity,
                                       scale=gain["x"][0][:, c:c + 1], bias=gain["x"][1][:, c:c + 1])\
                           .then_inc(*act_s.mark("full", m, C, c))
                    for c in range(C):
                        act.wait_ge(*act_s.at(i, "full", m, C, C - 1))
                        act.activation(z_hi[m][:, c, :], full[m][:, c, :], ACT.Copy).then_inc(*act_s.mark("hi", m, c))
                    act.wait_ge(*dve_s.at(i, "x2", m, NT - 1))
                    act.dma_start(x2_s[bass.ds(2 * i + m, 1)].rearrange("b (t p) d -> p (b t) d", p=P), x2[m][:, :, :])\
                       .then_inc(x2_out[m], 16)
                    act.wait_ge(*dve_s.at(i, "lo", m, C - 1))
                    act.dma_start(z_s[0][bass.ds(2 * i + m, 1)].rearrange("b p c z -> p (b c) z"), f32(z_hi[m][:, :, :])).then_inc(z_out[m], 16)
                    act.dma_start(z_s[1][bass.ds(2 * i + m, 1)].rearrange("b p c z -> p (b c) z"), f32(z_lo[m][:, :, :])).then_inc(z_out[m], 16)
            for m in range(2):
                act.wait_ge(x2_out[m], 16 * (PAIRS + 1))
                act.wait_ge(z_out[m], 32 * (PAIRS + 1))

        @block.vector
        def _(dve):
            dve.sem_inc(dve_s.sem, dve_s.per)
            dve.wait_ge(setup, 8)
            with dve.Fori(0, PAIRS) as i:
                for m in range(2):
                    dve.wait_ge(ins[m]["x1"], i * 16 + 16)
                    dve.wait_ge(x2_out[m], i * 16 + 16)
                    for t in range(NT):
                        dve.wait_ge(*pe_s.at(i, "x2", m, t))
                        dve.tensor_tensor(x2[m][:, t, :], banks["x2", m, t][:, :], x1[m][:, t, :], ALU.add)\
                           .then_inc(*dve_s.mark("x2", m, t))
                        dve.wait_ge(*dve_s.at(i, "x2", m, t))
                        dve.bn_stats(stats[m][:, t, :], x2[m][:, t, :]).then_inc(*dve_s.mark("stats", m, t))
                    dve.wait_ge(ins[m]["cx"], i * 16 + 16)
                    dve.bn_stats(stats[m][0:SK, NT, :], cx[m][:, :]).then_inc(*dve_s.mark("stats", m, NT))
                    wait_apart(dve, dve_s.at(i, "stats", m, NT), passed)
                    for t in range(NL):
                        rows = slice(0, SK if t == NT else P)
                        last = dve.bn_aggr(mv[m][rows, t, :], stats[m][rows, t, :])
                    last.then_inc(*dve_s.mark("var", m))
                    dve.wait_ge(*dve_s.at(i, "var", m))
                    dve.wait_ge(*pool_s.at(i, "rstd", m))
                    dve.wait_ge(*pe_s.before(i, "cT", m))
                    for t in range(NT):
                        dve.tensor_scalar(xn[m][:, t, :], x2[m][:, t, :], mv[m][:, t, 0:1], rstd[m][:, t:t + 1],
                                          ALU.subtract, ALU.mult).then_inc(*dve_s.mark("xn", m, t))
                    dve.tensor_scalar(cn[m][:, :], cx[m][:, :], mv[m][0:SK, NT, 0:1], rstd[m][0:SK, NT:NL],
                                      ALU.subtract, ALU.mult).then_inc(*dve_s.mark("cn", m))
                    for c in range(C):
                        dve.wait_ge(*act_s.at(i, "hi", m, c))
                        dve.tensor_tensor(z_lo[m][:, c, :], full[m][:, c, :], f32(z_hi[m][:, c, :]), ALU.subtract)\
                           .then_inc(*dve_s.mark("lo", m, c))



class Claims:

    def __init__(self, name, orders):
        self.known, self.order = orders.get(name), []
        orders[name] = self.order

    def before(self, bank, unit):
        self.order.append((bank, unit))
        if not self.known:
            return unit, True
        n = len(self.order) - 1
        earlier = [u for b, u in self.known[:n] if b == bank]
        if earlier:
            return earlier[-1], False
        return [u for b, u in self.known if b == bank][-1], True


def build_perceiver(nc, orders, a, z_s, o_s):
    B = z_s[0].shape[0]
    C, Z = z_s[0].shape[2], z_s[0].shape[3]
    INNER = a["L1_xattn_Wq"].shape[1]
    SK = a["ctx_1024"].shape[1]
    T = a["x"].shape[1]
    SKP = Z - T
    NK = T + SK
    NT = T // P
    HD, H = 64, INNER // 64
    NPAIR = H // 2
    NC = NT + 1
    QH = 4
    SCALE = HD ** -0.5
    MASKED = 2.0 ** 126
    KEYS = [P] * NT + [SK]

    with ExitStack() as ctx:
        st = Stage(nc, ctx, "pa", orders)
        sb, sem = st.sb, st.sem
        two = lambda name, shape, dt=F32: [sb(f"{name}{n}", shape, dt) for n in range(2)]
        pair = lambda name, shape: (sb(name + "_hi", shape, F32R), sb(name + "_lo", shape, F32R))
        ident = sb("ident", [P, P])
        one_row = sb("one_row", [1, P])
        ones = sb("ones", [1, P], F32R)
        mask_words = sb("mask_words", [1, B * SK // 4], I32)
        mask_u = mask_words[:, :].bitcast(mybir.dt.uint8)
        mrow = sb("mrow", [1, B, SKP], F32R)
        z = pair("z", [P, C, Z])
        Wq = pair("Wq", [P, C, INNER])
        Wkv = pair("Wkv", [P, C, 2 * INNER])
        U = [two(f"U{m}", [P, T], F32R) for m in range(2)]
        Uc = two("Uc", [P, NPAIR, SKP], F32R)
        Qh = [two(f"Qh{m}", [P, T], F32R) for m in range(2)]
        Ql = [two(f"Ql{m}", [P, T], F32R) for m in range(2)]
        V = two("V", [P, NC, QH, P], F32R)
        Pr = two("Pr", [P, NT, NK + 1])
        RING = 4
        PTh, PTl = (sb(n, [P, RING, T], F32R) for n in ("PTh", "PTl"))
        low = sb("low", [HD, T])
        O = sb("O_pair", [P, T])
        least, rs = (sb(n, [P, 2, NT]) for n in ("least", "rs"))

        S = [st.ps(f"S{n}", [P, 1024]) for n in range(2)]
        bank = {n: st.ps(n, [P, 512]) for n in ("T0", "T1", "O", "J")}

        setup, mask_in, consts = sem("setup"), sem("mask_in"), sem("consts")
        z_in = sem("z_in")
        dup = [sem(f"dup{m}") for m in range(2)]
        o_out = sem("o_out")
        pe_s, act_s, dve_s = (st.steps(n) for n in ("products", "act", "dve"))
        claims = Claims("pa_banks", orders)
        for h in range(H):
            dve_s.alias(("read", "O", h), ("O", h))

        rows = lambda w: w.rearrange("(c p) n -> p c n", p=P)
        weights = []
        half = lambda w, n: w[:, :, n * 512:(n + 1) * 512]
        for n in (2, 3, 0, 1):
            weights.append((half(rows(a["L1_xattn_Wkv"]), n), half(Wkv[0], n), half(Wkv[1], n)))
        for n in range(2):
            weights.append((half(rows(a["L1_xattn_Wq"]), n), half(Wq[0], n), half(Wq[1], n)))
        slots = [t[:, :, :].rearrange("p t k -> p (t k)")[:, 0:2048] for t in Pr]
        w_sync, w_scalar, w_vector, w_cut = load_and_split(st, weights, "w", slots)

        def parts(unit):
            if unit[0] == "V":
                return [j for j in range(unit[2], min(unit[2] + 2, NC))]
            return [(0, 1), (2, 3)] if unit[0] in ("Q", "K") else [(0, 1, 2, 3)]

        lead = [("Q", 0), ("K", 0), ("Kc", 0), ("Kc", 1), ("V", 0, 0), ("V", 0, 2)]
        begins = {3: ("V", 0, 4)}
        for n in range(2 * (NPAIR - 1)):
            begins[NT * n] = ("QK"[n % 2], 1 + n // 2)
        for q in range(1, H // QH):
            for n, (tick, j) in enumerate(((6, 0), (10, 2), (15, 4))):
                begins[16 * (q - 1) + tick] = ("V", q, j)
        begins.update(zip((60, 62, 64, 65, 66, 68), lead))
        starts = {tick + n: (unit, part) for tick, unit in begins.items() for n, part in enumerate(parts(unit))}

        work, dve_work, later = [("S", 0, 0)], [], []
        scored = lambda n: [divmod(n, NT)] if 0 <= n < H * NT else []
        for n in range((H + 2) * NT):
            h, t = divmod(n, NT)
            for kind, units in (("rsum", scored(n - 1)), ("norm", scored(n - 1)), ("least", scored(n))):
                dve_work += [(kind,) + u for u in units]
            dve_work += later
            work += [("S",) + u for u in scored(n + 1)]
            work += [("exp",) + u for u in scored(n)]
            later = []
            if n - 1 in starts:
                unit, part = starts[n - 1]
                if part == parts(unit)[-1]:
                    later.append(("R",) + unit)
            tick = ([("PV", h - 2, 3), ("PV", h - 2, 4), ("O", h - 2)],
                    [("T", h - 1, 0), ("T", h - 1, 1)],
                    [("PV", h - 1, 0), ("T", h - 1, 2), ("PV", h - 1, 1), ("T", h - 1, 3)],
                    [("PV", h - 1, 2), ("T", h - 1, 4)])[t]
            later += [u for u in tick if 0 <= u[1] < H]
            work += later
            if n in starts:
                work.append(("X",) + starts[n])
        dve_work += later
        last_projection = ("K", NPAIR - 1)

        def bank_of(u):
            if u[0] == "T":
                return "T%d" % ((u[1] * NC + u[2]) % 2)
            return "O" if u[0] == "PV" else "J"

        def values(u):
            _, q, j = u
            n, J = KEYS[j], len(parts(u))
            src = bank["J"][0:n, 0:J * QH * HD].rearrange("p (j h d) -> p j h d", j=J, d=HD)
            to = V[q % 2][0:n, j:j + J, :, :]
            return src, to[:, :, :, 0:HD], to[:, :, :, HD:P]

        ring = lambda h, c: (h * NC + c) % RING

        def wait(engine, signal, i, earlier, *name):
            engine.wait_ge(*(signal.before if earlier else signal.at)(i, *name))

        block = ctx.enter_context(nc.Block())

        @block.sync
        def _(sp):
            sp.dma_start(mask_words[:, :], a["mask_BxS2_bk0"]).then_inc(mask_in, 16)
            w_sync(sp)

            def load(i):
                for n in range(2):
                    sp.dma_start(f32(z[n][:, :, :]), z_s[n][bass.ds(i, 1)].rearrange("b p c z -> p (b c) z")).then_inc(z_in, 16)

            def duplicate(i, p):
                m = p % 2
                sp.wait_ge(*act_s.at(i, "hi", "Q", p, 0))
                sp.dma_start(f32(Qh[m][0][HD:P, :]), f32(Qh[m][0][0:HD, :])).then_inc(dup[m], 16)
                sp.wait_ge(*act_s.at(i, "hi", "Q", p, 1))
                sp.dma_start(f32(Qh[m][1][0:HD, :]), f32(Qh[m][1][HD:P, :])).then_inc(dup[m], 16)

            def one_round(i, coming):
                for p in range(1, NPAIR):
                    duplicate(i, p)
                sp.wait_ge(*pe_s.at(i, *last_projection))
                load(coming)
                duplicate(i, 0)

            load(0)
            duplicate(-1, 0)
            with sp.Fori(0, B - 1) as i:
                one_round(i, i + 1)
            one_round(B - 1, B - 1)
            sp.wait_ge(dup[0], 32 * (B * NPAIR // 2 + 1))

        @block.gpsimd
        def _(pool):
            make_identity(pool, ident, setup)
            pool.memset(one_row[:, :], 1.0).then_inc(setup, 1)
            pool.memset(f32(mrow[:, :, :]), 0.0).then_inc(setup, 1)
            for m in range(2):
                for x in range(2):
                    pool.memset(f32(Ql[m][x][:, :]), 0.0).then_inc(setup, 1)

        @block.tensor
        def _(pe):
            pe.wait_ge(setup, 8)
            pe.wait_ge(consts, 2)
            w_cut(pe)

            def claim(i, u, b):
                last, earlier = claims.before(b, u)
                for s in (act_s, dve_s):
                    if s.has("read", *last):
                        wait(pe, s, i, earlier, "read", *last)
                return bank[b] if b in bank else S[int(b[1])]

            def project(u, part):
                ps, kind = bank[bank_of(u)], u[0]
                if kind == "Kc":
                    for n in range(NPAIR // 2):
                        p = u[1] * (NPAIR // 2) + n
                        for k in part:
                            last = product(pe, ps[:, n * SKP:(n + 1) * SKP], [w[:, k, p * P:(p + 1) * P] for w in Wkv],
                                           [x[:, k, T:Z] for x in z], k == 0, k == C - 1)
                elif kind in ("Q", "K"):
                    for k in part:
                        last = product(pe, ps[:, :], [w[:, k, u[1] * P:(u[1] + 1) * P] for w in (Wq if kind == "Q" else Wkv)],
                                       [x[:, k, 0:T] for x in z], k == 0, k == C - 1)
                else:
                    _, q, first = u
                    j = part
                    n0, out = INNER + q * QH * HD, ps[0:KEYS[j], (j - first) * QH * HD:(j - first + 1) * QH * HD]
                    for k in range(C):
                        last = product(pe, out, [x[:, k, j * P:j * P + KEYS[j]] for x in z],
                                       [w[:, k, n0:n0 + QH * HD] for w in Wkv], k == 0, k == C - 1)
                if part == parts(u)[-1]:
                    last.then_inc(*pe_s.mark(*u))

            pe_s.lead = True
            pe.wait_ge(z_in, 32)
            for n, u in enumerate(lead):
                if n:
                    pe.wait_ge(*dve_s.at(-1, "read", *lead[n - 1]))
                pe_s.lead_up(pe, *u)
                for part in parts(u):
                    project(u, part)
            pe_s.lead_up(pe)
            pe_s.lead = False
            with pe.Fori(0, B) as i:
                for u in work:
                    kind = u[0]
                    if kind == "X":
                        _, unit, part = u
                        if part == parts(unit)[0]:
                            if unit == lead[0]:
                                pe.wait_ge(z_in, i * 32 + 64)
                            claim(i, unit, bank_of(unit))
                        project(unit, part)
                    elif kind == "S":
                        _, h, t = u
                        p, x = h // 2, h % 2
                        if t == 0 and x == 0:
                            pe.wait_ge(dup[p % 2], (i * (NPAIR // 2) + (p // 2 + 1)) * 32)
                            if h:
                                pe.wait_ge(*dve_s.at(i, "read", "K", p))
                            else:
                                pe.wait_ge(*dve_s.before(i, "read", "Kc", 1))
                        ps = claim(i, u, "S%d" % (t % 2))
                        cols = slice(t * P, (t + 1) * P)
                        qh, ql = Qh[p % 2][x][:, cols], Ql[p % 2][x][:, cols]
                        pe.matmul(ps[:, 0:T], qh, U[p % 2][x][:, :], start=True, stop=False)
                        pe.matmul(ps[:, 0:T], ql, U[p % 2][x][:, :], start=False, stop=True)
                        out = ps[:, T:Z]
                        pe.matmul(out, qh, Uc[x][:, p, :], start=True, stop=False)
                        pe.matmul(out, ql, Uc[x][:, p, :], start=False, stop=False)
                        pe.matmul(out, ones[:, :], mrow[:, bass.ds(i, 1), :].rearrange("o b s -> o (b s)"),
                                  start=False, stop=True).then_inc(*pe_s.mark(*u))
                    elif kind == "T":
                        _, h, c = u
                        if (h, c) == (0, 0):
                            claims.before(bank_of(u), u)
                            ps = bank[bank_of(u)]
                            pe.wait_ge(*dve_s.at(i, "probs", h, NT - 1))
                        else:
                            ps = claim(i, u, bank_of(u))
                        for t in range(NT):
                            m = pe.transpose(ps[0:KEYS[c], t * P:(t + 1) * P], Pr[h % 2][:, t, c * P:c * P + KEYS[c]], ident[:, :])
                        m.then_inc(*pe_s.mark(*u))
                    elif kind == "PV":
                        _, h, c = u
                        if c == 0:
                            claims.before("O", ("O", h))
                        ps, r, n = bank["O"], ring(h, c), KEYS[c]
                        v = V[(h // QH) % 2][0:n, c, h % QH, :]
                        pe.wait_ge(*dve_s.at(i, "read", "T", h, c))
                        pe.matmul(ps[:, :], v, PTh[0:n, r, :], start=(c == 0), stop=False)
                        pe.matmul(ps[:, :], v, PTl[0:n, r, :], start=False, stop=(c == NC - 1)).then_inc(*pe_s.mark(*u))

        @block.scalar
        def _(act):
            act.sem_inc(o_out, 16)
            w_scalar(act)

            def copy(out, src, *name, scale=1.0):
                act.activation(out, src, ACT.Copy, scale=scale).then_inc(*act_s.mark(*name))

            def read(i, u):
                act.wait_ge(*pe_s.at(i, *u))
                ps, kind = bank[bank_of(u)], u[0]
                if kind == "V":
                    if act_s.lead:
                        act_s.lead_up(act, "hi", *u)
                    src, v_hi, _ = values(u)
                    copy(v_hi, src, "hi", *u)
                    return
                for x in range(2):
                    r = slice(x * HD, (x + 1) * HD)
                    name = ("hi", *u, x)
                    if act_s.lead:
                        act_s.lead_up(act, *name)
                    if kind == "Kc":
                        g = slice(u[1] * (NPAIR // 2), (u[1] + 1) * (NPAIR // 2))
                        copy(Uc[x][r, g, :], ps[r, 0:(NPAIR // 2) * SKP].rearrange("p (g s) -> p g s", s=SKP), *name)
                    elif kind == "Q":
                        copy(Qh[u[1] % 2][x][r, :], ps[r, :], *name, scale=-SCALE)
                    else:
                        copy(U[u[1] % 2][x][r, :], ps[r, :], *name)

            act_s.lead = True
            for u in lead:
                read(-1, u)
            act_s.lead_up(act)
            act_s.lead = False
            with act.Fori(0, B) as i:
                def store(p):
                    act.wait_ge(*dve_s.at(i, "O", 2 * p + 1))
                    act.dma_start(o_s[bass.ds(i, 1), p].rearrange("b p t -> (b p) t"), O[:, :]).then_inc(o_out, 16)

                for u in work:
                    kind = u[0]
                    if kind == "R":
                        read(i, u[1:])
                    elif kind == "exp":
                        _, h, t = u
                        if t == 2 and h % 2 and h >= 3:
                            store((h - 3) // 2)
                        act.wait_ge(*dve_s.at(i, "least", h, t))
                        act.activation(Pr[h % 2][:, t, 0:NK], S[t % 2][:, 0:NK], ACT.Exp, scale=-1.0,
                                       bias=least[:, h % 2, t:t + 1], accum_out=rs[:, h % 2, t:t + 1])\
                           .then_inc(*act_s.mark("read", "S", h, t))
                    elif kind == "T":
                        _, h, c = u
                        act.wait_ge(*pe_s.at(i, *u))
                        copy(PTh[0:KEYS[c], ring(h, c), :], bank[bank_of(u)][0:KEYS[c], :], "hi", *u)
                    elif kind == "O":
                        h = u[1]
                        act.wait_ge(*pe_s.at(i, "PV", h, NC - 1))
                        copy(low[:, :], bank["O"][HD:P, :], "low", h)
                store(NPAIR - 1)
            act.wait_ge(o_out, 16 * (B * NPAIR + 1))

        @block.vector
        def _(dve):
            dve.wait_ge(setup, 8)
            dve.tensor_copy(ones[:, :], one_row[:, :]).then_inc(consts, 1)
            dve.wait_ge(mask_in, 16)
            dve.tensor_scalar(mrow[:, :, 0:SK], mask_u.rearrange("o (b s) -> o b s", b=B), 1.0, -MASKED,
                              ALU.subtract, ALU.mult).then_inc(consts, 1)
            w_vector(dve)

            def lo(out, src, hi_ap, *name):
                dve.tensor_tensor(out, src, f32(hi_ap), ALU.subtract).then_inc(*dve_s.mark(*name))

            def read(i, u):
                ps, kind = bank[bank_of(u)], u[0]
                if kind == "V":
                    dve.wait_ge(*act_s.at(i, "hi", *u))
                    if dve_s.lead:
                        dve_s.lead_up(dve, "read", *u)
                    src, v_hi, v_lo = values(u)
                    lo(v_lo, src, v_hi, "read", *u)
                    return
                for x in range(2):
                    r, o = slice(x * HD, (x + 1) * HD), slice((1 - x) * HD, (2 - x) * HD)
                    name = ("read", *u) if x else ("lo", *u)
                    dve.wait_ge(*act_s.at(i, "hi", *u, x))
                    if dve_s.lead:
                        dve_s.lead_up(dve, *name)
                    if kind == "Kc":
                        g = slice(u[1] * (NPAIR // 2), (u[1] + 1) * (NPAIR // 2))
                        lo(Uc[x][o, g, :], ps[r, 0:(NPAIR // 2) * SKP].rearrange("p (g s) -> p g s", s=SKP), Uc[x][r, g, :], *name)
                    elif kind == "Q":
                        dve.scalar_tensor_tensor(Ql[u[1] % 2][x][r, :], ps[r, :], -SCALE, f32(Qh[u[1] % 2][x][r, :]),
                                                 ALU.mult, ALU.subtract).then_inc(*dve_s.mark(*name))
                    else:
                        lo(U[u[1] % 2][x][o, :], ps[r, :], U[u[1] % 2][x][r, :], *name)

            dve_s.lead = True
            for u in lead:
                read(-1, u)
            dve_s.lead_up(dve)
            dve_s.lead = False
            with dve.Fori(0, B) as i:
                def normalise(h, t):
                    dve.wait_ge(*dve_s.at(i, "rsum", h, t))
                    p = Pr[h % 2][:, t, 0:NK]
                    dve.tensor_scalar(p, p, rs[:, h % 2, t:t + 1], None, ALU.mult).then_inc(*dve_s.mark("probs", h, t))

                for u in dve_work:
                    kind = u[0]
                    if kind == "R":
                        read(i, u[1:])
                    elif kind == "least":
                        _, h, t = u
                        dve.wait_ge(*pe_s.at(i, "S", h, t))
                        dve.tensor_reduce(least[:, h % 2, t:t + 1], S[t % 2][:, 0:NK], AX, ALU.min)\
                           .then_inc(*dve_s.mark("least", h, t))
                    elif kind == "rsum":
                        _, h, t = u
                        dve.wait_ge(*act_s.at(i, "read", "S", h, t))
                        dve.reciprocal(rs[:, h % 2, t:t + 1], rs[:, h % 2, t:t + 1]).then_inc(*dve_s.mark(*u))
                    elif kind == "norm":
                        normalise(*u[1:])
                    elif kind == "T":
                        _, h, c = u
                        dve.wait_ge(*act_s.at(i, "hi", *u))
                        n, r, ps = KEYS[c], ring(h, c), bank[bank_of(u)]
                        lo(PTl[0:n, r, :], ps[0:n, :], PTh[0:n, r, :], "read", *u)
                    elif kind == "O":
                        h = u[1]
                        p = h // 2
                        dve.wait_ge(*act_s.at(i, "low", h))
                        if h % 2 == 0:
                            dve.wait_ge(o_out, (i * NPAIR + (p + 1)) * 16)
                        dve.tensor_tensor(O[(h % 2) * HD:(h % 2 + 1) * HD, :], bank["O"][0:HD, :], low[:, :], ALU.add)\
                           .then_inc(*dve_s.mark("O", h))



def build_experts(nc, orders, a, o_s, x2_s, out):
    B, T, D = a["x"].shape
    C, NT = D // P, T // P
    K = a["L1_xattn_Wout"].shape[0] // P
    E, _, HE = a["L1_ffn_W1"].shape
    HALVES = (range(0, NT // 2), range(NT // 2, NT))

    with ExitStack() as ctx:
        st = Stage(nc, ctx, "ex", orders)
        sb, sem = st.sb, st.sem
        pair = lambda name, shape: (sb(name + "_hi", shape, F32R), sb(name + "_lo", shape, F32R))
        ident = sb("ident", [P, P])
        eight = sb("eight", [P, E])
        minus_half = sb("minus_half", [P, NT])
        sel = sb("sel", [E, E, P], F32R)
        Wout = pair("Wout", [P, K, D])
        W1 = pair("W1", [HE, E * C, HE])
        W2 = pair("W2", [HE, E, D])
        Wg = pair("Wg", [P, C, E])
        Wg_raw = sb("Wg_raw", [P, C, E])
        b2 = pair("b2", [E, D])
        g_bc, b_bc = sb("g_bc", [P, D]), sb("b_bc", [P, D])
        gain, shift = sb("gain", [P, E * C]), sb("shift", [P, E * C])
        b1 = sb("b1", [P, E])
        b1x = sb("b1x", [P, E])
        o_raw = sb("o_raw", [P, K, T])
        o = pair("o", [P, K, T])
        x = sb("x", [P, NT, D])
        xh = sb("xh", [P, NT, D])
        stats, mv = sb("stats", [P, NT, 6]), sb("mv", [P, NT, 2])
        ve, rstd = sb("ve", [P, NT]), sb("rstd", [P, NT])
        xT = pair("xT", [P, C, T])
        LT = sb("LT", [E, T])
        L = sb("L", [P, NT, E])
        top = sb("top", [P, NT, E])
        idx = sb("idx", [P, NT, E], U32)
        idx_f = sb("idx_f", [P, NT])
        hot = sb("hot", [P, NT, E])
        hotT = sb("hotT", [E, T], F32R)
        g_both = sb("g", [P, 2 * T])
        g = [g_both[:, n * T:(n + 1) * T] for n in range(2)]
        sel_f = g_both[0:E, 0:E * P].rearrange("k (e p) -> k e p", e=E)
        b2_raw = g_both[0:E, 0:D]
        h = [pair(f"h{n}", [P, T]) for n in range(2)]

        acc = [st.ps(f"acc{n}", [P, 512]) for n in range(4)]
        bank = {n: st.ps(n, [P, 512]) for n in "ABCD"}

        setup, small, w1_in, b2_in = sem("setup"), sem("small"), sem("w1_in"), sem("b2_in")
        passed = sem("passed")
        consts, bias_ps, w1_ready, w1_hi = sem("consts"), sem("bias_ps"), sem("w1_ready"), sem("w1_hi")
        small_cut = sem("small_cut")
        o_in, x_in, stored = sem("o_in"), sem("x_in"), sem("stored")
        pe_s, act_s, dve_s, pool_s = (st.steps(n) for n in ("products", "act", "dve", "pool"))
        claims = Claims("ex_banks", orders)
        for t in range(NT):
            dve_s.alias(("read", "Wout", t), ("y", t))
            dve_s.alias(("read", "out", t), ("x4", t))
        dve_s.alias(("read", "hotT"), ("hotT",))

        rows = lambda w: w.rearrange("(c p) n -> p c n", p=P)
        w1_slots = [t[:, :, :].rearrange("p t d -> p (t d)") for t in (x, xh)]
        EH = E // 2
        w1_raw = [s.rearrange("p (k n) -> p k n", n=HE) for s in w1_slots]
        weights = []
        for n in range(2):
            s = slice(n * K // 2, (n + 1) * K // 2)
            weights.append((rows(a["L1_xattn_Wout"])[:, s, :], Wout[0][:, s, :], Wout[1][:, s, :]))
        for n in range(2):
            s = slice(n * EH, (n + 1) * EH)
            weights.append((a["L1_ffn_W2"].rearrange("e h d -> h e d")[:, s, :], W2[0][:, s, :], W2[1][:, s, :]))
        flat = o_raw[:, :, :].rearrange("p k t -> p (k t)")
        w_sync, w_scalar, w_vector, w_cut = load_and_split(st, weights, "w", [flat[:, 0:2048], flat[:, 2048:4096]])

        smalls = [(gain[:, :], a["L1_ffn_ln_scale"]), (shift[:, :], a["L1_ffn_ln_bias"]), (b1[:, :], a["L1_ffn_b1"]),
                  (Wg_raw[:, :, :], rows(a["Wg_T"])),
                  (g_bc[:, :], a["L1_xattn_ln_o_g"].partition_broadcast(P)),
                  (b_bc[:, :], a["L1_xattn_ln_o_b"].partition_broadcast(P))]
        one = lambda ap, i: ap[bass.ds(i, 1)].rearrange("b (t p) d -> p (b t) d", p=P)
        block = ctx.enter_context(nc.Block())

        @block.sync
        def _(sp):
            for dst, src in smalls:
                sp.dma_start(dst, src).then_inc(small, 16)
            for n in range(2):
                src = a["L1_ffn_W1"][n * EH:(n + 1) * EH].rearrange("e (c p) h -> p (e c) h", p=P)
                sp.dma_start(w1_raw[n], src).then_inc(w1_in, 16)
            sp.wait_ge(consts, 1)
            sp.dma_start(b2_raw, a["L1_ffn_b2"]).then_inc(b2_in, 16)
            w_sync(sp)
            w_cut(sp)
            sp.wait_ge(small_cut, 3)

            def load(last, i):
                if last is not None:
                    sp.wait_ge(*dve_s.before(last, "olo", K - 1))
                sp.dma_start(o_raw[:, :, :], o_s[bass.ds(i, 1)].rearrange("b k p t -> p (b k) t")).then_inc(o_in, 16)
                if last is not None:
                    sp.wait_ge(*dve_s.at(last, "x4", NT - 1))
                sp.dma_start(x[:, :, :], one(x2_s, i)).then_inc(x_in, 16)

            load(None, 0)
            with sp.Fori(0, B - 1) as i:
                load(i, i + 1)
            load(B - 1, B - 1)
            sp.wait_ge(x_in, 16 * (B + 1))

        @block.gpsimd
        def _(pool):
            pool.sem_inc(pool_s.sem, pool_s.per)
            make_identity(pool, ident, setup)
            pool.memset(minus_half[:, :], -0.5).then_inc(setup, 1)
            pool.iota(eight[:, :], pattern=[[1, E]], base=0, channel_multiplier=0,
                      allow_small_or_imprecise_dtypes=True).then_inc(setup, 1)
            pool.memset(sel_f[:, :, :], 0.0).then_inc(setup, 1)
            pool.wait_ge(setup, 5)
            pool.affine_select(out=sel_f[:, :, :], in_=sel_f[:, :, :], compare_op=ALU.not_equal, fill=1.0,
                               base=0, pattern=[[-1, E], [0, P]], channel_multiplier=1).then_inc(setup, 1)
            with pool.Fori(0, B) as i:
                for n, half in enumerate(HALVES):
                    s = slice(half[0], half[-1] + 1)
                    for ln, scale, eps in (("ln_o", 1.0, EPS), ("ln", 1.0 + EPS, EPS * EPS)):
                        wait_apart(pool, dve_s.at(i, ln, "var", n), passed)
                        pool.tensor_scalar(ve[:, s], mv[:, s, 1], scale, eps, ALU.mult, ALU.add).then_inc(*pool_s.mark(ln, "ve", n))
                        pool.wait_ge(*pool_s.at(i, ln, "ve", n))
                        pool.tensor_tensor(rstd[:, s], ve[:, s], minus_half[:, s], ALU.pow).then_inc(*pool_s.mark(ln, "rstd", n))

        @block.tensor
        def _(pe):
            pe.sem_inc(pe_s.sem, pe_s.per)
            pe.wait_ge(small, 16 * len(smalls))
            pe.wait_ge(w1_in, 32)
            for e in range(E):
                for c in range(C):
                    m = pe.matmul(bank["A"][:, e:e + 1], w1_raw[e // EH][:, (e % EH) * C + c, :],
                                  shift[:, e * C + c:e * C + c + 1], start=(c == 0), stop=(c == C - 1))
            m.then_inc(bias_ps, 1)
            pe.wait_ge(setup, 6)
            pe.wait_ge(consts, 1)
            pe.wait_ge(small_cut, 3)
            w_cut(pe)
            with pe.Fori(0, B) as i:
                def claim(ps, b, *u):
                    last, earlier = claims.before(b, u)
                    for s in (act_s, dve_s):
                        if s.has("read", *last):
                            pe.wait_ge(*(s.before if earlier else s.at)(i, "read", *last))
                    return ps

                on = lambda b, *u: claim(bank[b], b, *u)

                for half in HALVES:
                    for k in range(K):
                        if half[0] == 0:
                            pe.wait_ge(*dve_s.before(i, "olo", k))
                        for t in half:
                            if k == 0:
                                claim(acc[t], t, "Wout", t)
                            m = product(pe, acc[t][:, :], [z[:, k, t * P:(t + 1) * P] for z in o],
                                        [w[:, k, :] for w in Wout], k == 0, k == K - 1)
                            if k == K - 1:
                                m.then_inc(*pe_s.mark("Wout", t))
                for c in range(C):
                    ps = on("ABCD"[c], "xT", c)
                    for t in range(NT):
                        if c == 0:
                            pe.wait_ge(*dve_s.at(i, "xh", t))
                        m = pe.transpose(ps[:, t * P:(t + 1) * P], xh[:, t, c * P:(c + 1) * P], ident[:, :])
                    m.then_inc(*pe_s.mark("xT", c))

                ps = on("C", "LT")
                pe.wait_ge(*dve_s.at(i, "read", "xT", C - 1))
                for c in range(C):
                    m = product(pe, ps[0:E, :], [w[:, c, :] for w in Wg], [z[:, c, :] for z in xT], c == 0, c == C - 1)
                m.then_inc(*pe_s.mark("LT"))

                def hidden(e):
                    ps = on("AB"[e % 2], "h", e)
                    for c in range(C):
                        m = product(pe, ps[:, :], [w[:, e * C + c, :] for w in W1], [z[:, c, :] for z in xT], c == 0, c == C - 1)
                    m.then_inc(*pe_s.mark("h", e))

                def mask(e):
                    ps = on("CD"[e % 2], "M", e)
                    pe.matmul(ps[:, :], sel[:, e, :], hotT[:, :], start=True, stop=True).then_inc(*pe_s.mark("M", e))

                hidden(0)
                ps = on("D", "L")
                wait_apart(pe, dve_s.at(i, "read", "LT"), passed)
                for t in range(NT):
                    m = pe.transpose(ps[:, t * E:(t + 1) * E], LT[:, t * P:(t + 1) * P], ident[0:E, 0:E])
                m.then_inc(*pe_s.mark("L"))
                hidden(1)
                ps = on("D", "hotT")
                pe.wait_ge(*dve_s.at(i, "hot"))
                for t in range(NT):
                    m = pe.transpose(ps[0:E, t * P:(t + 1) * P], hot[:, t, :], ident[:, :])
                m.then_inc(*pe_s.mark("hotT"))
                pe.wait_ge(*dve_s.at(i, "hotT"))
                for e in range(2):
                    mask(e)
                for t in range(NT):
                    claim(acc[t], t, "out", t)
                    for n in range(2):
                        pe.matmul(acc[t][:, :], hotT[:, t * P:(t + 1) * P], b2[n][:, :], start=(n == 0), stop=False)
                for e in range(E):
                    pe.wait_ge(*dve_s.at(i, "lo", e))
                    for t in range(NT):
                        m = product(pe, acc[t][:, :], [z[:, t * P:(t + 1) * P] for z in h[e % 2]],
                                    [w[:, e, :] for w in W2], False, e == E - 1)
                        if e == E - 1:
                            m.then_inc(*pe_s.mark("out", t))
                    if e < E - 1:
                        m.then_inc(*pe_s.mark("used", e))
                    if e + 2 < E:
                        hidden(e + 2)
                        mask(e + 2)

        @block.scalar
        def _(act):
            act.sem_inc(stored, 16)
            for n in range(2):
                act.wait_ge(w1_ready, n + 1)
                s = slice(n * EH * C, (n + 1) * EH * C)
                act.activation(W1[0][:, s, :], w1_raw[n], ACT.Copy).then_inc(w1_hi, 1)
            w_scalar(act)

            def cut_o(k):
                act.activation(o[0][:, k, :], o_raw[:, k, :], ACT.Copy).then_inc(*act_s.mark("ohi", k))

            act_s.lead = True
            act.wait_ge(o_in, 16)
            for k in range(K):
                act_s.lead_up(act, "ohi", k)
                cut_o(k)
            act_s.lead_up(act)
            act_s.lead = False
            with act.Fori(0, B) as i:
                for c in range(C):
                    act.wait_ge(*pe_s.at(i, "xT", c))
                    act.activation(xT[0][:, c, :], bank["ABCD"[c]][:, :], ACT.Copy).then_inc(*act_s.mark("hi", "xT", c))

                def gelu(e):
                    act.wait_ge(*pe_s.at(i, "h", e))
                    if e < 2:
                        act.wait_ge(*dve_s.before(i, "lo", e + E - 2))
                    else:
                        act.wait_ge(*dve_s.at(i, "lo", e - 2))
                    act.activation(g[e % 2], bank["AB"[e % 2]][:, :], ACT.Gelu, bias=b1x[:, e:e + 1])\
                       .then_inc(*act_s.mark("read", "h", e))

                for e in range(E):
                    gelu(e)
                    act.wait_ge(*dve_s.at(i, "read", "M", e))
                    if e >= 2:
                        act.wait_ge(*pe_s.at(i, "used", e - 2))
                    else:
                        act.wait_ge(*pe_s.before(i, "out", NT - 1))
                    act.activation(h[e % 2][0][:, :], g[e % 2], ACT.Copy).then_inc(*act_s.mark("hhi", e))
                act.wait_ge(o_in, i * 16 + 32)
                for k in range(K):
                    cut_o(k)
                act.wait_ge(*dve_s.at(i, "x4", NT - 1))
                act.dma_start(one(out, i), xh[:, :, :]).then_inc(stored, 16)
            act.wait_ge(stored, 16 * (B + 1))

        @block.vector
        def _(dve):
            dve.wait_ge(setup, 6)
            dve.tensor_copy(sel[:, :, :], sel_f[:, :, :]).then_inc(consts, 1)
            dve.wait_ge(bias_ps, 1)
            dve.tensor_tensor(b1x[:, :], bank["A"][:, 0:E], b1[:, :], ALU.add).then_inc(small_cut, 1)
            for n in range(2):
                s = slice(n * EH * C, (n + 1) * EH * C)
                dve.tensor_tensor(w1_raw[n], w1_raw[n], gain[:, s].unsqueeze(2).to_broadcast([P, EH * C, HE]), ALU.mult)\
                   .then_inc(w1_ready, 1)
            for n in range(2):
                s = slice(n * EH * C, (n + 1) * EH * C)
                dve.wait_ge(w1_hi, n + 1)
                dve.tensor_tensor(W1[1][:, s, :], w1_raw[n], f32(W1[0][:, s, :]), ALU.subtract).then_inc(w1_ready, 1)
            for raw, cut, loaded in ((Wg_raw[:, :, :], [w[:, :, :] for w in Wg], None),
                                     (b2_raw, [w[:, :] for w in b2], b2_in)):
                if loaded is not None:
                    dve.wait_ge(loaded, 16)
                dve.tensor_copy(cut[0], raw).then_inc(consts, 1)
                dve.wait_ge(consts, 2 if loaded is None else 3)
                dve.tensor_tensor(cut[1], raw, f32(cut[0]), ALU.subtract).then_inc(small_cut, 1)
            dve.wait_ge(w1_ready, 4)
            w_vector(dve)

            def cut_o(i, k):
                dve.wait_ge(*act_s.at(i, "ohi", k))
                if dve_s.lead:
                    dve_s.lead_up(dve, "olo", k)
                dve.tensor_tensor(o[1][:, k, :], o_raw[:, k, :], f32(o[0][:, k, :]), ALU.subtract)\
                   .then_inc(*dve_s.mark("olo", k))

            dve_s.lead = True
            for k in range(K):
                cut_o(-1, k)
            dve_s.lead_up(dve)
            dve_s.lead = False
            with dve.Fori(0, B) as i:
                def moments(ln, t, src):
                    dve.bn_stats(stats[:, t, :], src).then_inc(*dve_s.mark(ln, "stats", t))

                def aggregate(ln, n, half, meanwhile=lambda: None):
                    wait_apart(dve, dve_s.at(i, ln, "stats", half[-1]), passed)
                    for t in half:
                        m = dve.bn_aggr(mv[:, t, :], stats[:, t, :])
                    m.then_inc(*dve_s.mark(ln, "var", n))
                    meanwhile()
                    dve.wait_ge(*dve_s.at(i, ln, "var", n))
                    dve.wait_ge(*pool_s.at(i, ln, "rstd", n))

                dve.wait_ge(stored, i * 16 + 16)
                for n, half in enumerate(HALVES):
                    for t in half:
                        dve.wait_ge(*pe_s.at(i, "Wout", t))
                        moments("ln_o", t, acc[t][:, :])

                    def add_shift():
                        s = slice(half[0], half[-1] + 1)
                        dve.wait_ge(x_in, i * 16 + 16)
                        dve.tensor_tensor(x[:, s, :], x[:, s, :], b_bc[:, :].unsqueeze(1).to_broadcast([P, len(half), D]), ALU.add)\
                           .then_inc(*dve_s.mark("x+b", n))

                    aggregate("ln_o", n, half, add_shift)
                    for t in half:
                        dve.scalar_tensor_tensor(xh[:, t, :], acc[t][:, :], mv[:, t, 0:1], g_bc[:, :], ALU.subtract, ALU.mult)\
                           .then_inc(*dve_s.mark("y", t))
                    for t in half:
                        dve.wait_ge(*dve_s.at(i, "y", t))
                        dve.scalar_tensor_tensor(x[:, t, :], xh[:, t, :], rstd[:, t:t + 1], x[:, t, :], ALU.mult, ALU.add)\
                           .then_inc(*dve_s.mark("x3", t))
                    for t in half:
                        dve.wait_ge(*dve_s.at(i, "x3", t))
                        moments("ln", t, x[:, t, :])
                    aggregate("ln", n, half)
                    for t in half:
                        dve.tensor_scalar(xh[:, t, :], x[:, t, :], mv[:, t, 0:1], rstd[:, t:t + 1], ALU.subtract, ALU.mult)\
                           .then_inc(*dve_s.mark("xh", t))
                for c in range(C):
                    dve.wait_ge(*act_s.at(i, "hi", "xT", c))
                    dve.tensor_tensor(xT[1][:, c, :], bank["ABCD"[c]][:, :], f32(xT[0][:, c, :]), ALU.subtract)\
                       .then_inc(*dve_s.mark("read", "xT", c))
                dve.wait_ge(*pe_s.at(i, "LT"))
                dve.tensor_copy(LT[:, :], bank["C"][0:E, :]).then_inc(*dve_s.mark("read", "LT"))
                dve.wait_ge(*pe_s.at(i, "L"))
                dve.tensor_copy(L[:, :, :], bank["D"][:, 0:NT * E].rearrange("p (t e) -> p t e", e=E)).then_inc(*dve_s.mark("read", "L"))
                wait_apart(dve, dve_s.at(i, "read", "L"), passed)
                for t in range(NT):
                    dve.max(top[:, t, :], L[:, t, :]).then_inc(*dve_s.mark("top", t))
                wait_apart(dve, dve_s.at(i, "top", NT - 1), passed)
                for t in range(NT):
                    dve.max_index(idx[:, t, :], top[:, t, :], L[:, t, :]).then_inc(*dve_s.mark("idx", t))
                dve.wait_ge(*dve_s.at(i, "idx", NT - 1))
                dve.tensor_copy(idx_f[:, :], idx[:, :, 0]).then_inc(*dve_s.mark("idx_f"))
                dve.wait_ge(*dve_s.at(i, "idx_f"))
                dve.tensor_tensor(hot[:, :, :], idx_f[:, :].unsqueeze(2).to_broadcast([P, NT, E]),
                                  eight[:, :].unsqueeze(1).to_broadcast([P, NT, E]), ALU.is_equal).then_inc(*dve_s.mark("hot"))
                dve.wait_ge(*pe_s.at(i, "hotT"))
                dve.tensor_copy(hotT[:, :], bank["D"][0:E, :]).then_inc(*dve_s.mark("hotT"))

                def masked(e):
                    dve.wait_ge(*pe_s.at(i, "M", e))
                    dve.wait_ge(*act_s.at(i, "read", "h", e))
                    dve.tensor_tensor(g[e % 2], g[e % 2], bank["CD"[e % 2]][:, :], ALU.mult)\
                       .then_inc(*dve_s.mark("read", "M", e))

                for e in range(E):
                    masked(e)
                    dve.wait_ge(*act_s.at(i, "hhi", e))
                    dve.tensor_tensor(h[e % 2][1][:, :], g[e % 2], f32(h[e % 2][0][:, :]), ALU.subtract)\
                       .then_inc(*dve_s.mark("lo", e))
                for k in range(K // 2):
                    cut_o(i, k)
                for t in range(NT):
                    dve.wait_ge(*pe_s.at(i, "out", t))
                    dve.tensor_tensor(xh[:, t, :], acc[t][:, :], x[:, t, :], ALU.add).then_inc(*dve_s.mark("x4", t))
                for k in range(K // 2, K):
                    cut_o(i, k)



INPUTS = ["x", "ctx_1024", "mask_BxS2_ik0", "mask_BxS2_bk0",
          "L0_xattn_Wq", "L0_xattn_bq", "L0_xattn_Wk", "L0_xattn_bk", "L0_xattn_Wv", "L0_xattn_bv",
          "L0_xattn_Wo", "L0_xattn_bo",
          "L0_ffn_slot_init", "L0_ffn_w1", "L0_ffn_b1", "L0_ffn_w2", "L0_ffn_b2", "L0_ffn_tau",
          "L0_ffn_bih", "L0_ffn_bhh", "L0_ffn_wq", "L0_ffn_bq", "L0_ffn_wk", "L0_ffn_bk",
          "L0_ffn_wv", "L0_ffn_bv", "L0_ffn_ln_g", "L0_ffn_ln_b", "L0_ffn_wvp", "L0_ffn_bvp", "L0_ffn_wo", "L0_ffn_bo",
          "L1_xattn_ln_x_g", "L1_xattn_ln_x_b", "L1_xattn_ln_l_g", "L1_xattn_ln_l_b",
          "L1_xattn_Wq", "L1_xattn_Wkv", "L1_xattn_Wout", "L1_xattn_ln_o_g", "L1_xattn_ln_o_b",
          "L1_ffn_ln_scale", "L1_ffn_ln_bias", "L1_ffn_W1", "L1_ffn_b1", "L1_ffn_W2", "L1_ffn_b2",
          "Wih_T", "Whh_T", "slot_init_T", "Wg_T"]
TRANSPOSED = {"Wih_T": "L0_ffn_Wih", "Whh_T": "L0_ffn_Whh", "slot_init_T": "L0_ffn_slot_init", "Wg_T": "L1_ffn_Wg"}


def two_layers(nc, orders, a, out):
    B, T, D = a["x"].shape
    SK = a["ctx_1024"].shape[1]
    NS = a["L0_ffn_slot_init"].shape[0]
    INNER = a["L1_xattn_Wq"].shape[1]
    Z = T + SK + SK % 2

    def scratch(name, *shape):
        return nc.dram_tensor(name, shape, F32, kind="Internal").ap()

    x1_s, x2_s = scratch("x1_s", B, T, D), scratch("x2_s", B, T, D)
    alphaT_s = scratch("alphaT_s", B, NS, T)
    si_s, vo_s = scratch("si_s", B, NS, D), scratch("vo_s", B, NS, D)
    z_s = [scratch(f"z{n}_s", B, P, D // P, Z) for n in range(2)]
    o_s = scratch("o_s", B, INNER // P, P, T)

    build_layer0(nc, orders, a, x1_s, alphaT_s, si_s)
    build_slots(nc, orders, a, si_s, vo_s)
    build_latents(nc, orders, a, x1_s, alphaT_s, vo_s, x2_s, z_s)
    build_perceiver(nc, orders, a, z_s, o_s)
    build_experts(nc, orders, a, o_s, x2_s, out)


def kernel(**inputs):
    import concourse.bacc as bacc
    from concourse.bass_utils import run_bass_kernel_spmd

    arrays = {}
    for name in INPUTS:
        v = np.asarray(inputs[TRANSPOSED.get(name, name)])
        if name in TRANSPOSED:
            v = v.T
        elif name in COLUMNS:
            v = v.reshape(-1, P).T
        v = np.ascontiguousarray(v)
        if v.dtype == np.bool_:
            v = v.reshape(1, -1).view(np.int32)
        arrays[name] = v

    def program(orders):
        nc = bacc.Bacc("TRN2", target_bir_lowering=False, num_devices=1)
        a = {n: nc.dram_tensor(n, v.shape, mybir.dt.from_np(v.dtype), kind="ExternalInput").ap()
             for n, v in arrays.items()}
        out = nc.dram_tensor("out", arrays["x"].shape, F32, kind="ExternalOutput").ap()
        two_layers(nc, orders, a, out)
        return nc

    orders = {}
    program(orders)
    r = run_bass_kernel_spmd(program(orders), [arrays], core_ids=[0])
    return r.results[0]["out"]
```

```python
from contextlib import ExitStack

import numpy as np
import concourse.bass as bass
from concourse import mybir

F32 = mybir.dt.float32
F32R = mybir.dt.float32r
I32 = mybir.dt.int32
U32 = mybir.dt.uint32
ALU = mybir.AluOpType
ACT = mybir.ActivationFunctionType
AX = mybir.AxisListType.X

P = 128
EPS = 1e-5

COLUMNS = ["L0_xattn_bq", "L0_xattn_bk", "L0_xattn_bv", "L0_ffn_b1", "L0_ffn_bih", "L0_ffn_bhh", "L0_ffn_bq",
           "L0_ffn_bk", "L0_ffn_bvp", "L1_xattn_ln_x_g", "L1_xattn_ln_x_b", "L1_xattn_ln_l_g", "L1_xattn_ln_l_b",
           "L1_ffn_ln_scale", "L1_ffn_ln_bias", "L1_ffn_b1"]


class Signal:

    def __init__(self, sem, orders):
        self.sem, self.known, self.order, self.same = sem, orders.get(sem.name), [], {}
        self.lead, self.reached = False, 0
        orders[sem.name] = self.order

    @property
    def per(self):
        return len(self.known) if self.known else 1

    def mark(self, *name):
        if name not in self.order and not self.lead:
            self.order.append(name)
        return self.sem, 1

    def start(self, engine):
        engine.sem_inc(self.sem, self.per)

    def due(self, engine, *name):
        if self.lead:
            self.lead_up(engine, *name)

    def lead_up(self, engine, *name):
        until = self.ordinal(name) - 1 if name else self.per
        if self.reached:
            engine.wait_ge(self.sem, self.reached)
        if until > self.reached:
            engine.sem_inc(self.sem, until - self.reached)
        self.reached = until + 1

    def alias(self, name, step):
        self.same[name] = step

    def has(self, *name):
        return not self.known or self.same.get(name, name) in self.known

    def ordinal(self, name):
        return self.known.index(self.same.get(name, name)) + 1 if self.known else 1

    def at(self, i, *name):
        return self.sem, i * self.per + (self.per + self.ordinal(name))

    def before(self, i, *name):
        return self.sem, i * self.per + self.ordinal(name)


class Stage:

    def __init__(self, nc, ctx, name, orders):
        self.nc, self.ctx, self.name, self.orders = nc, ctx, name, orders

    def sb(self, name, shape, dt=F32):
        return self.ctx.enter_context(self.nc.sbuf_tensor(f"{self.name}_{name}", shape, dt))

    def ps(self, name, shape):
        return self.ctx.enter_context(self.nc.psum_tensor(f"{self.name}_{name}", shape, F32))

    def sem(self, name):
        return self.ctx.enter_context(self.nc.semaphore(f"{self.name}_{name}"))

    def steps(self, name):
        return Signal(self.sem(name), self.orders)


def wait_apart(engine, step, passed):
    engine.wait_ge(*step)
    engine.sem_inc(passed, 1)


def f32(ap):
    return ap.bitcast(F32)


def product(pe, out, a, b, first, last):
    pe.matmul(out, a[0], b[0], start=first, stop=False)
    pe.matmul(out, a[0], b[1], start=False, stop=False)
    return pe.matmul(out, a[1], b[0], start=False, stop=last)


def make_identity(pool, ident, done):
    pool.memset(ident[:, :], 0.0).then_inc(done, 1)
    pool.wait_ge(done, 1)
    pool.affine_select(out=ident[:, :], in_=ident[:, :], compare_op=ALU.not_equal, fill=1.0,
                       base=0, pattern=[[-1, P]], channel_multiplier=1).then_inc(done, 1)



def load_and_split(st, weights, tag, slots):
    loaded = [st.sem(f"{tag}_w{j}_loaded") for j in range(2)]
    hi_cut, lo_cut = st.sem(f"{tag}_hi_cut"), st.sem(f"{tag}_lo_cut")

    def slot(n):
        _, k, m = weights[n][0].shape
        return slots[n % 2][:, 0:k * m].rearrange("p (k m) -> p k m", k=k)

    def on_sync(sp, first=0, end=len(weights)):
        for n in range(first, end):
            if n >= 2:
                sp.wait_ge(lo_cut, n - 1)
            sp.dma_start(slot(n), weights[n][0]).then_inc(loaded[n % 2], 16)

    def on_scalar(act, first=0, end=len(weights)):
        for n in range(first, end):
            act.wait_ge(loaded[n % 2], 16 * (n // 2 + 1))
            act.activation(weights[n][1], slot(n), ACT.Copy).then_inc(hi_cut, 1)

    def on_vector(dve, first=0, end=len(weights)):
        for n in range(first, end):
            dve.wait_ge(hi_cut, n + 1)
            dve.tensor_tensor(weights[n][2], slot(n), f32(weights[n][1]), ALU.subtract).then_inc(lo_cut, 1)

    def cut(engine, n=len(weights)):
        engine.wait_ge(lo_cut, n)

    return on_sync, on_scalar, on_vector, cut


class Banks:

    def __init__(self, tiles, units):
        self.tiles, self.units = tiles, units

    def __getitem__(self, unit):
        return self.tiles[self.units.index(unit) % len(self.tiles)]

    def user_before(self, unit):
        n, r = self.units.index(unit), len(self.tiles)
        if n >= r:
            return self.units[n - r], False
        return self.units[max(m for m in range(len(self.units)) if m % r == n % r)], True


def take(engine, banks, read, i, unit):
    last, earlier = banks.user_before(unit)
    for signal in read:
        if signal.has("read", *last):
            engine.wait_ge(*(signal.before if earlier else signal.at)(i, "read", *last))



def build_layer0(nc, orders, a, x1_s, alphaT_s, si_s):
    B, T, D = a["x"].shape
    SK = a["ctx_1024"].shape[1]
    SKP = SK + SK % 2
    C, NT = D // P, T // P
    H, HD = 16, 32
    HC = P // HD
    DH = a["L0_ffn_w1"].shape[1]
    J = DH // P
    NS = a["L0_ffn_slot_init"].shape[0]
    KTOP = 8
    SCALE = 1.0 / float(np.sqrt(HD))
    MASKED = 1e9 / SCALE

    with ExitStack() as ctx:
        st = Stage(nc, ctx, "l0", orders)
        sb, sem = st.sb, st.sem
        pair = lambda name, shape: (sb(name + "_hi", shape, F32R), sb(name + "_lo", shape, F32R))

        ident = sb("ident", [P, P])
        minus_half = sb("minus_half", [P, NT])
        ones = sb("ones", [P, P])
        ones_r = sb("ones_r", [1, P], F32R)
        Wq, Wk, Wv, Wo = (pair(n, [P, C, D]) for n in ("Wq", "Wk", "Wv", "Wo"))
        W1 = pair("W1", [P, C, DH])
        W2 = pair("W2", [P, J, NS])
        smean = sb("smean", [P, C])
        b1c = sb("b1c", [P, J])
        hbias = sb("hbias", [P, J])
        bq, bk, bv = (sb(n, [P, C]) for n in ("bq", "bk", "bv"))
        bo_bc = sb("bo_bc", [P, D])
        b2_bc = sb("b2_bc", [P, NS])
        tau = sb("tau", [P, 4])

        x = sb("x", [P, NT, D])
        x1 = sb("x1", [P, NT, D])
        cx = sb("cx", [SK, D])
        mask_i = sb("mask_i", [P, SK], I32)
        valid = sb("valid", [P, SKP])
        mrow = sb("mrow", [1, HC, SKP], F32R)
        stats = sb("stats", [P, NT, 6])
        mv = sb("mv", [P, NT, 2])
        ve = sb("ve", [P, NT])
        rstd = sb("rstd", [P, NT])
        xn = sb("xn", [P, NT, D])
        xT = pair("xT", [P, C, T])
        cT = pair("cT", [P, C, SKP])
        Kv = sb("Kv", [P, C, SKP])
        Kd = pair("Kd", [P, C, HC * SKP])
        Vd = pair("Vd", [SK, C, HC * (P + HD)])
        qT = pair("qT", [P, C, T])
        mx = sb("mx", [P, NT, H])
        E = sb("E", [P, NT, H, SK])
        rs = sb("rs", [P, NT, H])
        PT = [pair(f"PT{n}", [SK, T]) for n in range(2)]
        oT = qT
        flat = E[:, :, :, :].rearrange("p t h s -> p (t h s)")
        w1s = flat[:, 0:C * DH].rearrange("p (c n) -> p c n", c=C)
        slots0 = flat[0:NS, C * DH:C * DH + D]
        hT = flat[:, 0:J * T].rearrange("p (j t) -> p j t", j=J)
        K_rows = flat[0:SK, J * T:J * T + D]
        hTs = tuple(z[:, 0:J, :] for z in oT)
        L = sb("L", [P, NT, NS])
        top = sb("top", [P, NT, KTOP])
        rest = sb("rest", [P, NT, NS])
        el = sb("el", [P, NT, NS])
        asum = sb("asum", [P, NT])
        alpha = sb("alpha", [P, NT, NS])
        aT = sb("aT", [NS, T])
        den = sb("den", [NS, 1])
        si = sb("si", [NS, D])

        flat_slots = [z[:, :, :].rearrange("p t d -> p (t d)") for z in (x1, xn)]

        bank = [st.ps(f"bank{n}", [P, 512]) for n in range(8)]

        setup = sem("setup")
        passed = sem("passed")
        small = sem("small")
        x_in, cx_in, mask_in = sem("x_in"), sem("cx_in"), sem("mask_in")
        x1_out, aT_out, si_out = sem("x1_out"), sem("aT_out"), sem("si_out")
        consts = sem("consts")
        mean_ps, mean_sb, hb_ps = sem("mean_ps"), sem("mean_sb"), sem("hb_ps")
        hb_ready, tau_ready = sem("hb_ready"), sem("tau_ready")
        pe_s, act_s, dve_s, pool_s = (st.steps(n) for n in ("products", "act", "dve", "rstd"))

        dve_s.alias(("read", "KT"), ("Kv",))
        dve_s.alias(("read", "aT"), ("aT",))
        dve_s.alias(("read", "si"), ("si",))
        for t in range(NT):
            for c in range(C):
                dve_s.alias(("read", "S", t, c), ("shifted", t, c))

        rows = lambda w: w.rearrange("(c p) n -> p c n", p=P)
        weights = []
        for name, tile in (("Wk", Wk), ("Wv", Wv), ("Wq", Wq), ("Wo", Wo)):
            weights.append((rows(a["L0_xattn_" + name]), tile[0][:, :, :], tile[1][:, :, :]))
        weights.append((rows(a["L0_ffn_w1"][0:D, :]), W1[0][:, :, :], W1[1][:, :, :]))
        weights.append((rows(a["L0_ffn_w2"]), W2[0][:, :, :], W2[1][:, :, :]))
        for_lead = 2
        w_sync, w_scalar, w_vector, w_cut = load_and_split(st, weights, "w", flat_slots)

        smalls = [(slots0, a["L0_ffn_slot_init"]), (w1s, rows(a["L0_ffn_w1"][D:2 * D, :])),
                  (b1c[:, :], a["L0_ffn_b1"]),
                  (bq[:, :], a["L0_xattn_bq"]), (bk[:, :], a["L0_xattn_bk"]),
                  (bv[:, :], a["L0_xattn_bv"]),
                  (bo_bc[:, :], a["L0_xattn_bo"].partition_broadcast(P)),
                  (b2_bc[:, :], a["L0_ffn_b2"].partition_broadcast(P)),
                  (tau[:, 0:1], a["L0_ffn_tau"].partition_broadcast(P))]

        units = [("xT", c) for c in range(C)]
        groups = [range(c * HC, (c + 1) * HC) for c in range(C)]
        units += [("Q", 0)]
        for c in range(C + 1):
            if c < C:
                units += [("S", t, c) for t in range(NT)]
            if c:
                for h in groups[c - 1]:
                    units += [("PT", h)] + ([("O", c - 1)] if h % HC == 1 else [])
            if c + 1 < C:
                units.append(("Q", c + 1))
        units += [("cT",)] + [("Wo", t) for t in range(NT)] + [("V",)] + [("fT", c) for c in range(C)]
        units += [("h", j) for j in range(J)] + [("K",), ("LT",), ("L",), ("KT",), ("aT",), ("si",), ("den",)]
        banks = Banks(bank, units)

        block = ctx.enter_context(nc.Block())

        @block.sync
        def _(sp):
            for out in (x1_out, aT_out, si_out):
                sp.sem_inc(out, 16)
            for dst, src in smalls:
                sp.dma_start(dst, src).then_inc(small, 16)

            def load_x(i):
                sp.dma_start(x[:, :, :], a["x"][bass.ds(i, 1)].rearrange("b (t p) d -> p (b t) d", p=P)).then_inc(x_in, 16)

            def load_context(i, last=None):
                one = lambda ap: ap[bass.ds(i, 1)]
                if last is not None:
                    sp.wait_ge(*pe_s.before(last, "cT"))
                sp.dma_start(cx[:, :], one(a["ctx_1024"]).rearrange("b s d -> (b s) d")).then_inc(cx_in, 16)
                if last is not None:
                    sp.wait_ge(*dve_s.before(last, "valid"))
                sp.dma_start(mask_i[:, :], one(a["mask_BxS2_ik0"]).rearrange("b s -> (b s)").partition_broadcast(P)).then_inc(mask_in, 16)

            def store(i):
                one = lambda ap: ap[bass.ds(i, 1)]
                sp.wait_ge(*dve_s.at(i, "aT"))
                sp.dma_start(one(alphaT_s).rearrange("b s t -> (b s) t"), aT[:, :]).then_inc(aT_out, 16)
                sp.wait_ge(*dve_s.at(i, "si"))
                sp.dma_start(one(si_s).rearrange("b s d -> (b s) d"), si[:, :]).then_inc(si_out, 16)

            def store_x1(i):
                sp.wait_ge(*dve_s.at(i, "res", NT - 1))
                sp.dma_start(x1_s[bass.ds(i, 1)].rearrange("b (t p) d -> p (b t) d", p=P), x1[:, :, :]).then_inc(x1_out, 16)

            def one_round(i, coming):
                load_context(coming, i)
                store_x1(i)
                load_x(coming)
                store(i)

            w_sync(sp, 0, for_lead)
            load_context(0)
            load_x(0)
            w_sync(sp, for_lead, len(weights))
            with sp.Fori(0, B - 1) as i:
                one_round(i, i + 1)
            one_round(B - 1, B - 1)
            for out in (x1_out, aT_out, si_out):
                sp.wait_ge(out, 16 * (B + 1))

        @block.gpsimd
        def _(pool):
            make_identity(pool, ident, setup)
            pool.memset(minus_half[:, :], -0.5).then_inc(setup, 1)
            pool.memset(ones[:, :], 1.0).then_inc(setup, 1)
            pool.memset(valid[:, :], 0.0).then_inc(setup, 1)
            pool.memset(Kv[:, :, :], 0.0).then_inc(setup, 1)
            for n in range(2):
                pool.memset(cT[n][:, :, :].bitcast(F32), 0.0).then_inc(setup, 1)
                pool.memset(Kd[n][:, :, :].bitcast(F32), 0.0).then_inc(setup, 1)
                pool.memset(Vd[n][:, :, :].bitcast(F32), 0.0).then_inc(setup, 1)
            pool.wait_ge(setup, 12)

            def invert(i, ln):
                wait_apart(pool, dve_s.at(i, ln, "var"), passed)
                pool_s.due(pool, ln, "ve")
                pool.tensor_scalar(ve[:, :], mv[:, :, 1], EPS, None, ALU.add).then_inc(*pool_s.mark(ln, "ve"))
                pool.wait_ge(*pool_s.at(i, ln, "ve"))
                pool_s.due(pool, ln, "rstd")
                pool.tensor_tensor(rstd[:, :], ve[:, :], minus_half[:, :], ALU.pow).then_inc(*pool_s.mark(ln, "rstd"))

            pool_s.lead = True
            invert(-1, "ln1")
            pool_s.lead_up(pool)
            pool_s.lead = False
            with pool.Fori(0, B) as i:
                invert(i, "ln2")
                invert(i, "ln1")

        @block.tensor
        def _(pe):
            pe.wait_ge(small, 16 * len(smalls))
            pe.wait_ge(setup, 12)
            for c in range(C):
                m = pe.matmul(bank[0][:, c:c + 1], slots0[:, c * P:(c + 1) * P], ones[0:NS, 0:1], start=True, stop=True)
            m.then_inc(mean_ps, 1)
            pe.wait_ge(mean_sb, 1)
            for j in range(J):
                for c in range(C):
                    m = pe.matmul(bank[1][:, j:j + 1], w1s[:, c, j * P:(j + 1) * P], smean[:, c:c + 1],
                                  start=(c == 0), stop=(c == C - 1))
            m.then_inc(hb_ps, 1)
            w_cut(pe, for_lead)
            pe.wait_ge(consts, 3)
            pe.wait_ge(hb_ready, 1)

            def unit_of(i, *name):
                if not pe_s.lead:
                    take(pe, banks, (act_s, dve_s), i, name)
                pe_s.due(pe, *name)
                return banks[name]

            def project(out, w, m0, m1, x, n0, n1, chunks=C):
                for k in range(chunks):
                    last = product(pe, out, (w[0][:, k, m0:m1], w[1][:, k, m0:m1]),
                                   (x[0][:, k, n0:n1], x[1][:, k, n0:n1]), k == 0, k == chunks - 1)
                return last

            def context_transposed(i):
                ps = unit_of(i, "cT")
                pe.wait_ge(cx_in, i * 16 + 32)
                for c in range(C):
                    m = pe.transpose(ps[:, c * SK:(c + 1) * SK], cx[:, c * P:(c + 1) * P], ident[0:SK, 0:SK])
                m.then_inc(*pe_s.mark("cT"))

            def keys(i):
                ps = unit_of(i, "K")
                project(ps[0:SK, :], cT, 0, SK, Wk, 0, D).then_inc(*pe_s.mark("K"))

            def values(i):
                ps = unit_of(i, "V")
                pe.wait_ge(*dve_s.at(i, "read", "cT"))
                project(ps[0:SK, :], cT, 0, SK, Wv, 0, D).then_inc(*pe_s.mark("V"))

            def keys_transposed(i):
                ps = unit_of(i, "KT")
                pe.wait_ge(*act_s.at(i, "read", "K"))
                for c in range(C):
                    m = pe.transpose(ps[:, c * SKP:c * SKP + SK], K_rows[:, c * P:(c + 1) * P], ident[0:SK, 0:SK])
                m.then_inc(*pe_s.mark("KT"))

            pe_s.lead = True
            for part in (context_transposed, values, keys, keys_transposed):
                part(-1)
            pe_s.lead_up(pe)
            pe_s.lead = False
            w_cut(pe)
            with pe.Fori(0, B) as i:
                unit = lambda *name: unit_of(i, *name)

                def transposes(name, ln):
                    for c in range(C):
                        ps = unit(name, c)
                        for t in range(NT):
                            if c == 0:
                                pe.wait_ge(*dve_s.at(i, ln, "xn", t))
                            m = pe.transpose(ps[:, t * P:(t + 1) * P], xn[:, t, c * P:(c + 1) * P], ident[:, :])
                        m.then_inc(*pe_s.mark(name, c))

                transposes("xT", "ln1")
                def queries(c):
                    ps = unit("Q", c)
                    project(ps[:, :], Wq, c * P, (c + 1) * P, xT, 0, T).then_inc(*pe_s.mark("Q", c))

                def scores(c):
                    for t in range(NT):
                        ps = unit("S", t, c)
                        if t == 0:
                            pe.wait_ge(*dve_s.at(i, "read", "Q", c))
                        q = [z[:, c, t * P:(t + 1) * P] for z in qT]
                        out = ps[:, 0:HC * SKP]
                        product(pe, out, q, [z[:, c, :] for z in Kd], True, False)
                        pe.matmul(out, ones_r[:, :], mrow[:, :, :].rearrange("p h s -> p (h s)"),
                                  start=False, stop=True).then_inc(*pe_s.mark("S", t, c))

                def values_of(h):
                    c, n = divmod(h, HC)
                    ps = unit("O", c) if n == 0 else banks["O", c]
                    pe.wait_ge(*dve_s.at(i, "read", "PT", h))
                    product(pe, ps[:, :], [z[:, c, n * P:(n + 1) * P] for z in Vd], [z[:, :] for z in PT[h % 2]],
                            n == 0, n == HC - 1).then_inc(*pe_s.mark("PV", h))

                pe.wait_ge(*dve_s.at(i, "read", "xT", C - 1))
                queries(0)
                for c in range(C + 1):
                    if c < C:
                        if c == 0:
                            pe.wait_ge(*dve_s.before(i, "Kd"))
                        scores(c)
                    if c:
                        for h in groups[c - 1]:
                            ps = unit("PT", h)
                            for t in range(NT):
                                if h == groups[c - 1][0] and t == 0:
                                    pe.wait_ge(*dve_s.at(i, "probs", c - 1))
                                m = pe.transpose(ps[0:SK, t * P:(t + 1) * P], E[:, t, h, :], ident[:, :])
                            m.then_inc(*pe_s.mark("PT", h))
                            if h % HC:
                                values_of(h - 1)
                    if c + 1 < C:
                        queries(c + 1)
                    if c:
                        values_of(groups[c - 1][-1])
                context_transposed(i)
                for t in range(NT):
                    ps = unit("Wo", t)
                    pe.wait_ge(*dve_s.at(i, "read", "O", C - 1))
                    project(ps[:, :], oT, t * P, (t + 1) * P, Wo, 0, D).then_inc(*pe_s.mark("Wo", t))
                values(i)
                transposes("fT", "ln2")
                pe.wait_ge(*dve_s.at(i, "read", "fT", C - 1))
                for j in range(J):
                    ps = unit("h", j)
                    project(ps[:, :], W1, j * P, (j + 1) * P, xT, 0, T).then_inc(*pe_s.mark("h", j))
                keys(i)
                ps = unit("LT")
                pe.wait_ge(*dve_s.at(i, "hlo", J - 1))
                project(ps[0:NS, :], W2, 0, NS, hTs, 0, T, J).then_inc(*pe_s.mark("LT"))
                ps = unit("L")
                wait_apart(pe, act_s.at(i, "read", "LT"), passed)
                for t in range(NT):
                    m = pe.transpose(ps[:, t * NS:(t + 1) * NS], si[:, t * P:(t + 1) * P], ident[0:NS, 0:NS])
                m.then_inc(*pe_s.mark("L"))
                keys_transposed(i)
                ps = unit("aT")
                wait_apart(pe, dve_s.at(i, "alpha"), passed)
                for t in range(NT):
                    m = pe.transpose(ps[0:NS, t * P:(t + 1) * P], alpha[:, t, :], ident[:, :])
                m.then_inc(*pe_s.mark("aT"))
                ps, ps2 = unit("si"), unit("den")
                for t in range(NT):
                    pe.matmul(ps[0:NS, :], alpha[:, t, :], xn[:, t, :], start=(t == 0), stop=(t == NT - 1))
                    m = pe.matmul(ps2[0:NS, 0:1], alpha[:, t, :], ones[:, 0:1], start=(t == 0), stop=(t == NT - 1))
                m.then_inc(*pe_s.mark("si"))

        @block.scalar
        def _(act):
            w_scalar(act, 0, for_lead)
            act.wait_ge(tau_ready, 1)
            act.wait_ge(hb_ready, 1)

            def hi_of(i, step, out, src, func=ACT.Copy, **kw):
                act.wait_ge(*pe_s.at(i, *step))
                act_s.due(act, "hi", *step)
                return act.activation(out, src, func, **kw).then_inc(*act_s.mark("hi", *step))

            def context_hi(i):
                if not act_s.lead:
                    act.wait_ge(*pe_s.before(i, "K"))
                hi_of(i, ("cT",), cT[0][:, :, 0:SK], banks["cT",][:, 0:C * SK].rearrange("p (c s) -> p c s", c=C))

            def keys_out(i):
                act.wait_ge(*pe_s.at(i, "K"))
                act_s.due(act, "read", "K")
                act.activation(K_rows, banks["K",][0:SK, :], ACT.Copy).then_inc(*act_s.mark("read", "K"))

            def values_hi(i):
                hi_of(i, ("V",), vdiag(Vd[0], C, HC, P, HD, SK), banks["V",][0:SK, :].rearrange("p (c h d) -> p c h d", c=C, h=HC))

            def keys_hi(i):
                act.wait_ge(*dve_s.at(i, "Kv"))
                for n in range(HC):
                    q = slice(n * HD, (n + 1) * HD)
                    act_s.due(act, "Kd", n)
                    act.activation(Kd[0][q, :, n * SKP:(n + 1) * SKP], Kv[q, :, :], ACT.Copy)\
                       .then_inc(*act_s.mark("Kd", n))

            act_s.lead = True
            for n, part in enumerate((context_hi, values_hi, keys_out, keys_hi)):
                part(-1)
                w_scalar(act, for_lead + n, for_lead + n + 1)
            act_s.lead_up(act)
            act_s.lead = False
            with act.Fori(0, B) as i:
                hi = lambda *args, **kw: hi_of(i, *args, **kw)
                for c in range(C):
                    if c == 0:
                        act.wait_ge(*pe_s.before(i, "h", J - 1))
                    hi(("xT", c), xT[0][:, c, :], banks["xT", c][:, :])
                def queries_hi(c):
                    hi(("Q", c), qT[0][:, c, :], banks["Q", c][:, :], ACT.Identity, bias=bq[:, c:c + 1])

                def probabilities_hi(heads):
                    for h in heads:
                        if h >= 2:
                            act.wait_ge(*pe_s.at(i, "PV", h - 2))
                        hi(("PT", h), PT[h % 2][0][:, :], banks["PT", h][0:SK, :])

                queries_hi(0)
                for c in range(C + 1):
                    if c:
                        probabilities_hi(groups[c - 1][0:2])
                    if c < C:
                        hs = slice(c * HC, (c + 1) * HC)
                        act.wait_ge(*dve_s.at(i, "shifted", NT - 1, c))
                        act.activation(E[:, :, hs, :], E[:, :, hs, :], ACT.Exp, scale=SCALE).then_inc(*act_s.mark("exp", c))
                    if c:
                        probabilities_hi(groups[c - 1][2:])
                    if c + 1 < C:
                        queries_hi(c + 1)
                    if c:
                        act.wait_ge(*pe_s.at(i, "PV", groups[c - 1][-1]))
                        act.activation(oT[0][:, c - 1, :], banks["O", c - 1][:, :], ACT.Identity, bias=bv[:, c - 1:c])\
                           .then_inc(*act_s.mark("hi", "O", c - 1))
                context_hi(i)
                values_hi(i)
                for c in range(C):
                    if c == 0:
                        act.wait_ge(*pe_s.at(i, "Q", C - 1))
                    hi(("fT", c), xT[0][:, c, :], banks["fT", c][:, :])
                act.wait_ge(*dve_s.before(i, "hlo", J - 1))
                act.wait_ge(*pe_s.before(i, "L"))
                for j in range(J):
                    act.wait_ge(*pe_s.at(i, "h", j))
                    act.activation(hT[:, j, :], banks["h", j][:, :], ACT.Gelu, bias=hbias[:, j:j + 1])\
                       .then_inc(*act_s.mark("read", "h", j))
                for j in range(J):
                    act.wait_ge(*act_s.at(i, "read", "h", j))
                    act.activation(hTs[0][:, j, :], hT[:, j, :], ACT.Copy).then_inc(*act_s.mark("hhi", j))
                keys_out(i)
                act.wait_ge(*pe_s.at(i, "LT"))
                act.wait_ge(si_out, i * 16 + 16)
                act.activation(si[:, :], banks["LT",][0:NS, :], ACT.Copy).then_inc(*act_s.mark("read", "LT"))
                act.wait_ge(*dve_s.at(i, "lshift"))
                act.activation(el[:, :, :], el[:, :, :], ACT.Exp, scale=tau[:, 3:4]).then_inc(*act_s.mark("lexp"))
                keys_hi(i)

        @block.vector
        def _(dve):
            dve.wait_ge(small, 16 * len(smalls))
            dve.wait_ge(setup, 12)
            dve.tensor_copy(ones_r[:, :], ones[0:1, :]).then_inc(consts, 1)
            dve.tensor_scalar(tau[:, 1:2], tau[:, 0:1], -1.0, None, ALU.mult).then_inc(consts, 1)
            dve.wait_ge(consts, 2)
            dve.tensor_scalar(tau[:, 2:3], tau[:, 1:2], tau[:, 0:1], 0.1, ALU.max, ALU.add).then_inc(consts, 1)
            dve.wait_ge(consts, 3)
            dve.reciprocal(tau[:, 3:4], tau[:, 2:3]).then_inc(tau_ready, 1)
            dve.wait_ge(mean_ps, 1)
            dve.tensor_scalar(smean[:, :], bank[0][:, 0:C], 1.0 / NS, None, ALU.mult).then_inc(mean_sb, 1)
            dve.wait_ge(hb_ps, 1)
            dve.tensor_tensor(hbias[:, :], bank[1][:, 0:J], b1c[:, :], ALU.add).then_inc(hb_ready, 1)
            w_vector(dve, 0, for_lead)

            def moments(i, src, ln, t):
                dve_s.due(dve, ln, "stats", t)
                dve.bn_stats(stats[:, t, :], src[:, t, :]).then_inc(*dve_s.mark(ln, "stats", t))

            def aggregate(i, ln):
                wait_apart(dve, dve_s.at(i, ln, "stats", NT - 1), passed)
                dve_s.due(dve, ln, "var")
                for t in range(NT):
                    m = dve.bn_aggr(mv[:, t, :], stats[:, t, :])
                m.then_inc(*dve_s.mark(ln, "var"))

            def lo_of(i, name, out, ps, hi_ap, bias=None):
                dve.wait_ge(*act_s.at(i, "hi", *name))
                dve_s.due(dve, "read", *name)
                if bias is None:
                    m = dve.tensor_tensor(out, ps, f32(hi_ap), ALU.subtract)
                else:
                    m = dve.scalar_tensor_tensor(out, ps, bias, f32(hi_ap), ALU.add, ALU.subtract)
                return m.then_inc(*dve_s.mark("read", *name))

            def context_lo(i):
                lo_of(i, ("cT",), cT[1][:, :, 0:SK], banks["cT",][:, 0:C * SK].rearrange("p (c s) -> p c s", c=C), cT[0][:, :, 0:SK])
                dve.wait_ge(mask_in, i * 16 + 32)
                dve_s.due(dve, "valid")
                dve.tensor_scalar(valid[:, 0:SK], mask_i[:, :], 0.0, None, ALU.not_equal).then_inc(*dve_s.mark("valid"))
                dve.wait_ge(*dve_s.at(i, "valid"))
                dve_s.due(dve, "mrow")
                dve.tensor_scalar(mrow[:, :, :], valid[0:1, :].unsqueeze(1).to_broadcast([1, HC, SKP]), 1.0, MASKED,
                                  ALU.subtract, ALU.mult).then_inc(*dve_s.mark("mrow"))

            def x_moments(i):
                dve.wait_ge(x_in, i * 16 + 32)
                for t in range(NT):
                    moments(i, x, "ln1", t)
                aggregate(i, "ln1")

            def values_lo(i):
                lo_of(i, ("V",), vdiag(Vd[1], C, HC, P, HD, SK), banks["V",][0:SK, :].rearrange("p (c h d) -> p c h d", c=C, h=HC),
                      vdiag(Vd[0], C, HC, P, HD, SK))

            def keys_masked(i):
                dve.wait_ge(*pe_s.at(i, "KT"))
                for c in range(C):
                    name = ("Kv",) if c == C - 1 else ("Kv", c)
                    dve_s.due(dve, *name)
                    dve.scalar_tensor_tensor(Kv[:, c, 0:SK], banks["KT",][:, c * SKP:c * SKP + SK], bk[:, c:c + 1],
                                             valid[:, 0:SK], ALU.add, ALU.mult).then_inc(*dve_s.mark(*name))

            def keys_lo(i):
                dve.wait_ge(*dve_s.at(i, "Kv"))
                for n in range(HC):
                    q = slice(n * HD, (n + 1) * HD)
                    name = ("Kd",) if n == HC - 1 else ("Kd", n)
                    dve.wait_ge(*act_s.at(i, "Kd", n))
                    dve_s.due(dve, *name)
                    dve.tensor_tensor(Kd[1][q, :, n * SKP:(n + 1) * SKP], Kv[q, :, :],
                                      f32(Kd[0][q, :, n * SKP:(n + 1) * SKP]), ALU.subtract).then_inc(*dve_s.mark(*name))

            dve_s.lead = True
            for part, n in ((context_lo, 2), (values_lo, 3), (x_moments, 4), (keys_masked, None), (keys_lo, 5)):
                part(-1)
                if n is not None:
                    w_vector(dve, n, n + 1)
            dve_s.lead_up(dve)
            dve_s.lead = False
            w_cut(dve)
            with dve.Fori(0, B) as i:
                lo = lambda *args: lo_of(i, *args)

                def normalise(src, ln, step):
                    dve.wait_ge(*step)
                    for t in range(NT):
                        dve.tensor_scalar(xn[:, t, :], src[:, t, :], mv[:, t, 0:1], rstd[:, t:t + 1],
                                          ALU.subtract, ALU.mult).then_inc(*dve_s.mark(ln, "xn", t))

                dve.wait_ge(*pe_s.before(i, "si"))
                dve.wait_ge(*dve_s.before(i, "ln1", "var"))
                normalise(x, "ln1", pool_s.before(i, "ln1", "rstd"))
                for c in range(C):
                    lo(("xT", c), xT[1][:, c, :], banks["xT", c][:, :], xT[0][:, c, :])
                def queries_lo(c):
                    lo(("Q", c), qT[1][:, c, :], banks["Q", c][:, :], qT[0][:, c, :], bq[:, c:c + 1])

                def scores(t, c):
                    return banks["S", t, c][:, 0:HC * SKP].rearrange("p (h s) -> p h s", h=HC)[:, :, 0:SK], slice(c * HC, (c + 1) * HC)

                def shift(t, c):
                    s, hs = scores(t, c)
                    dve.wait_ge(*dve_s.at(i, "max", t, c))
                    dve.tensor_tensor(E[:, t, hs, :], s, mx[:, t, hs].unsqueeze(2).to_broadcast([P, HC, SK]),
                                      ALU.subtract).then_inc(*dve_s.mark("shifted", t, c))

                def softmax_end(c):
                    hs = slice(c * HC, (c + 1) * HC)
                    dve.wait_ge(*act_s.at(i, "exp", c))
                    dve.reduce_sum(rs[:, :, hs], E[:, :, hs, :], AX).then_inc(*dve_s.mark("sum", c))
                    dve.wait_ge(*dve_s.at(i, "sum", c))
                    dve.reciprocal(rs[:, :, hs], rs[:, :, hs]).then_inc(*dve_s.mark("rsum", c))
                    dve.wait_ge(*dve_s.at(i, "rsum", c))
                    dve.tensor_tensor(E[:, :, hs, :], E[:, :, hs, :], rs[:, :, hs].unsqueeze(3).to_broadcast([P, NT, HC, SK]),
                                      ALU.mult).then_inc(*dve_s.mark("probs", c))

                queries_lo(0)
                for c in range(C + 1):
                    if c < C:
                        for t in range(NT):
                            s, hs = scores(t, c)
                            dve.wait_ge(*pe_s.at(i, "S", t, c))
                            dve.reduce_max(mx[:, t, hs], s, AX).then_inc(*dve_s.mark("max", t, c))
                            if t:
                                shift(t - 1, c)
                        shift(NT - 1, c)
                    if c:
                        for h in groups[c - 1]:
                            lo(("PT", h), PT[h % 2][1][:, :], banks["PT", h][0:SK, :], PT[h % 2][0][:, :])
                    if c < C:
                        softmax_end(c)
                    if c + 1 < C:
                        queries_lo(c + 1)
                    if c:
                        lo(("O", c - 1), oT[1][:, c - 1, :], banks["O", c - 1][:, :], oT[0][:, c - 1, :], bv[:, c - 1:c])
                context_lo(i)
                dve.wait_ge(x1_out, i * 16 + 16)
                for t in range(NT):
                    dve.wait_ge(*pe_s.at(i, "Wo", t))
                    dve.tensor_tensor(x1[:, t, :], banks["Wo", t][:, :], x[:, t, :], ALU.add).then_inc(*dve_s.mark("read", "Wo", t))
                    dve.wait_ge(*dve_s.at(i, "read", "Wo", t))
                    dve.tensor_tensor(x1[:, t, :], x1[:, t, :], bo_bc[:, :], ALU.add).then_inc(*dve_s.mark("res", t))
                    if t:
                        dve.wait_ge(*dve_s.at(i, "res", t - 1))
                        moments(i, x1, "ln2", t - 1)
                dve.wait_ge(*dve_s.at(i, "res", NT - 1))
                moments(i, x1, "ln2", NT - 1)
                aggregate(i, "ln2")
                values_lo(i)
                dve.wait_ge(*dve_s.at(i, "ln2", "var"))
                dve.wait_ge(*pe_s.at(i, "xT", C - 1))
                normalise(x1, "ln2", pool_s.at(i, "ln2", "rstd"))
                for c in range(C):
                    lo(("fT", c), xT[1][:, c, :], banks["fT", c][:, :], xT[0][:, c, :])
                x_moments(i)
                for j in range(J):
                    dve.wait_ge(*act_s.at(i, "hhi", j))
                    dve.tensor_tensor(hTs[1][:, j, :], hT[:, j, :], f32(hTs[0][:, j, :]), ALU.subtract)\
                       .then_inc(*dve_s.mark("hlo", j))
                dve.wait_ge(*pe_s.at(i, "L"))
                dve.tensor_tensor(L[:, :, :], banks["L",][:, 0:NT * NS].rearrange("p (t s) -> p t s", t=NT),
                                  b2_bc[:, :].unsqueeze(1).to_broadcast([P, NT, NS]), ALU.add)\
                   .then_inc(*dve_s.mark("read", "L"))
                wait_apart(dve, dve_s.at(i, "read", "L"), passed)
                for t in range(NT):
                    dve.max(top[:, t, :], L[:, t, :]).then_inc(*dve_s.mark("top", t))
                wait_apart(dve, dve_s.at(i, "top", NT - 1), passed)
                for t in range(NT):
                    dve.match_replace(rest[:, t, :], top[:, t, :], L[:, t, :], -3e38).then_inc(*dve_s.mark("rest", t))
                dve.tensor_tensor(el[:, :, :], L[:, :, :], top[:, :, 0:1].to_broadcast([P, NT, NS]), ALU.subtract)\
                   .then_inc(*dve_s.mark("lshift"))
                dve.wait_ge(*dve_s.at(i, "rest", NT - 1))
                dve.tensor_tensor(rest[:, :, :], rest[:, :, :], L[:, :, :], ALU.not_equal).then_inc(*dve_s.mark("chosen"))
                dve.wait_ge(*dve_s.at(i, "chosen"))
                dve.wait_ge(*act_s.at(i, "lexp"))
                dve.tensor_tensor(el[:, :, :], el[:, :, :], rest[:, :, :], ALU.mult).then_inc(*dve_s.mark("kept"))
                dve.wait_ge(*dve_s.at(i, "kept"))
                dve.reduce_sum(asum[:, :], el[:, :, :], AX).then_inc(*dve_s.mark("asum"))
                dve.wait_ge(*dve_s.at(i, "asum"))
                dve.reciprocal(asum[:, :], asum[:, :]).then_inc(*dve_s.mark("rasum"))
                dve.wait_ge(*dve_s.at(i, "rasum"))
                dve.wait_ge(*pe_s.before(i, "si"))
                dve.tensor_tensor(alpha[:, :, :], el[:, :, :], asum[:, :].unsqueeze(2).to_broadcast([P, NT, NS]), ALU.mult)\
                   .then_inc(*dve_s.mark("alpha"))
                keys_masked(i)
                keys_lo(i)
                dve.wait_ge(*pe_s.at(i, "aT"))
                dve.wait_ge(aT_out, i * 16 + 16)
                dve.tensor_copy(aT[:, :], banks["aT",][0:NS, :]).then_inc(*dve_s.mark("aT"))
                dve.wait_ge(*pe_s.at(i, "si"))
                dve.tensor_scalar(den[:, :], banks["den",][0:NS, 0:1], 1e-8, None, ALU.add).then_inc(*dve_s.mark("read", "den"))
                dve.wait_ge(*dve_s.at(i, "read", "den"))
                dve.reciprocal(den[:, :], den[:, :]).then_inc(*dve_s.mark("rden"))
                dve.wait_ge(*dve_s.at(i, "rden"))
                dve.wait_ge(si_out, i * 16 + 16)
                dve.tensor_scalar(si[:, :], banks["si",][0:NS, :], den[:, :], None, ALU.mult).then_inc(*dve_s.mark("si"))


def vdiag(tile, C, HC, p, hd, sk):
    return tile[0:sk, :, :].rearrange("k c (h w) -> k c h w", h=HC)[:, :, :, 0:hd]



def build_slots(nc, orders, a, si_s, vo_s):
    B = si_s.shape[0]
    NS, D = a["L0_ffn_slot_init"].shape
    DQ = a["L0_ffn_wq"].shape[1]
    C = D // P
    BS = B * NS
    NP = BS // P
    SCALE = float(DQ) ** -0.5

    with ExitStack() as ctx:
        st = Stage(nc, ctx, "sl", orders)
        sb, sem = st.sb, st.sem
        ident = sb("ident", [P, P])
        minus_half = sb("minus_half", [P, NP])
        WihT = sb("WihT", [P, C, 3 * D])
        WhhT = sb("WhhT", [P, C, 3 * D])
        wq, wk = sb("wq", [P, C, DQ]), sb("wk", [P, C, DQ])
        wv, wvp, wo = (sb(n, [P, C, D]) for n in ("wv", "wvp", "wo"))
        S0T = sb("S0T", [P, C, NS])
        bih, bhh = sb("bih", [P, 3 * C]), sb("bhh", [P, 3 * C])
        bq, bk, bvp = sb("bq", [P, 1]), sb("bk", [P, 1]), sb("bvp", [P, C])
        bv_bc, g_bc, b_bc = (sb(n, [P, D]) for n in ("bv_bc", "g_bc", "b_bc"))
        si = sb("si", [P, NP, D])
        siT = sb("siT", [P, C, BS])
        gh = sb("gh", [P, 3 * C, NS])
        gate = [sb(f"gate{n}", [P, BS]) for n in range(3)]
        SnT = sb("SnT", [P, C, BS])
        qT, kT = sb("qT", [P, BS]), sb("kT", [P, BS])
        v = si
        A = sb("A", [P, NP, P])
        AT = sb("AT", [P, NP, P])
        amx, asum = sb("amx", [P, NP]), sb("asum", [P, NP])
        y = sb("y", [P, NP, D])
        stats, mv = sb("stats", [P, NP, 6]), sb("mv", [P, NP, 2])
        rstd = sb("rstd", [P, NP])
        yT = siT
        svT = SnT
        vo = y

        bank = [st.ps(f"bank{n}", [P, 512]) for n in range(8)]
        setup, small, si_in, out = sem("setup"), sem("small"), sem("si_in"), sem("out")
        w_in = {n: sem(n + "_in") for n in ("WihT", "WhhT", "wqk", "wv", "wvp", "wo")}
        pe_s, act_s, dve_s, pool_s = (st.steps(n) for n in ("products", "act", "dve", "rstd"))
        rows = lambda w: w.rearrange("(c p) n -> p c n", p=P)

        units = [("siT", c) for c in range(C)] + [("gh", n) for n in range(3)]
        units += [("gi", c, n) for c in range(C) for n in range(3)]
        units += [("q",), ("k",)] + [("v", j) for j in range(NP)]
        for j in range(NP):
            units += [("A", j), ("AT", j), ("y", j)]
        units += [("yT", c) for c in range(C)] + [("sv", c) for c in range(C)] + [("vo", j) for j in range(NP)]
        banks = Banks(bank, units)
        dve_s.alias(("read", "q"), ("q",))
        dve_s.alias(("read", "k"), ("k",))
        for j in range(NP):
            dve_s.alias(("read", "v", j), ("v", j))
            dve_s.alias(("read", "y", j), ("y+bv", j))
            dve_s.alias(("read", "AT", j), ("AT", j))
            dve_s.alias(("read", "vo", j), ("vo", j))
            act_s.alias(("read", "A", j), ("A", j, 1))
        for c in range(C):
            dve_s.alias(("read", "siT", c), ("siT", c))
            dve_s.alias(("read", "gi", c, 0), ("r in", c))
            dve_s.alias(("read", "gi", c, 1), ("z in", c))
            dve_s.alias(("read", "gi", c, 2), ("n in", c))
            dve_s.alias(("read", "yT", c), ("yT", c))
            dve_s.alias(("read", "sv", c), ("sv", c))
        for n in range(3):
            dve_s.alias(("read", "gh", n), ("gh", n, C - 1))

        block = ctx.enter_context(nc.Block())

        smalls = [(S0T[:, :, :], rows(a["slot_init_T"])), (bih[:, :], a["L0_ffn_bih"]), (bhh[:, :], a["L0_ffn_bhh"]),
                  (bq[:, :], a["L0_ffn_bq"]), (bk[:, :], a["L0_ffn_bk"]), (bvp[:, :], a["L0_ffn_bvp"]),
                  (bv_bc[:, :], a["L0_ffn_bv"].partition_broadcast(P)),
                  (g_bc[:, :], a["L0_ffn_ln_g"].partition_broadcast(P)),
                  (b_bc[:, :], a["L0_ffn_ln_b"].partition_broadcast(P))]

        @block.sync
        def _(sp):
            sp.dma_start(si[:, :, :], si_s.rearrange("(j b) s d -> (b s) j d", j=NP)).then_inc(si_in, 16)
            sp.dma_start(WhhT[:, :, :], rows(a["Whh_T"])).then_inc(w_in["WhhT"], 16)
            sp.dma_start(WihT[:, :, :], rows(a["Wih_T"])).then_inc(w_in["WihT"], 16)
            sp.dma_start(wq[:, :, :], rows(a["L0_ffn_wq"])).then_inc(w_in["wqk"], 16)
            sp.dma_start(wk[:, :, :], rows(a["L0_ffn_wk"])).then_inc(w_in["wqk"], 16)
            for n, t in (("wv", wv), ("wvp", wvp), ("wo", wo)):
                sp.dma_start(t[:, :, :], rows(a["L0_ffn_" + n])).then_inc(w_in[n], 16)
            for j in range(NP):
                sp.wait_ge(*dve_s.at(0, "vo", j))
                sp.dma_start(vo_s[2 * j:2 * j + 2].rearrange("b s d -> (b s) d"), vo[:, j, :]).then_inc(out, 16)
            sp.wait_ge(out, 16 * NP)

        @block.gpsimd
        def _(pool):
            pool.sem_inc(pool_s.sem, pool_s.per)
            make_identity(pool, ident, setup)
            pool.memset(minus_half[:, :], -0.5).then_inc(setup, 1)
            pool.memset(A[:, :, :], 0.0).then_inc(setup, 1)
            pool.wait_ge(*dve_s.at(0, "var"))
            pool.tensor_scalar(rstd[:, :], mv[:, :, 1], EPS, None, ALU.add).then_inc(*pool_s.mark("ve"))
            pool.wait_ge(*pool_s.at(0, "ve"))
            pool.tensor_tensor(rstd[:, :], rstd[:, :], minus_half[:, :], ALU.pow).then_inc(*pool_s.mark("rstd"))

        @block.tensor
        def _(pe):
            pe.sem_inc(pe_s.sem, pe_s.per)
            pe.wait_ge(setup, 4)
            pe.wait_ge(si_in, 16)

            def unit(*name):
                if banks.user_before(name)[1] is False:
                    take(pe, banks, (act_s, dve_s), 0, name)
                return banks[name]

            def matmuls(out, w, m0, m1, x, n0, n1):
                for k in range(C):
                    last = pe.matmul(out, w[:, k, m0:m1], x[:, k, n0:n1], start=(k == 0), stop=(k == C - 1))
                return last

            for c in range(C):
                ps = unit("siT", c)
                for j in range(NP):
                    m = pe.transpose(ps[:, j * P:(j + 1) * P], si[:, j, c * P:(c + 1) * P], ident[:, :])
                m.then_inc(*pe_s.mark("siT", c))
            pe.wait_ge(small, 16 * len(smalls))
            pe.wait_ge(w_in["WhhT"], 16)
            for n in range(3):
                ps = unit("gh", n)
                for c in range(C):
                    m = matmuls(ps[:, c * NS:(c + 1) * NS], WhhT, n * D + c * P, n * D + (c + 1) * P, S0T, 0, NS)
                m.then_inc(*pe_s.mark("gh", n))
            pe.wait_ge(w_in["WihT"], 16)
            pe.wait_ge(*dve_s.at(0, "siT", C - 1))
            for c in range(C):
                for n in range(3):
                    ps = unit("gi", c, n)
                    matmuls(ps[:, :], WihT, n * D + c * P, n * D + (c + 1) * P, siT, 0, BS).then_inc(*pe_s.mark("gi", c, n))
            pe.wait_ge(w_in["wqk"], 32)
            pe.wait_ge(*dve_s.at(0, "S", C - 1))
            for name, w in (("q", wq), ("k", wk)):
                ps = unit(name)
                matmuls(ps[:, :], w, 0, DQ, SnT, 0, BS).then_inc(*pe_s.mark(name))
            pe.wait_ge(w_in["wv"], 16)
            for j in range(NP):
                ps = unit("v", j)
                matmuls(ps[:, :], SnT, j * P, (j + 1) * P, wv, 0, D).then_inc(*pe_s.mark("v", j))
            for j in range(NP):
                ps = unit("A", j)
                pe.wait_ge(*dve_s.at(0, "k"))
                pe.matmul(ps[:, 0:P], qT[:, j * P:(j + 1) * P], kT[:, j * P:(j + 1) * P], start=True, stop=True)\
                  .then_inc(*pe_s.mark("A", j))
                ps = unit("AT", j)
                pe.wait_ge(*dve_s.at(0, "A", j))
                pe.transpose(ps[:, 0:P], A[:, j, :], ident[:, :]).then_inc(*pe_s.mark("AT", j))
                ps = unit("y", j)
                pe.wait_ge(*dve_s.at(0, "AT", j))
                for c in range(C):
                    cols = slice(c * P, (c + 1) * P)
                    pe.matmul(ps[:, cols], AT[:, j, :], v[:, j, cols], start=True, stop=False)
                    m = pe.matmul(ps[:, cols], SnT[:, c, j * P:(j + 1) * P], ident[:, :], start=False, stop=True)
                m.then_inc(*pe_s.mark("y", j))
            for c in range(C):
                ps = unit("yT", c)
                for j in range(NP):
                    pe.wait_ge(*dve_s.at(0, "yn", j))
                    m = pe.transpose(ps[:, j * P:(j + 1) * P], y[:, j, c * P:(c + 1) * P], ident[:, :])
                m.then_inc(*pe_s.mark("yT", c))
            pe.wait_ge(w_in["wvp"], 16)
            pe.wait_ge(*dve_s.at(0, "yT", C - 1))
            for c in range(C):
                ps = unit("sv", c)
                matmuls(ps[:, :], wvp, c * P, (c + 1) * P, yT, 0, BS).then_inc(*pe_s.mark("sv", c))
            pe.wait_ge(w_in["wo"], 16)
            pe.wait_ge(*dve_s.at(0, "sv", C - 1))
            for j in range(NP):
                ps = unit("vo", j)
                matmuls(ps[:, :], svT, j * P, (j + 1) * P, wo, 0, D).then_inc(*pe_s.mark("vo", j))

        @block.scalar
        def _(act):
            act.sem_inc(act_s.sem, act_s.per)
            for dst, src in smalls:
                act.dma_start(dst, src).then_inc(small, 16)
            act.wait_ge(small, 16 * len(smalls))
            for c in range(C):
                for n, (name, func) in enumerate((("r", ACT.Sigmoid), ("z", ACT.Sigmoid), ("n", ACT.Tanh))):
                    act.wait_ge(*dve_s.at(0, name + " in", c))
                    if name == "n":
                        act.wait_ge(*dve_s.at(0, "r*h", c))
                        act.activation(gate[n][:, :], gate[n][:, :], func, bias=bih[:, 2 * C + c:2 * C + c + 1])\
                           .then_inc(*act_s.mark(name, c))
                    else:
                        act.activation(gate[n][:, :], gate[n][:, :], func).then_inc(*act_s.mark(name, c))
            for j in range(NP):
                act.wait_ge(*dve_s.at(0, "amx", j))
                for b in range(2):
                    s = slice(b * NS, (b + 1) * NS)
                    act.activation(A[s, j, s], banks["A", j][s, s], ACT.Exp, scale=SCALE, bias=amx[s, j:j + 1],
                                   accum_out=asum[s, j:j + 1]).then_inc(*act_s.mark("A", j, b))

        @block.vector
        def _(dve):
            dve.sem_inc(dve_s.sem, dve_s.per)
            dve.wait_ge(setup, 4)
            dve.wait_ge(small, 16 * len(smalls))

            def copy(name, dst, *bias):
                dve.wait_ge(*pe_s.at(0, *name))
                if bias:
                    m = dve.tensor_scalar(dst, banks[name][:, :], bias[0], None, ALU.add)
                else:
                    m = dve.tensor_copy(dst, banks[name][:, 0:dst.shape[-1]])
                return m.then_inc(*dve_s.mark(*name))

            for c in range(C):
                copy(("siT", c), siT[:, c, :])
            dve.tensor_tensor(bhh[:, 0:2 * C], bhh[:, 0:2 * C], bih[:, 0:2 * C], ALU.add).then_inc(*dve_s.mark("b"))
            dve.wait_ge(*dve_s.at(0, "b"))
            for n in range(3):
                dve.wait_ge(*pe_s.at(0, "gh", n))
                for c in range(C):
                    g = n * C + c
                    dve.tensor_scalar(gh[:, g, :], banks["gh", n][:, c * NS:(c + 1) * NS], bhh[:, g:g + 1], None, ALU.add)\
                       .then_inc(*dve_s.mark("gh", n, c))
            dve.wait_ge(*dve_s.at(0, "gh", 2, C - 1))
            by_batch = lambda t: t.rearrange("p (b s) -> p b s", b=B)
            same = lambda t: t.unsqueeze(1).to_broadcast([P, B, NS])
            for c in range(C):
                r, z, n = (by_batch(g[:, :]) for g in gate)
                gi = [by_batch(banks["gi", c, m][:, :]) for m in range(3)]
                if c:
                    dve.wait_ge(*dve_s.at(0, "S", c - 1))
                dve.wait_ge(*pe_s.at(0, "gi", c, 0))
                dve.tensor_tensor(r, gi[0], same(gh[:, c, :]), ALU.add).then_inc(*dve_s.mark("r in", c))
                dve.wait_ge(*pe_s.at(0, "gi", c, 1))
                dve.tensor_tensor(z, gi[1], same(gh[:, C + c, :]), ALU.add).then_inc(*dve_s.mark("z in", c))
                dve.wait_ge(*act_s.at(0, "r", c))
                dve.tensor_tensor(r, r, same(gh[:, 2 * C + c, :]), ALU.mult).then_inc(*dve_s.mark("r*h", c))
                dve.wait_ge(*dve_s.at(0, "r*h", c))
                dve.wait_ge(*pe_s.at(0, "gi", c, 2))
                dve.tensor_tensor(n, gi[2], r, ALU.add).then_inc(*dve_s.mark("n in", c))
                dve.wait_ge(*act_s.at(0, "n", c))
                dve.tensor_tensor(r, same(S0T[:, c, :]), n, ALU.subtract).then_inc(*dve_s.mark("S0-n", c))
                dve.wait_ge(*dve_s.at(0, "S0-n", c))
                dve.tensor_tensor(r, r, z, ALU.mult).then_inc(*dve_s.mark("z*", c))
                dve.wait_ge(*dve_s.at(0, "z*", c))
                dve.tensor_tensor(by_batch(SnT[:, c, :]), r, n, ALU.add).then_inc(*dve_s.mark("S", c))
            copy(("q",), qT[:, :], bq[:, 0:1])
            copy(("k",), kT[:, :], bk[:, 0:1])
            for j in range(NP):
                copy(("v", j), v[:, j, :])
            for j in range(NP):
                dve.wait_ge(*pe_s.at(0, "A", j))
                for b in range(2):
                    s = slice(b * NS, (b + 1) * NS)
                    m = dve.reduce_max(amx[s, j:j + 1], banks["A", j][s, s], AX)
                m.then_inc(*dve_s.mark("max", j))
                dve.wait_ge(*dve_s.at(0, "max", j))
                dve.tensor_scalar(amx[:, j:j + 1], amx[:, j:j + 1], -SCALE, None, ALU.mult).then_inc(*dve_s.mark("amx", j))
                dve.wait_ge(*act_s.at(0, "A", j, 1))
                dve.reciprocal(asum[:, j:j + 1], asum[:, j:j + 1]).then_inc(*dve_s.mark("rsum", j))
                dve.wait_ge(*dve_s.at(0, "rsum", j))
                dve.tensor_scalar(A[:, j, :], A[:, j, :], asum[:, j:j + 1], None, ALU.mult).then_inc(*dve_s.mark("A", j))
                copy(("AT", j), AT[:, j, :])
                dve.wait_ge(*pe_s.at(0, "y", j))
                dve.tensor_tensor(y[:, j, :], banks["y", j][:, :], bv_bc[:, :], ALU.add).then_inc(*dve_s.mark("y+bv", j))
                dve.wait_ge(*dve_s.at(0, "y+bv", j))
                dve.bn_stats(stats[:, j, :], y[:, j, :]).then_inc(*dve_s.mark("stats", j))
                dve.wait_ge(*dve_s.at(0, "stats", j))
                m = dve.bn_aggr(mv[:, j, :], stats[:, j, :])
            m.then_inc(*dve_s.mark("var"))
            dve.wait_ge(*dve_s.at(0, "var"))
            dve.wait_ge(*pool_s.at(0, "rstd"))
            for j in range(NP):
                dve.tensor_scalar(y[:, j, :], y[:, j, :], mv[:, j, 0:1], rstd[:, j:j + 1], ALU.subtract, ALU.mult)\
                   .then_inc(*dve_s.mark("normed", j))
                dve.wait_ge(*dve_s.at(0, "normed", j))
                dve.tensor_tensor(y[:, j, :], y[:, j, :], g_bc[:, :], ALU.mult).then_inc(*dve_s.mark("*g", j))
                dve.wait_ge(*dve_s.at(0, "*g", j))
                dve.tensor_tensor(y[:, j, :], y[:, j, :], b_bc[:, :], ALU.add).then_inc(*dve_s.mark("yn", j))
            for c in range(C):
                copy(("yT", c), yT[:, c, :])
            for c in range(C):
                copy(("sv", c), svT[:, c, :], bvp[:, c:c + 1])
            for j in range(NP):
                copy(("vo", j), vo[:, j, :])



def build_latents(nc, orders, a, x1_s, alphaT_s, vo_s, x2_s, z_s):
    B, T, D = x1_s.shape
    SK = a["ctx_1024"].shape[1]
    Z = z_s[0].shape[3]
    C, NT = D // P, T // P
    NS = vo_s.shape[1]
    NL = NT + 1

    with ExitStack() as ctx:
        st = Stage(nc, ctx, "la", orders)
        sb, sem = st.sb, st.sem
        two = lambda name, shape, dt=F32: [sb(f"{name}{n}", shape, dt) for n in range(2)]
        ident = sb("ident", [P, P])
        minus_half = sb("minus_half", [P, NL])
        ones = sb("ones", [1, P])
        bo = sb("bo", [1, D])
        gain = {n: (sb(n + "g", [P, C]), sb(n + "b", [P, C])) for n in ("x", "l")}
        x1, x2 = two("x1", [P, NT, D]), two("x2", [P, NT, D])
        aT, vo, cx = two("aT", [NS, T]), two("vo", [NS, D]), two("cx", [SK, D])
        stats, mv = two("stats", [P, NL, 6]), two("mv", [P, NL, 2])
        ve, rstd = two("ve", [P, NL]), two("rstd", [P, NL])
        xn, cn = two("xn", [P, NT, D]), two("cn", [SK, D])
        full = two("full", [P, C, Z])
        z_hi, z_lo = two("z_hi", [P, C, Z], F32R), two("z_lo", [P, C, Z], F32R)
        bank = [st.ps(f"bank{n}", [P, 512]) for n in range(8)]

        setup, small = sem("setup"), sem("small")
        passed = sem("passed")
        ins = [{n: sem(f"{n}_in{m}") for n in ("x1", "aT", "vo", "cx")} for m in range(2)]
        x2_out, z_out = [sem(f"x2_out{m}") for m in range(2)], [sem(f"z_out{m}") for m in range(2)]
        pe_s, act_s, dve_s, pool_s = (st.steps(n) for n in ("products", "act", "dve", "rstd"))

        units = []
        for m in range(2):
            units += [("x2", m, t) for t in range(NT)] + [("zT", m, c) for c in range(C)] + [("cT", m)]
        banks = Banks(bank, units)
        for m in range(2):
            for t in range(NT):
                dve_s.alias(("read", "x2", m, t), ("x2", m, t))
            for c in range(C):
                act_s.alias(("read", "zT", m, c), ("full", m, c))
            act_s.alias(("read", "cT", m), ("full", m, C, C - 1))

        smalls = [(bo[:, :], a["L0_ffn_bo"].rearrange("(o n) -> o n", o=1))]
        for n in gain:
            smalls += [(gain[n][0][:, :], a[f"L1_xattn_ln_{n}_g"]), (gain[n][1][:, :], a[f"L1_xattn_ln_{n}_b"])]
        PAIRS = B // 2
        block = ctx.enter_context(nc.Block())

        @block.sync
        def _(sp):
            for dst, src in smalls:
                sp.dma_start(dst, src).then_inc(small, 16)
            with sp.Fori(0, PAIRS) as i:
                for m in range(2):
                    one = lambda ap: ap[bass.ds(2 * i + m, 1)]
                    sp.wait_ge(*dve_s.before(i, "x2", m, NT - 1))
                    sp.dma_start(x1[m][:, :, :], one(x1_s).rearrange("b (t p) d -> p (b t) d", p=P)).then_inc(ins[m]["x1"], 16)
                    sp.dma_start(aT[m][:, :], one(alphaT_s).rearrange("b s t -> (b s) t")).then_inc(ins[m]["aT"], 16)
                    sp.dma_start(vo[m][:, :], one(vo_s).rearrange("b s d -> (b s) d")).then_inc(ins[m]["vo"], 16)
                    sp.wait_ge(*dve_s.before(i, "cn", m))
                    sp.dma_start(cx[m][:, :], one(a["ctx_1024"]).rearrange("b s d -> (b s) d")).then_inc(ins[m]["cx"], 16)

        @block.gpsimd
        def _(pool):
            pool.sem_inc(pool_s.sem, pool_s.per)
            make_identity(pool, ident, setup)
            pool.memset(minus_half[:, :], -0.5).then_inc(setup, 1)
            pool.memset(ones[:, :], 1.0).then_inc(setup, 1)
            for m in range(2):
                pool.memset(mv[m][:, :, :], 1.0).then_inc(setup, 1)
                pool.memset(full[m][:, :, :], 0.0).then_inc(setup, 1)
            with pool.Fori(0, PAIRS) as i:
                for m in range(2):
                    wait_apart(pool, dve_s.at(i, "var", m), passed)
                    pool.tensor_scalar(ve[m][:, 0:NT], mv[m][:, 0:NT, 1], 1.0 + EPS, EPS * EPS, ALU.mult, ALU.add)\
                        .then_inc(*pool_s.mark("ve", m))
                    pool.tensor_scalar(ve[m][:, NT:NL], mv[m][:, NT:NL, 1], EPS, None, ALU.add).then_inc(*pool_s.mark("vc", m))
                    pool.wait_ge(*pool_s.at(i, "vc", m))
                    pool.tensor_tensor(rstd[m][:, :], ve[m][:, :], minus_half[:, :], ALU.pow).then_inc(*pool_s.mark("rstd", m))

        @block.tensor
        def _(pe):
            pe.sem_inc(pe_s.sem, pe_s.per)
            pe.wait_ge(setup, 8)
            pe.wait_ge(small, 16 * len(smalls))
            with pe.Fori(0, PAIRS) as i:
                def unit(*name):
                    take(pe, banks, (act_s, dve_s), i, name)
                    return banks[name]

                for m in range(2):
                    pe.wait_ge(ins[m]["aT"], i * 16 + 16)
                    pe.wait_ge(ins[m]["vo"], i * 16 + 16)
                    for t in range(NT):
                        ps = unit("x2", m, t)
                        pe.matmul(ps[:, :], ones[:, :], bo[:, :], start=True, stop=False)
                        pe.matmul(ps[:, :], aT[m][:, t * P:(t + 1) * P], vo[m][:, :], start=False, stop=True)\
                          .then_inc(*pe_s.mark("x2", m, t))
                    for c in range(C):
                        ps = unit("zT", m, c)
                        for t in range(NT):
                            if c == 0:
                                pe.wait_ge(*dve_s.at(i, "xn", m, t))
                            tr = pe.transpose(ps[:, t * P:(t + 1) * P], xn[m][:, t, c * P:(c + 1) * P], ident[:, :])
                        tr.then_inc(*pe_s.mark("zT", m, c))
                    ps = unit("cT", m)
                    pe.wait_ge(*dve_s.at(i, "cn", m))
                    for c in range(C):
                        tr = pe.transpose(ps[:, c * SK:(c + 1) * SK], cn[m][:, c * P:(c + 1) * P], ident[0:SK, 0:SK])
                    tr.then_inc(*pe_s.mark("cT", m))

        @block.scalar
        def _(act):
            act.sem_inc(act_s.sem, act_s.per)
            for m in range(2):
                act.sem_inc(x2_out[m], 16)
                act.sem_inc(z_out[m], 32)
            act.wait_ge(small, 16 * len(smalls))
            act.wait_ge(setup, 8)
            with act.Fori(0, PAIRS) as i:
                for m in range(2):
                    act.wait_ge(*dve_s.before(i, "lo", m, C - 1))
                    act.wait_ge(z_out[m], i * 32 + 32)
                    for c in range(C):
                        act.wait_ge(*pe_s.at(i, "zT", m, c))
                        act.activation(full[m][:, c, 0:T], banks["zT", m, c][:, :], ACT.Identity,
                                       scale=gain["l"][0][:, c:c + 1], bias=gain["l"][1][:, c:c + 1])\
                           .then_inc(*act_s.mark("full", m, c))
                    act.wait_ge(*pe_s.at(i, "cT", m))
                    for c in range(C):
                        act.activation(full[m][:, c, T:T + SK], banks["cT", m][:, c * SK:(c + 1) * SK], ACT.Identity,
                                       scale=gain["x"][0][:, c:c + 1], bias=gain["x"][1][:, c:c + 1])\
                           .then_inc(*act_s.mark("full", m, C, c))
                    for c in range(C):
                        act.wait_ge(*act_s.at(i, "full", m, C, C - 1))
                        act.activation(z_hi[m][:, c, :], full[m][:, c, :], ACT.Copy).then_inc(*act_s.mark("hi", m, c))
                    act.wait_ge(*dve_s.at(i, "x2", m, NT - 1))
                    act.dma_start(x2_s[bass.ds(2 * i + m, 1)].rearrange("b (t p) d -> p (b t) d", p=P), x2[m][:, :, :])\
                       .then_inc(x2_out[m], 16)
                    act.wait_ge(*dve_s.at(i, "lo", m, C - 1))
                    act.dma_start(z_s[0][bass.ds(2 * i + m, 1)].rearrange("b p c z -> p (b c) z"), f32(z_hi[m][:, :, :])).then_inc(z_out[m], 16)
                    act.dma_start(z_s[1][bass.ds(2 * i + m, 1)].rearrange("b p c z -> p (b c) z"), f32(z_lo[m][:, :, :])).then_inc(z_out[m], 16)
            for m in range(2):
                act.wait_ge(x2_out[m], 16 * (PAIRS + 1))
                act.wait_ge(z_out[m], 32 * (PAIRS + 1))

        @block.vector
        def _(dve):
            dve.sem_inc(dve_s.sem, dve_s.per)
            dve.wait_ge(setup, 8)
            with dve.Fori(0, PAIRS) as i:
                for m in range(2):
                    dve.wait_ge(ins[m]["x1"], i * 16 + 16)
                    dve.wait_ge(x2_out[m], i * 16 + 16)
                    for t in range(NT):
                        dve.wait_ge(*pe_s.at(i, "x2", m, t))
                        dve.tensor_tensor(x2[m][:, t, :], banks["x2", m, t][:, :], x1[m][:, t, :], ALU.add)\
                           .then_inc(*dve_s.mark("x2", m, t))
                        dve.wait_ge(*dve_s.at(i, "x2", m, t))
                        dve.bn_stats(stats[m][:, t, :], x2[m][:, t, :]).then_inc(*dve_s.mark("stats", m, t))
                    dve.wait_ge(ins[m]["cx"], i * 16 + 16)
                    dve.bn_stats(stats[m][0:SK, NT, :], cx[m][:, :]).then_inc(*dve_s.mark("stats", m, NT))
                    wait_apart(dve, dve_s.at(i, "stats", m, NT), passed)
                    for t in range(NL):
                        rows = slice(0, SK if t == NT else P)
                        last = dve.bn_aggr(mv[m][rows, t, :], stats[m][rows, t, :])
                    last.then_inc(*dve_s.mark("var", m))
                    dve.wait_ge(*dve_s.at(i, "var", m))
                    dve.wait_ge(*pool_s.at(i, "rstd", m))
                    dve.wait_ge(*pe_s.before(i, "cT", m))
                    for t in range(NT):
                        dve.tensor_scalar(xn[m][:, t, :], x2[m][:, t, :], mv[m][:, t, 0:1], rstd[m][:, t:t + 1],
                                          ALU.subtract, ALU.mult).then_inc(*dve_s.mark("xn", m, t))
                    dve.tensor_scalar(cn[m][:, :], cx[m][:, :], mv[m][0:SK, NT, 0:1], rstd[m][0:SK, NT:NL],
                                      ALU.subtract, ALU.mult).then_inc(*dve_s.mark("cn", m))
                    for c in range(C):
                        dve.wait_ge(*act_s.at(i, "hi", m, c))
                        dve.tensor_tensor(z_lo[m][:, c, :], full[m][:, c, :], f32(z_hi[m][:, c, :]), ALU.subtract)\
                           .then_inc(*dve_s.mark("lo", m, c))



class Claims:

    def __init__(self, name, orders):
        self.known, self.order = orders.get(name), []
        orders[name] = self.order

    def before(self, bank, unit):
        self.order.append((bank, unit))
        if not self.known:
            return unit, True
        n = len(self.order) - 1
        earlier = [u for b, u in self.known[:n] if b == bank]
        if earlier:
            return earlier[-1], False
        return [u for b, u in self.known if b == bank][-1], True


def build_perceiver(nc, orders, a, z_s, o_s):
    B = z_s[0].shape[0]
    C, Z = z_s[0].shape[2], z_s[0].shape[3]
    INNER = a["L1_xattn_Wq"].shape[1]
    SK = a["ctx_1024"].shape[1]
    T = a["x"].shape[1]
    SKP = Z - T
    NK = T + SK
    NT = T // P
    HD, H = 64, INNER // 64
    NPAIR = H // 2
    NC = NT + 1
    QH = 4
    SCALE = HD ** -0.5
    MASKED = 2.0 ** 126
    KEYS = [P] * NT + [SK]

    with ExitStack() as ctx:
        st = Stage(nc, ctx, "pa", orders)
        sb, sem = st.sb, st.sem
        two = lambda name, shape, dt=F32: [sb(f"{name}{n}", shape, dt) for n in range(2)]
        pair = lambda name, shape: (sb(name + "_hi", shape, F32R), sb(name + "_lo", shape, F32R))
        ident = sb("ident", [P, P])
        one_row = sb("one_row", [1, P])
        ones = sb("ones", [1, P], F32R)
        mask_words = sb("mask_words", [1, B * SK // 4], I32)
        mask_u = mask_words[:, :].bitcast(mybir.dt.uint8)
        mrow = sb("mrow", [1, B, SKP], F32R)
        z = pair("z", [P, C, Z])
        Wq = pair("Wq", [P, C, INNER])
        Wkv = pair("Wkv", [P, C, 2 * INNER])
        U = [two(f"U{m}", [P, T], F32R) for m in range(2)]
        Uc = two("Uc", [P, NPAIR, SKP], F32R)
        Qh = [two(f"Qh{m}", [P, T], F32R) for m in range(2)]
        Ql = [two(f"Ql{m}", [P, T], F32R) for m in range(2)]
        V = two("V", [P, NC, QH, P], F32R)
        Pr = two("Pr", [P, NT, NK + 1])
        RING = 4
        PTh, PTl = (sb(n, [P, RING, T], F32R) for n in ("PTh", "PTl"))
        low_or_keys = sb("low_or_keys", [SK, T])
        low = low_or_keys[0:HD, :]
        O = sb("O_pair", [P, T])
        least, rs = (sb(n, [P, 2, NT]) for n in ("least", "rs"))

        S = [st.ps(f"S{n}", [P, 1024]) for n in range(2)]
        bank = {n: st.ps(n, [P, 512]) for n in ("T0", "T1", "O", "J")}

        setup, mask_in, consts = sem("setup"), sem("mask_in"), sem("consts")
        z_in = sem("z_in")
        dup = [sem(f"dup{m}") for m in range(2)]
        o_out = sem("o_out")
        pe_s, act_s, dve_s = (st.steps(n) for n in ("products", "act", "dve"))
        claims = Claims("pa_banks", orders)
        for h in range(H):
            dve_s.alias(("read", "O", h), ("O", h))

        rows = lambda w: w.rearrange("(c p) n -> p c n", p=P)
        weights = []
        half = lambda w, n: w[:, :, n * 512:(n + 1) * 512]
        for name, tile, n in (("Wq", Wq, 0), ("Wkv", Wkv, 0), ("Wkv", Wkv, 1), ("Wkv", Wkv, 2), ("Wq", Wq, 1), ("Wkv", Wkv, 3)):
            weights.append((half(rows(a["L1_xattn_" + name]), n), half(tile[0], n), half(tile[1], n)))
        for_lead = 4
        others = {2: 4, 4: 5}
        slots = [t[:, :, :].rearrange("p t k -> p (t k)")[:, 0:2048] for t in Pr]
        w_sync, w_scalar, w_vector, w_cut = load_and_split(st, weights, "w", slots)

        ON_ACT = (0, 2)

        def parts(unit):
            if unit[0] == "V":
                return [j for j in range(unit[2], min(unit[2] + 2, NC))]
            return [(0, 1), (2, 3)] if unit[0] in ("Q", "K") else [(0, 1, 2, 3)]

        lead = [("Q", 0), ("Kr", 0), ("Kc", 0), ("Kr", 1), ("Kc", 1), ("K", 0), ("V", 0, 0), ("V", 0, 2)]
        begins = {3: ("V", 0, 4)}
        for n in range(2 * (NPAIR - 1)):
            begins[NT * n] = ("QK"[n % 2], 1 + n // 2)
        for q in range(1, H // QH):
            for n, (tick, j) in enumerate(((6, 0), (10, 2), (14, 4))):
                begins[16 * (q - 1) + tick] = ("V", q, j)
        begins.update(zip((60, 62, 63, 64, 65, 66, 68, 70), lead))
        starts = {tick + n: (unit, part) for tick, unit in begins.items() for n, part in enumerate(parts(unit))}

        work, dve_work, later = [("S", 0, 0)], [], []
        scored = lambda n: [divmod(n, NT)] if 0 <= n < H * NT else []
        for n in range((H + 2) * NT + 1):
            h, t = divmod(n, NT)
            for kind, units in (("rsum", scored(n - 1)), ("norm", scored(n - 1)), ("least", scored(n))):
                dve_work += [(kind,) + u for u in units if kind != "norm" or u[1] not in ON_ACT]
            dve_work += later
            work += [("S",) + u for u in scored(n + 1)]
            work += [("exp",) + u for u in scored(n)]
            work += [("norm",) + u for u in scored(n - 1) if u[1] in ON_ACT]
            later = []
            if n - 1 in starts:
                unit, part = starts[n - 1]
                if part == parts(unit)[-1]:
                    later.append(("R",) + unit)
            tick = ([("PV", h - 2, 3), ("PV", h - 2, 4), ("O", h - 2)],
                    [("T", h - 1, 0), ("T", h - 1, 1)],
                    [("T", h - 1, 2), ("PV", h - 1, 0), ("T", h - 1, 3), ("PV", h - 1, 1)],
                    [("T", h - 1, 4), ("PV", h - 1, 2)])[t]
            later += [u for u in tick if 0 <= u[1] < H]
            work += later
            if n in starts:
                work.append(("X",) + starts[n])
        dve_work += later
        last_projection = ("K", NPAIR - 1)

        def bank_of(u):
            if u[0] == "T":
                return "T%d" % ((u[1] * NC + u[2]) % 2)
            return "O" if u[0] == "PV" else "J"

        def values(u):
            _, q, j = u
            n, J = KEYS[j], len(parts(u))
            src = bank["J"][0:n, 0:J * QH * HD].rearrange("p (j h d) -> p j h d", j=J, d=HD)
            to = V[q % 2][0:n, j:j + J, :, :]
            return src, to[:, :, :, 0:HD], to[:, :, :, HD:P]

        ring = lambda h, c: (h * NC + c) % RING

        def wait(engine, signal, i, earlier, *name):
            engine.wait_ge(*(signal.before if earlier else signal.at)(i, *name))

        block = ctx.enter_context(nc.Block())

        @block.sync
        def _(sp):
            sp.dma_start(mask_words[:, :], a["mask_BxS2_bk0"]).then_inc(mask_in, 16)
            w_sync(sp, 0, for_lead)

            def load(i):
                for n in range(2):
                    sp.dma_start(f32(z[n][:, :, :]), z_s[n][bass.ds(i, 1)].rearrange("b p c z -> p (b c) z")).then_inc(z_in, 16)

            def duplicate(i, p):
                m = p % 2
                sp.wait_ge(*act_s.at(i, "hi", "Q", p, 0))
                sp.dma_start(f32(Qh[m][0][HD:P, :]), f32(Qh[m][0][0:HD, :])).then_inc(dup[m], 16)
                sp.wait_ge(*act_s.at(i, "hi", "Q", p, 1))
                sp.dma_start(f32(Qh[m][1][0:HD, :]), f32(Qh[m][1][HD:P, :])).then_inc(dup[m], 16)

            def one_round(i, coming):
                for p in range(1, NPAIR):
                    duplicate(i, p)
                sp.wait_ge(*pe_s.at(i, *last_projection))
                load(coming)
                duplicate(i, 0)

            load(0)
            w_sync(sp, for_lead, len(weights))
            duplicate(-1, 0)
            with sp.Fori(0, B - 1) as i:
                one_round(i, i + 1)
            one_round(B - 1, B - 1)
            sp.wait_ge(dup[0], 32 * (B * NPAIR // 2 + 1))

        @block.gpsimd
        def _(pool):
            make_identity(pool, ident, setup)
            pool.memset(one_row[:, :], 1.0).then_inc(setup, 1)
            pool.memset(f32(mrow[:, :, :]), 0.0).then_inc(setup, 1)
            for m in range(2):
                for x in range(2):
                    pool.memset(f32(Ql[m][x][:, :]), 0.0).then_inc(setup, 1)
                pool.memset(f32(Uc[m][:, :, :]), 0.0).then_inc(setup, 1)

        @block.tensor
        def _(pe):
            pe.wait_ge(setup, 10)
            pe.wait_ge(consts, 2)
            w_cut(pe, for_lead)

            def claim(i, u, b):
                last, earlier = claims.before(b, u)
                for s in (act_s, dve_s):
                    if s.has("read", *last):
                        wait(pe, s, i, earlier, "read", *last)
                return bank[b] if b in bank else S[int(b[1])]

            def project(u, part):
                ps, kind = bank[bank_of(u)], u[0]
                if kind == "Kr":
                    for k in part:
                        last = product(pe, ps[0:SK, :], [x[:, k, T:T + SK] for x in z],
                                       [w[:, k, u[1] * T:(u[1] + 1) * T] for w in Wkv], k == 0, k == C - 1)
                elif kind == "Kc":
                    for n in range(NPAIR // 2):
                        last = pe.transpose(ps[:, n * SKP:n * SKP + SK], low_or_keys[:, n * P:(n + 1) * P], ident[0:SK, 0:SK])
                elif kind in ("Q", "K"):
                    for k in part:
                        last = product(pe, ps[:, :], [w[:, k, u[1] * P:(u[1] + 1) * P] for w in (Wq if kind == "Q" else Wkv)],
                                       [x[:, k, 0:T] for x in z], k == 0, k == C - 1)
                else:
                    _, q, first = u
                    j = part
                    n0, out = INNER + q * QH * HD, ps[0:KEYS[j], (j - first) * QH * HD:(j - first + 1) * QH * HD]
                    for k in range(C):
                        last = product(pe, out, [x[:, k, j * P:j * P + KEYS[j]] for x in z],
                                       [w[:, k, n0:n0 + QH * HD] for w in Wkv], k == 0, k == C - 1)
                if part == parts(u)[-1]:
                    last.then_inc(*pe_s.mark(*u))

            pe_s.lead = True
            pe.wait_ge(z_in, 32)
            for n, u in enumerate(lead):
                if n:
                    pe.wait_ge(*(act_s if u[0] == "Kc" else dve_s).at(-1, "read", *lead[n - 1]))
                pe_s.lead_up(pe, *u)
                for part in parts(u):
                    project(u, part)
            pe_s.lead_up(pe)
            pe_s.lead = False
            w_cut(pe)
            with pe.Fori(0, B) as i:
                for u in work:
                    kind = u[0]
                    if kind == "X":
                        _, unit, part = u
                        if part == parts(unit)[0]:
                            if unit == lead[0]:
                                pe.wait_ge(z_in, i * 32 + 64)
                            claim(i, unit, bank_of(unit))
                        project(unit, part)
                    elif kind == "S":
                        _, h, t = u
                        p, x = h // 2, h % 2
                        if t == 0 and x == 0:
                            pe.wait_ge(dup[p % 2], (i * (NPAIR // 2) + (p // 2 + 1)) * 32)
                            if h:
                                pe.wait_ge(*dve_s.at(i, "read", "K", p))
                            else:
                                pe.wait_ge(*dve_s.before(i, "read", "K", 0))
                        ps = claim(i, u, "S%d" % (t % 2))
                        cols = slice(t * P, (t + 1) * P)
                        qh, ql = Qh[p % 2][x][:, cols], Ql[p % 2][x][:, cols]
                        pe.matmul(ps[:, 0:T], qh, U[p % 2][x][:, :], start=True, stop=False)
                        pe.matmul(ps[:, 0:T], ql, U[p % 2][x][:, :], start=False, stop=True)
                        out = ps[:, T:Z]
                        pe.matmul(out, qh, Uc[x][:, p, :], start=True, stop=False)
                        pe.matmul(out, ql, Uc[x][:, p, :], start=False, stop=False)
                        pe.matmul(out, ones[:, :], mrow[:, bass.ds(i, 1), :].rearrange("o b s -> o (b s)"),
                                  start=False, stop=True).then_inc(*pe_s.mark(*u))
                    elif kind == "T":
                        _, h, c = u
                        if c == 0:
                            pe.wait_ge(*act_s.at(i, "probs", h, ON_ACT[-1]))
                        if (h, c) == (0, 0):
                            claims.before(bank_of(u), u)
                            ps = bank[bank_of(u)]
                            pe.wait_ge(*dve_s.at(i, "probs", h, NT - 1))
                        else:
                            ps = claim(i, u, bank_of(u))
                        for t in range(NT):
                            m = pe.transpose(ps[0:KEYS[c], t * P:(t + 1) * P], Pr[h % 2][:, t, c * P:c * P + KEYS[c]], ident[:, :])
                        m.then_inc(*pe_s.mark(*u))
                    elif kind == "PV":
                        _, h, c = u
                        if c == 0:
                            claims.before("O", ("O", h))
                        ps, r, n = bank["O"], ring(h, c), KEYS[c]
                        v = V[(h // QH) % 2][0:n, c, h % QH, :]
                        pe.wait_ge(*dve_s.at(i, "read", "T", h, c))
                        pe.matmul(ps[:, :], v, PTh[0:n, r, :], start=(c == 0), stop=False)
                        pe.matmul(ps[:, :], v, PTl[0:n, r, :], start=False, stop=(c == NC - 1)).then_inc(*pe_s.mark(*u))

        @block.scalar
        def _(act):
            act.sem_inc(o_out, 16)
            w_scalar(act, 0, for_lead)

            def copy(out, src, *name, scale=1.0):
                act.activation(out, src, ACT.Copy, scale=scale).then_inc(*act_s.mark(*name))

            def read(i, u):
                act.wait_ge(*pe_s.at(i, *u))
                ps, kind = bank[bank_of(u)], u[0]
                if kind == "V":
                    if act_s.lead:
                        act_s.lead_up(act, "hi", *u)
                    src, v_hi, _ = values(u)
                    copy(v_hi, src, "hi", *u)
                    return
                if kind == "Kr":
                    if act_s.lead:
                        act_s.lead_up(act, "read", *u)
                    else:
                        act.wait_ge(*dve_s.at(i, "O", H - 3 + u[1]))
                    copy(low_or_keys[:, :], ps[0:SK, :], "read", *u)
                    return
                for x in range(2):
                    r = slice(x * HD, (x + 1) * HD)
                    name = ("hi", *u, x)
                    if act_s.lead:
                        act_s.lead_up(act, *name)
                    if kind == "Kc":
                        g = slice(u[1] * (NPAIR // 2), (u[1] + 1) * (NPAIR // 2))
                        copy(Uc[x][r, g, 0:SK], ps[r, 0:(NPAIR // 2) * SKP].rearrange("p (g s) -> p g s", s=SKP)[:, :, 0:SK], *name)
                    elif kind == "Q":
                        copy(Qh[u[1] % 2][x][r, :], ps[r, :], *name, scale=-SCALE)
                    else:
                        copy(U[u[1] % 2][x][r, :], ps[r, :], *name)

            act_s.lead = True
            for n, u in enumerate(lead):
                read(-1, u)
                if n in others:
                    w_scalar(act, others[n], others[n] + 1)
            act_s.lead_up(act)
            act_s.lead = False
            with act.Fori(0, B) as i:
                def store(p):
                    act.wait_ge(*dve_s.at(i, "O", 2 * p + 1))
                    act.dma_start(o_s[bass.ds(i, 1), p].rearrange("b p t -> (b p) t"), O[:, :]).then_inc(o_out, 16)

                for u in work:
                    kind = u[0]
                    if kind == "R":
                        read(i, u[1:])
                    elif kind == "exp":
                        _, h, t = u
                        if t == 2 and h % 2 and h >= 3:
                            store((h - 3) // 2)
                        act.wait_ge(*dve_s.at(i, "least", h, t))
                        act.activation(Pr[h % 2][:, t, 0:NK], S[t % 2][:, 0:NK], ACT.Exp, scale=-1.0,
                                       bias=least[:, h % 2, t:t + 1], accum_out=rs[:, h % 2, t:t + 1])\
                           .then_inc(*act_s.mark("read", "S", h, t))
                    elif kind == "norm":
                        _, h, t = u
                        act.wait_ge(*dve_s.at(i, "rsum", h, t))
                        act.activation(Pr[h % 2][:, t, 0:NK], Pr[h % 2][:, t, 0:NK], ACT.Copy, scale=rs[:, h % 2, t:t + 1])\
                           .then_inc(*act_s.mark("probs", h, t))
                    elif kind == "T":
                        _, h, c = u
                        act.wait_ge(*pe_s.at(i, *u))
                        copy(PTh[0:KEYS[c], ring(h, c), :], bank[bank_of(u)][0:KEYS[c], :], "hi", *u)
                    elif kind == "O":
                        h = u[1]
                        act.wait_ge(*pe_s.at(i, "PV", h, NC - 1))
                        copy(low, bank["O"][HD:P, :], "low", h)
                store(NPAIR - 1)
            act.wait_ge(o_out, 16 * (B * NPAIR + 1))

        @block.vector
        def _(dve):
            dve.wait_ge(setup, 10)
            dve.tensor_copy(ones[:, :], one_row[:, :]).then_inc(consts, 1)
            dve.wait_ge(mask_in, 16)
            dve.tensor_scalar(mrow[:, :, 0:SK], mask_u.rearrange("o (b s) -> o b s", b=B), 1.0, -MASKED,
                              ALU.subtract, ALU.mult).then_inc(consts, 1)
            w_vector(dve, 0, for_lead)

            def lo(out, src, hi_ap, *name):
                dve.tensor_tensor(out, src, f32(hi_ap), ALU.subtract).then_inc(*dve_s.mark(*name))

            def read(i, u):
                ps, kind = bank[bank_of(u)], u[0]
                if kind == "Kr":
                    return
                if kind == "V":
                    dve.wait_ge(*act_s.at(i, "hi", *u))
                    if dve_s.lead:
                        dve_s.lead_up(dve, "read", *u)
                    src, v_hi, v_lo = values(u)
                    lo(v_lo, src, v_hi, "read", *u)
                    return
                for x in range(2):
                    r, o = slice(x * HD, (x + 1) * HD), slice((1 - x) * HD, (2 - x) * HD)
                    name = ("read", *u) if x else ("lo", *u)
                    dve.wait_ge(*act_s.at(i, "hi", *u, x))
                    if dve_s.lead:
                        dve_s.lead_up(dve, *name)
                    if kind == "Kc":
                        g = slice(u[1] * (NPAIR // 2), (u[1] + 1) * (NPAIR // 2))
                        lo(Uc[x][o, g, 0:SK], ps[r, 0:(NPAIR // 2) * SKP].rearrange("p (g s) -> p g s", s=SKP)[:, :, 0:SK],
                           Uc[x][r, g, 0:SK], *name)
                    elif kind == "Q":
                        dve.scalar_tensor_tensor(Ql[u[1] % 2][x][r, :], ps[r, :], -SCALE, f32(Qh[u[1] % 2][x][r, :]),
                                                 ALU.mult, ALU.subtract).then_inc(*dve_s.mark(*name))
                    else:
                        lo(U[u[1] % 2][x][o, :], ps[r, :], U[u[1] % 2][x][r, :], *name)

            dve_s.lead = True
            for n, u in enumerate(lead):
                read(-1, u)
                if n in others:
                    w_vector(dve, others[n], others[n] + 1)
            dve_s.lead_up(dve)
            dve_s.lead = False
            with dve.Fori(0, B) as i:
                def normalise(h, t):
                    dve.wait_ge(*dve_s.at(i, "rsum", h, t))
                    p = Pr[h % 2][:, t, 0:NK]
                    dve.tensor_scalar(p, p, rs[:, h % 2, t:t + 1], None, ALU.mult).then_inc(*dve_s.mark("probs", h, t))

                for u in dve_work:
                    kind = u[0]
                    if kind == "R":
                        read(i, u[1:])
                    elif kind == "least":
                        _, h, t = u
                        dve.wait_ge(*pe_s.at(i, "S", h, t))
                        dve.tensor_reduce(least[:, h % 2, t:t + 1], S[t % 2][:, 0:NK], AX, ALU.min)\
                           .then_inc(*dve_s.mark("least", h, t))
                    elif kind == "rsum":
                        _, h, t = u
                        dve.wait_ge(*act_s.at(i, "read", "S", h, t))
                        dve.reciprocal(rs[:, h % 2, t:t + 1], rs[:, h % 2, t:t + 1]).then_inc(*dve_s.mark(*u))
                    elif kind == "norm":
                        normalise(*u[1:])
                    elif kind == "T":
                        _, h, c = u
                        dve.wait_ge(*act_s.at(i, "hi", *u))
                        n, r, ps = KEYS[c], ring(h, c), bank[bank_of(u)]
                        lo(PTl[0:n, r, :], ps[0:n, :], PTh[0:n, r, :], "read", *u)
                    elif kind == "O":
                        h = u[1]
                        p = h // 2
                        dve.wait_ge(*act_s.at(i, "low", h))
                        if h % 2 == 0:
                            dve.wait_ge(o_out, (i * NPAIR + (p + 1)) * 16)
                        dve.tensor_tensor(O[(h % 2) * HD:(h % 2 + 1) * HD, :], bank["O"][0:HD, :], low, ALU.add)\
                           .then_inc(*dve_s.mark("O", h))



def build_experts(nc, orders, a, o_s, x2_s, out):
    B, T, D = a["x"].shape
    C, NT = D // P, T // P
    K = a["L1_xattn_Wout"].shape[0] // P
    E, _, HE = a["L1_ffn_W1"].shape
    GROUPS = (range(0, NT // 2), range(NT // 2, NT))

    with ExitStack() as ctx:
        st = Stage(nc, ctx, "ex", orders)
        sb, sem = st.sb, st.sem
        pair = lambda name, shape: (sb(name + "_hi", shape, F32R), sb(name + "_lo", shape, F32R))
        ident = sb("ident", [P, P])
        eight = sb("eight", [P, E])
        minus_half = sb("minus_half", [P, NT])
        sel = sb("sel", [E, E, P], F32R)
        Wout = pair("Wout", [P, K, D])
        W1 = pair("W1", [HE, E * C, HE])
        W2 = pair("W2", [HE, E, D])
        Wg = pair("Wg", [P, C, E])
        Wg_raw = sb("Wg_raw", [P, C, E])
        b2 = pair("b2", [E, D])
        g_bc, b_bc = sb("g_bc", [P, D]), sb("b_bc", [P, D])
        gain, shift = sb("gain", [P, E * C]), sb("shift", [P, E * C])
        b1 = sb("b1", [P, E])
        b1x = sb("b1x", [P, E])
        o_raw = sb("o_raw", [P, K, T])
        o = pair("o", [P, K, T])
        x = sb("x", [P, NT, D])
        xh = sb("xh", [P, NT, D])
        stats, mv = sb("stats", [P, NT, 6]), sb("mv", [P, NT, 2])
        ve, rstd = sb("ve", [P, NT]), sb("rstd", [P, NT])
        xT = pair("xT", [P, C, T])
        LT = sb("LT", [E, T])
        L = sb("L", [P, NT, E])
        top = sb("top", [P, NT, E])
        idx = sb("idx", [P, NT, E], U32)
        idx_f = sb("idx_f", [P, NT])
        hot = sb("hot", [P, NT, E])
        hotT = sb("hotT", [E, T], F32R)
        g_both = sb("g", [P, 2 * T])
        g = [g_both[:, n * T:(n + 1) * T] for n in range(2)]
        sel_f = g_both[0:E, 0:E * P].rearrange("k (e p) -> k e p", e=E)
        b2_raw = g_both[0:E, 0:D]
        h = [pair(f"h{n}", [P, T]) for n in range(2)]

        acc = [st.ps(f"acc{n}", [P, 512]) for n in range(4)]
        bank = {n: st.ps(n, [P, 512]) for n in "ABCD"}

        setup, small, w1_in, b2_in = sem("setup"), sem("small"), sem("w1_in"), sem("b2_in")
        passed = sem("passed")
        consts, bias_ps, w1_ready, w1_hi = sem("consts"), sem("bias_ps"), sem("w1_ready"), sem("w1_hi")
        small_cut = sem("small_cut")
        o_in, x_in, stored = sem("o_in"), sem("x_in"), sem("stored")
        pe_s, act_s, dve_s, pool_s = (st.steps(n) for n in ("products", "act", "dve", "pool"))
        claims = Claims("ex_banks", orders)
        for t in range(NT):
            dve_s.alias(("read", "Wout", t), ("y", t))
            dve_s.alias(("read", "out", t), ("x4", t))
        dve_s.alias(("read", "hotT"), ("hotT",))

        rows = lambda w: w.rearrange("(c p) n -> p c n", p=P)
        w1_slots = [t[:, :, :].rearrange("p t d -> p (t d)") for t in (x, xh)]
        EH = E // 2
        w1_raw = [s.rearrange("p (k n) -> p k n", n=HE) for s in w1_slots]
        weights = []
        for n in range(2):
            s = slice(n * K // 2, (n + 1) * K // 2)
            weights.append((rows(a["L1_xattn_Wout"])[:, s, :], Wout[0][:, s, :], Wout[1][:, s, :]))
        w2s = []
        for n in range(2):
            s = slice(n * EH, (n + 1) * EH)
            w2s.append((a["L1_ffn_W2"].rearrange("e h d -> h e d")[:, s, :], W2[0][:, s, :], W2[1][:, s, :]))
        flat = o_raw[:, :, :].rearrange("p k t -> p (k t)")
        w_sync, w_scalar, w_vector, w_cut = load_and_split(st, weights, "w", [flat[:, 0:2048], flat[:, 2048:4096]])
        w2_sync, w2_scalar, w2_vector, w2_cut = load_and_split(st, w2s, "w2", w1_slots)

        smalls = [(gain[:, :], a["L1_ffn_ln_scale"]), (shift[:, :], a["L1_ffn_ln_bias"]), (b1[:, :], a["L1_ffn_b1"]),
                  (Wg_raw[:, :, :], rows(a["Wg_T"])),
                  (g_bc[:, :], a["L1_xattn_ln_o_g"].partition_broadcast(P)),
                  (b_bc[:, :], a["L1_xattn_ln_o_b"].partition_broadcast(P))]
        one = lambda ap, i: ap[bass.ds(i, 1)].rearrange("b (t p) d -> p (b t) d", p=P)
        block = ctx.enter_context(nc.Block())

        @block.sync
        def _(sp):
            for dst, src in smalls:
                sp.dma_start(dst, src).then_inc(small, 16)
            w_sync(sp)
            for n in range(2):
                src = a["L1_ffn_W1"][n * EH:(n + 1) * EH].rearrange("e (c p) h -> p (e c) h", p=P)
                sp.dma_start(w1_raw[n], src).then_inc(w1_in, 16)
            sp.wait_ge(consts, 1)
            sp.dma_start(b2_raw, a["L1_ffn_b2"]).then_inc(b2_in, 16)

            def load_o(i):
                sp.dma_start(o_raw[:, :, :], o_s[bass.ds(i, 1)].rearrange("b k p t -> p (b k) t")).then_inc(o_in, 16)

            def load_x(i):
                sp.dma_start(x[:, :, :], one(x2_s, i)).then_inc(x_in, 16)

            def one_round(i, coming):
                sp.wait_ge(*dve_s.before(i, "olo", K - 1))
                load_o(coming)
                sp.wait_ge(*dve_s.at(i, "x4", NT - 1))
                load_x(coming)

            w_cut(sp)
            load_o(0)
            sp.wait_ge(w1_ready, 4)
            w2_sync(sp)
            w2_cut(sp)
            load_x(0)
            with sp.Fori(0, B - 1) as i:
                one_round(i, i + 1)
            one_round(B - 1, B - 1)
            sp.wait_ge(x_in, 16 * (B + 1))

        @block.gpsimd
        def _(pool):
            pool.sem_inc(pool_s.sem, pool_s.per)
            make_identity(pool, ident, setup)
            pool.memset(minus_half[:, :], -0.5).then_inc(setup, 1)
            pool.iota(eight[:, :], pattern=[[1, E]], base=0, channel_multiplier=0,
                      allow_small_or_imprecise_dtypes=True).then_inc(setup, 1)
            pool.memset(sel_f[:, :, :], 0.0).then_inc(setup, 1)
            pool.wait_ge(setup, 5)
            pool.affine_select(out=sel_f[:, :, :], in_=sel_f[:, :, :], compare_op=ALU.not_equal, fill=1.0,
                               base=0, pattern=[[-1, E], [0, P]], channel_multiplier=1).then_inc(setup, 1)
            with pool.Fori(0, B) as i:
                for n, group in enumerate(GROUPS):
                    s = slice(group[0], group[-1] + 1)
                    for ln, scale, eps in (("ln_o", 1.0, EPS), ("ln", 1.0 + EPS, EPS * EPS)):
                        wait_apart(pool, dve_s.at(i, ln, "var", n), passed)
                        pool.tensor_scalar(ve[:, s], mv[:, s, 1], scale, eps, ALU.mult, ALU.add).then_inc(*pool_s.mark(ln, "ve", n))
                        pool.wait_ge(*pool_s.at(i, ln, "ve", n))
                        pool.tensor_tensor(rstd[:, s], ve[:, s], minus_half[:, s], ALU.pow).then_inc(*pool_s.mark(ln, "rstd", n))

        @block.tensor
        def _(pe):
            pe.sem_inc(pe_s.sem, pe_s.per)
            pe.wait_ge(small, 16 * len(smalls))
            pe.wait_ge(w1_in, 32)
            for e in range(E):
                for c in range(C):
                    m = pe.matmul(bank["A"][:, e:e + 1], w1_raw[e // EH][:, (e % EH) * C + c, :],
                                  shift[:, e * C + c:e * C + c + 1], start=(c == 0), stop=(c == C - 1))
            m.then_inc(bias_ps, 1)
            pe.wait_ge(setup, 6)
            pe.wait_ge(consts, 1)
            pe.wait_ge(small_cut, 3)
            w_cut(pe)
            with pe.Fori(0, B) as i:
                def claim(ps, b, *u):
                    last, earlier = claims.before(b, u)
                    for s in (act_s, dve_s):
                        if s.has("read", *last):
                            pe.wait_ge(*(s.before if earlier else s.at)(i, "read", *last))
                    return ps

                on = lambda b, *u: claim(bank[b], b, *u)

                for group in GROUPS:
                    for k in range(K):
                        if group[0] == 0:
                            pe.wait_ge(*dve_s.before(i, "olo", k))
                        for t in group:
                            if k == 0:
                                claim(acc[t], t, "Wout", t)
                            m = product(pe, acc[t][:, :], [z[:, k, t * P:(t + 1) * P] for z in o],
                                        [w[:, k, :] for w in Wout], k == 0, k == K - 1)
                            if k == K - 1:
                                m.then_inc(*pe_s.mark("Wout", t))
                w2_cut(pe)
                for c in range(C):
                    ps = on("ABCD"[c], "xT", c)
                    for t in range(NT):
                        if c == 0:
                            pe.wait_ge(*dve_s.at(i, "xh", t))
                        m = pe.transpose(ps[:, t * P:(t + 1) * P], xh[:, t, c * P:(c + 1) * P], ident[:, :])
                    m.then_inc(*pe_s.mark("xT", c))

                ps = on("C", "LT")
                pe.wait_ge(*dve_s.at(i, "read", "xT", C - 1))
                for c in range(C):
                    m = product(pe, ps[0:E, :], [w[:, c, :] for w in Wg], [z[:, c, :] for z in xT], c == 0, c == C - 1)
                m.then_inc(*pe_s.mark("LT"))

                def hidden(e):
                    ps = on("AB"[e % 2], "h", e)
                    for c in range(C):
                        m = product(pe, ps[:, :], [w[:, e * C + c, :] for w in W1], [z[:, c, :] for z in xT], c == 0, c == C - 1)
                    m.then_inc(*pe_s.mark("h", e))

                def mask(e):
                    ps = on("CD"[e % 2], "M", e)
                    pe.matmul(ps[:, :], sel[:, e, :], hotT[:, :], start=True, stop=True).then_inc(*pe_s.mark("M", e))

                hidden(0)
                ps = on("D", "L")
                wait_apart(pe, dve_s.at(i, "read", "LT"), passed)
                for t in range(NT):
                    m = pe.transpose(ps[:, t * E:(t + 1) * E], LT[:, t * P:(t + 1) * P], ident[0:E, 0:E])
                m.then_inc(*pe_s.mark("L"))
                hidden(1)
                ps = on("D", "hotT")
                pe.wait_ge(*dve_s.at(i, "hot"))
                for t in range(NT):
                    m = pe.transpose(ps[0:E, t * P:(t + 1) * P], hot[:, t, :], ident[:, :])
                m.then_inc(*pe_s.mark("hotT"))
                pe.wait_ge(*dve_s.at(i, "hotT"))
                for e in range(2):
                    mask(e)
                for t in range(NT):
                    claim(acc[t], t, "out", t)
                    for n in range(2):
                        pe.matmul(acc[t][:, :], hotT[:, t * P:(t + 1) * P], b2[n][:, :], start=(n == 0), stop=False)
                for e in range(E):
                    pe.wait_ge(*dve_s.at(i, "lo", e))
                    for t in range(NT):
                        m = product(pe, acc[t][:, :], [z[:, t * P:(t + 1) * P] for z in h[e % 2]],
                                    [w[:, e, :] for w in W2], False, e == E - 1)
                        if e == E - 1:
                            m.then_inc(*pe_s.mark("out", t))
                    if e < E - 1:
                        m.then_inc(*pe_s.mark("used", e))
                    if e + 2 < E:
                        hidden(e + 2)
                        mask(e + 2)

        @block.scalar
        def _(act):
            act.sem_inc(stored, 16)
            w_scalar(act)
            for n in range(2):
                act.wait_ge(w1_ready, n + 1)
                s = slice(n * EH * C, (n + 1) * EH * C)
                act.activation(W1[0][:, s, :], w1_raw[n], ACT.Copy).then_inc(w1_hi, 1)

            def cut_o(k):
                act.activation(o[0][:, k, :], o_raw[:, k, :], ACT.Copy).then_inc(*act_s.mark("ohi", k))

            act_s.lead = True
            act.wait_ge(o_in, 16)
            for k in range(K):
                act_s.lead_up(act, "ohi", k)
                cut_o(k)
            act_s.lead_up(act)
            act_s.lead = False
            w2_scalar(act)
            with act.Fori(0, B) as i:
                for c in range(C):
                    act.wait_ge(*pe_s.at(i, "xT", c))
                    act.activation(xT[0][:, c, :], bank["ABCD"[c]][:, :], ACT.Copy).then_inc(*act_s.mark("hi", "xT", c))

                def gelu(e):
                    act.wait_ge(*pe_s.at(i, "h", e))
                    if e < 2:
                        act.wait_ge(*dve_s.before(i, "lo", e + E - 2))
                    else:
                        act.wait_ge(*dve_s.at(i, "lo", e - 2))
                    act.activation(g[e % 2], bank["AB"[e % 2]][:, :], ACT.Gelu, bias=b1x[:, e:e + 1])\
                       .then_inc(*act_s.mark("read", "h", e))

                for e in range(E):
                    gelu(e)
                    act.wait_ge(*dve_s.at(i, "read", "M", e))
                    if e >= 2:
                        act.wait_ge(*pe_s.at(i, "used", e - 2))
                    else:
                        act.wait_ge(*pe_s.before(i, "out", NT - 1))
                    act.activation(h[e % 2][0][:, :], g[e % 2], ACT.Copy).then_inc(*act_s.mark("hhi", e))
                act.wait_ge(o_in, i * 16 + 32)
                for k in range(K):
                    cut_o(k)
                act.wait_ge(*dve_s.at(i, "x4", NT - 1))
                act.dma_start(one(out, i), xh[:, :, :]).then_inc(stored, 16)
            act.wait_ge(stored, 16 * (B + 1))

        @block.vector
        def _(dve):
            dve.wait_ge(setup, 6)
            dve.tensor_copy(sel[:, :, :], sel_f[:, :, :]).then_inc(consts, 1)
            w_vector(dve)
            dve.wait_ge(bias_ps, 1)
            dve.tensor_tensor(b1x[:, :], bank["A"][:, 0:E], b1[:, :], ALU.add).then_inc(small_cut, 1)
            for n in range(2):
                s = slice(n * EH * C, (n + 1) * EH * C)
                dve.tensor_tensor(w1_raw[n], w1_raw[n], gain[:, s].unsqueeze(2).to_broadcast([P, EH * C, HE]), ALU.mult)\
                   .then_inc(w1_ready, 1)
            for n in range(2):
                s = slice(n * EH * C, (n + 1) * EH * C)
                dve.wait_ge(w1_hi, n + 1)
                dve.tensor_tensor(W1[1][:, s, :], w1_raw[n], f32(W1[0][:, s, :]), ALU.subtract).then_inc(w1_ready, 1)
            for raw, cut, loaded in ((Wg_raw[:, :, :], [w[:, :, :] for w in Wg], None),
                                     (b2_raw, [w[:, :] for w in b2], b2_in)):
                if loaded is not None:
                    dve.wait_ge(loaded, 16)
                dve.tensor_copy(cut[0], raw).then_inc(consts, 1)
                dve.wait_ge(consts, 2 if loaded is None else 3)
                dve.tensor_tensor(cut[1], raw, f32(cut[0]), ALU.subtract).then_inc(small_cut, 1)
            dve.wait_ge(w1_ready, 4)

            def cut_o(i, k):
                dve.wait_ge(*act_s.at(i, "ohi", k))
                if dve_s.lead:
                    dve_s.lead_up(dve, "olo", k)
                dve.tensor_tensor(o[1][:, k, :], o_raw[:, k, :], f32(o[0][:, k, :]), ALU.subtract)\
                   .then_inc(*dve_s.mark("olo", k))

            dve_s.lead = True
            for k in range(K):
                cut_o(-1, k)
            dve_s.lead_up(dve)
            dve_s.lead = False
            w2_vector(dve)
            w2_cut(dve)
            with dve.Fori(0, B) as i:
                def moments(ln, t, src):
                    dve.bn_stats(stats[:, t, :], src).then_inc(*dve_s.mark(ln, "stats", t))

                def aggregate(ln, n, group, meanwhile=lambda: None):
                    wait_apart(dve, dve_s.at(i, ln, "stats", group[-1]), passed)
                    for t in group:
                        m = dve.bn_aggr(mv[:, t, :], stats[:, t, :])
                    m.then_inc(*dve_s.mark(ln, "var", n))
                    meanwhile()
                    dve.wait_ge(*dve_s.at(i, ln, "var", n))
                    dve.wait_ge(*pool_s.at(i, ln, "rstd", n))

                dve.wait_ge(stored, i * 16 + 16)
                for n, group in enumerate(GROUPS):
                    for t in group:
                        dve.wait_ge(*pe_s.at(i, "Wout", t))
                        moments("ln_o", t, acc[t][:, :])

                    def add_shift():
                        s = slice(group[0], group[-1] + 1)
                        dve.wait_ge(x_in, i * 16 + 16)
                        dve.tensor_tensor(x[:, s, :], x[:, s, :], b_bc[:, :].unsqueeze(1).to_broadcast([P, len(group), D]), ALU.add)\
                           .then_inc(*dve_s.mark("x+b", n))

                    aggregate("ln_o", n, group, add_shift)
                    for t in group:
                        dve.scalar_tensor_tensor(xh[:, t, :], acc[t][:, :], mv[:, t, 0:1], g_bc[:, :], ALU.subtract, ALU.mult)\
                           .then_inc(*dve_s.mark("y", t))
                    for t in group:
                        dve.wait_ge(*dve_s.at(i, "y", t))
                        dve.scalar_tensor_tensor(x[:, t, :], xh[:, t, :], rstd[:, t:t + 1], x[:, t, :], ALU.mult, ALU.add)\
                           .then_inc(*dve_s.mark("x3", t))
                    for t in group:
                        dve.wait_ge(*dve_s.at(i, "x3", t))
                        moments("ln", t, x[:, t, :])
                    aggregate("ln", n, group)
                    for t in group:
                        dve.tensor_scalar(xh[:, t, :], x[:, t, :], mv[:, t, 0:1], rstd[:, t:t + 1], ALU.subtract, ALU.mult)\
                           .then_inc(*dve_s.mark("xh", t))
                for c in range(C):
                    dve.wait_ge(*act_s.at(i, "hi", "xT", c))
                    dve.tensor_tensor(xT[1][:, c, :], bank["ABCD"[c]][:, :], f32(xT[0][:, c, :]), ALU.subtract)\
                       .then_inc(*dve_s.mark("read", "xT", c))
                dve.wait_ge(*pe_s.at(i, "LT"))
                dve.tensor_copy(LT[:, :], bank["C"][0:E, :]).then_inc(*dve_s.mark("read", "LT"))
                dve.wait_ge(*pe_s.at(i, "L"))
                dve.tensor_copy(L[:, :, :], bank["D"][:, 0:NT * E].rearrange("p (t e) -> p t e", e=E)).then_inc(*dve_s.mark("read", "L"))
                wait_apart(dve, dve_s.at(i, "read", "L"), passed)
                for t in range(NT):
                    dve.max(top[:, t, :], L[:, t, :]).then_inc(*dve_s.mark("top", t))
                wait_apart(dve, dve_s.at(i, "top", NT - 1), passed)
                for t in range(NT):
                    dve.max_index(idx[:, t, :], top[:, t, :], L[:, t, :]).then_inc(*dve_s.mark("idx", t))
                dve.wait_ge(*dve_s.at(i, "idx", NT - 1))
                dve.tensor_copy(idx_f[:, :], idx[:, :, 0]).then_inc(*dve_s.mark("idx_f"))
                dve.wait_ge(*dve_s.at(i, "idx_f"))
                dve.tensor_tensor(hot[:, :, :], idx_f[:, :].unsqueeze(2).to_broadcast([P, NT, E]),
                                  eight[:, :].unsqueeze(1).to_broadcast([P, NT, E]), ALU.is_equal).then_inc(*dve_s.mark("hot"))
                dve.wait_ge(*pe_s.at(i, "hotT"))
                dve.tensor_copy(hotT[:, :], bank["D"][0:E, :]).then_inc(*dve_s.mark("hotT"))

                def masked(e):
                    dve.wait_ge(*pe_s.at(i, "M", e))
                    dve.wait_ge(*act_s.at(i, "read", "h", e))
                    dve.tensor_tensor(g[e % 2], g[e % 2], bank["CD"[e % 2]][:, :], ALU.mult)\
                       .then_inc(*dve_s.mark("read", "M", e))

                for e in range(E):
                    masked(e)
                    dve.wait_ge(*act_s.at(i, "hhi", e))
                    dve.tensor_tensor(h[e % 2][1][:, :], g[e % 2], f32(h[e % 2][0][:, :]), ALU.subtract)\
                       .then_inc(*dve_s.mark("lo", e))
                for k in range(K // 2):
                    cut_o(i, k)
                for t in range(NT):
                    dve.wait_ge(*pe_s.at(i, "out", t))
                    dve.tensor_tensor(xh[:, t, :], acc[t][:, :], x[:, t, :], ALU.add).then_inc(*dve_s.mark("x4", t))
                for k in range(K // 2, K):
                    cut_o(i, k)



INPUTS = ["x", "ctx_1024", "mask_BxS2_ik0", "mask_BxS2_bk0",
          "L0_xattn_Wq", "L0_xattn_bq", "L0_xattn_Wk", "L0_xattn_bk", "L0_xattn_Wv", "L0_xattn_bv",
          "L0_xattn_Wo", "L0_xattn_bo",
          "L0_ffn_slot_init", "L0_ffn_w1", "L0_ffn_b1", "L0_ffn_w2", "L0_ffn_b2", "L0_ffn_tau",
          "L0_ffn_bih", "L0_ffn_bhh", "L0_ffn_wq", "L0_ffn_bq", "L0_ffn_wk", "L0_ffn_bk",
          "L0_ffn_wv", "L0_ffn_bv", "L0_ffn_ln_g", "L0_ffn_ln_b", "L0_ffn_wvp", "L0_ffn_bvp", "L0_ffn_wo", "L0_ffn_bo",
          "L1_xattn_ln_x_g", "L1_xattn_ln_x_b", "L1_xattn_ln_l_g", "L1_xattn_ln_l_b",
          "L1_xattn_Wq", "L1_xattn_Wkv", "L1_xattn_Wout", "L1_xattn_ln_o_g", "L1_xattn_ln_o_b",
          "L1_ffn_ln_scale", "L1_ffn_ln_bias", "L1_ffn_W1", "L1_ffn_b1", "L1_ffn_W2", "L1_ffn_b2",
          "Wih_T", "Whh_T", "slot_init_T", "Wg_T"]
TRANSPOSED = {"Wih_T": "L0_ffn_Wih", "Whh_T": "L0_ffn_Whh", "slot_init_T": "L0_ffn_slot_init", "Wg_T": "L1_ffn_Wg"}


def two_layers(nc, orders, a, out):
    B, T, D = a["x"].shape
    SK = a["ctx_1024"].shape[1]
    NS = a["L0_ffn_slot_init"].shape[0]
    INNER = a["L1_xattn_Wq"].shape[1]
    Z = T + SK + SK % 2

    def scratch(name, *shape):
        return nc.dram_tensor(name, shape, F32, kind="Internal").ap()

    x1_s, x2_s = scratch("x1_s", B, T, D), scratch("x2_s", B, T, D)
    alphaT_s = scratch("alphaT_s", B, NS, T)
    si_s, vo_s = scratch("si_s", B, NS, D), scratch("vo_s", B, NS, D)
    z_s = [scratch(f"z{n}_s", B, P, D // P, Z) for n in range(2)]
    o_s = scratch("o_s", B, INNER // P, P, T)

    build_layer0(nc, orders, a, x1_s, alphaT_s, si_s)
    build_slots(nc, orders, a, si_s, vo_s)
    build_latents(nc, orders, a, x1_s, alphaT_s, vo_s, x2_s, z_s)
    build_perceiver(nc, orders, a, z_s, o_s)
    build_experts(nc, orders, a, o_s, x2_s, out)


def kernel(**inputs):
    import concourse.bacc as bacc
    from concourse.bass_utils import run_bass_kernel_spmd

    arrays = {}
    for name in INPUTS:
        v = np.asarray(inputs[TRANSPOSED.get(name, name)])
        if name in TRANSPOSED:
            v = v.T
        elif name in COLUMNS:
            v = v.reshape(-1, P).T
        v = np.ascontiguousarray(v)
        if v.dtype == np.bool_:
            v = v.reshape(1, -1).view(np.int32)
        arrays[name] = v

    def program(orders):
        nc = bacc.Bacc("TRN2", target_bir_lowering=False, num_devices=1)
        a = {n: nc.dram_tensor(n, v.shape, mybir.dt.from_np(v.dtype), kind="ExternalInput").ap()
             for n, v in arrays.items()}
        out = nc.dram_tensor("out", arrays["x"].shape, F32, kind="ExternalOutput").ap()
        two_layers(nc, orders, a, out)
        return nc

    orders = {}
    program(orders)
    r = run_bass_kernel_spmd(program(orders), [arrays], core_ids=[0])
    return r.results[0]["out"]
```
